# Optimizing a Trainium2 kernel written in Bass

```python
import numpy as np
import jax
import jax.numpy as jnp

def _softmax(x, axis=-1):
    return jax.nn.softmax(x, axis=axis)

def _gelu(x):
    return jax.nn.gelu(x, approximate=True)

def _silu(x):
    return jax.nn.silu(x)

def _sigmoid(x):
    return jax.nn.sigmoid(x)

def _layernorm(x, axis=-1, eps=1e-05):
    m = jnp.mean(x, axis=axis, keepdims=True)
    v = jnp.var(x, axis=axis, keepdims=True)
    return (x - m) / jnp.sqrt(v + eps)

def _scatter_add(tgt, idx, src, axis=0):
    return tgt.at[idx].add(src)

def _segment_sum(src, seg, n):
    return jax.ops.segment_sum(src, seg, n)
kernel_name = 'mk_adj_ffn_d2_adj_r2_094799'

def setup_inputs(seed: int=0):
    np.random.seed(seed)
    _w = jnp.asarray

    def _rec_inputs():
        import jax
        import jax.numpy as jnp
        _gk = jax.random.key(seed)
        x = -0.0002928 + 1 * jax.random.normal(jax.random.fold_in(_gk, 1), (8, 1024, 128), jnp.float32)
        _a = jax.random.bernoulli(jax.random.fold_in(_gk, 2), 0.00390625, (8, 1024, 1024))
        _af = _a.astype(jnp.float32)
        _af = _af * jax.random.uniform(jax.random.fold_in(_gk, 3), (8, 1024, 1024), jnp.float32, 0.05, 0.999995)
        adj = _af
        return (x, adj)
    x, adj = _rec_inputs()

    def _L0_gnn_setup():
        import jax, jax.numpy as jnp
        import numpy as np
        B, N, D = (4, 2048, 128)
        DENSITY = 0.02
        key = jax.random.key(seed)
        kx, ka1, ka2, kwt, kbt, kwh, kth = jax.random.split(key, 7)
        x = jax.random.normal(kx, (B, N, D), dtype=jnp.float32)
        mask = jax.random.uniform(ka1, (B, N, N)) < DENSITY
        vals = jax.random.uniform(ka2, (B, N, N), dtype=jnp.float32)
        adj = jnp.where(mask, vals, 0.0).astype(jnp.float32)
        s = 0.02
        W_t = s * jax.random.normal(kwt, (D, D), dtype=jnp.float32)
        b_t = s * jax.random.normal(kbt, (D,), dtype=jnp.float32)
        W_h = s * jax.random.normal(kwh, (D, D), dtype=jnp.float32)
        theta = s * jax.random.normal(kth, (D, D), dtype=jnp.float32)
        return {'x': x, 'adj': adj, 'W_t': W_t, 'b_t': b_t, 'W_h': W_h, 'theta': theta}
    _L0_gnn_all = _L0_gnn_setup()
    _L0_gnn_in = {k: v for k, v in _L0_gnn_all.items() if k in ('W_t', 'b_t', 'W_h', 'theta')}
    del _L0_gnn_all

    def _L0_ffn_setup():
        import jax, jax.numpy as jnp
        import numpy as np
        B, S, D, F, E, K = (8, 1024, 128, 512, 8, 2)
        key = jax.random.key(seed)
        ks = jax.random.split(key, 10)
        s = 0.02
        return {'x': jax.random.normal(ks[0], (B, S, D), dtype=jnp.float32), 'Wr': jax.random.normal(ks[1], (D, E), dtype=jnp.float32) * s, 'W1s': jax.random.normal(ks[2], (D, F), dtype=jnp.float32) * s, 'b1s': jnp.zeros((F,), dtype=jnp.float32), 'W2s': jax.random.normal(ks[3], (F, D), dtype=jnp.float32) * s, 'b2s': jnp.zeros((D,), dtype=jnp.float32), 'W1p': jax.random.normal(ks[4], (E, D, F), dtype=jnp.float32) * s, 'b1p': jnp.zeros((E, F), dtype=jnp.float32), 'W2p': jax.random.normal(ks[5], (E, F, D), dtype=jnp.float32) * s, 'b2p': jnp.zeros((E, D), dtype=jnp.float32)}
    _L0_ffn_all = _L0_ffn_setup()
    _L0_ffn_in = {k: v for k, v in _L0_ffn_all.items() if k in ('Wr', 'W1s', 'b1s', 'W2s', 'b2s', 'W1p', 'b1p', 'W2p', 'b2p')}
    del _L0_ffn_all

    def _L1_gnn_setup():
        import jax, jax.numpy as jnp
        import numpy as np
        H = 4
        LN_EPS = 1e-05

        def _heads(x, B, N):
            return x.reshape(B, N, H, -1).transpose(0, 2, 1, 3)
        key = jax.random.key(seed)
        ks = jax.random.split(key, 6)
        B, N, IN, OUT = (4, 1024, 128, 128)
        return {'node_feats': jax.random.normal(ks[0], (B, N, IN), dtype=jnp.float32), 'adj_matrix': jax.random.uniform(ks[1], (B, N, N), dtype=jnp.float32), 'W_lin': jax.random.normal(ks[2], (IN, OUT), dtype=jnp.float32) * IN ** (-0.5), 'b_lin': jnp.zeros((OUT,), dtype=jnp.float32), 'W_q': jax.random.normal(ks[3], (IN, OUT), dtype=jnp.float32) * IN ** (-0.5), 'W_k': jax.random.normal(ks[4], (IN, OUT), dtype=jnp.float32) * IN ** (-0.5), 'ln_g': jnp.ones((OUT,), dtype=jnp.float32), 'ln_b': jnp.zeros((OUT,), dtype=jnp.float32)}
    _L1_gnn_all = _L1_gnn_setup()
    _L1_gnn_in = {k: v for k, v in _L1_gnn_all.items() if k in ('W_lin', 'b_lin', 'W_q', 'W_k', 'ln_g', 'ln_b')}
    del _L1_gnn_all

    def _L1_ffn_setup():
        import jax, jax.numpy as jnp
        import numpy as np
        H, P, G, NS, K = (8, 64, 64, 64, 3)
        D_INNER = H * P
        CONV_DIM = D_INNER + 2 * NS
        D_IN_PROJ = 2 * D_INNER + 2 * NS + 2 * H

        def _hydra(u, in_w, conv_w, conv_b, dt_bias, A_log, Dp, fcD_w, norm_w, out_w):
            Bt, L, _ = u.shape
            zxbcdt = u @ in_w.T
            z = zxbcdt[..., :D_INNER]
            xBC = zxbcdt[..., D_INNER:D_INNER + CONV_DIM]
            dt = zxbcdt[..., -2 * H:]
            dt = jnp.concatenate([dt[..., :H], jnp.flip(dt[..., H:], axis=1)], axis=0)
            dt = jax.nn.softplus(dt + dt_bias)
            xp = jnp.pad(xBC, ((0, 0), (K - 1, 0), (0, 0)))
            xBC = sum((xp[:, k:k + L, :] * conv_w[:, k] for k in range(K))) + conv_b
            xBC = jax.nn.silu(xBC)
            x = xBC[..., :D_INNER]
            Bm = xBC[..., D_INNER:D_INNER + NS]
            Cm = xBC[..., D_INNER + NS:]
            x_og = x
            x2 = jnp.concatenate([x, jnp.flip(x, 1)], 0).reshape(2 * Bt, L, H, P)
            B2 = jnp.concatenate([Bm, jnp.flip(Bm, 1)], 0)
            C2 = jnp.concatenate([Cm, jnp.flip(Cm, 1)], 0)
            dA = jnp.exp(dt * -jnp.exp(A_log))
            dBx = jnp.einsum('blh,bln,blhp->blhpn', dt, B2, x2)

            def step(h, inp):
                dA_t, dBx_t, C_t = inp
                h = h * dA_t[:, :, None, None] + dBx_t
                return (h, jnp.einsum('bhpn,bn->bhp', h, C_t))
            h0 = jnp.zeros((2 * Bt, H, P, NS), u.dtype)
            _, ys = jax.lax.scan(step, h0, (dA.transpose(1, 0, 2), dBx.transpose(1, 0, 2, 3, 4), C2.transpose(1, 0, 2)))
            y = ys.transpose(1, 0, 2, 3).reshape(2 * Bt, L, D_INNER)
            y_fw, y_bw = (y[:Bt], jnp.flip(y[Bt:], 1))
            y = jnp.pad(y_fw[:, :-1], ((0, 0), (1, 0), (0, 0))) + jnp.pad(y_bw[:, 1:], ((0, 0), (0, 1), (0, 0)))
            y = y + x_og * jnp.repeat(x_og @ fcD_w.T + Dp, P, axis=-1)
            yg = y * jax.nn.silu(z)
            yg = yg * jax.lax.rsqrt(jnp.mean(jnp.square(yg), -1, keepdims=True) + 1e-05) * norm_w
            return yg @ out_w.T
        key = jax.random.key(seed)
        ks = jax.random.split(key, 10)
        dim, Bsz, N = (128, 4, 4096)
        s = 0.02
        return {'x': jax.random.normal(ks[0], (Bsz, N, dim), jnp.float32), 'W_fx': jax.random.normal(ks[1], (D_INNER, dim), jnp.float32) * s, 'b_fx': jnp.zeros((D_INNER,), jnp.float32), 'W_x': jax.random.normal(ks[2], (D_INNER, dim), jnp.float32) * s, 'b_x': jnp.zeros((D_INNER,), jnp.float32), 'W_slice': jax.random.normal(ks[3], (G, P), jnp.float32) * s, 'b_slice': jnp.zeros((G,), jnp.float32), 'temperature': jnp.full((1, H, 1, 1), 0.5, jnp.float32), 'hy_in_w': jax.random.normal(ks[4], (D_IN_PROJ, D_INNER), jnp.float32) * s, 'hy_conv_w': jax.random.normal(ks[5], (CONV_DIM, K), jnp.float32) * s, 'hy_conv_b': jnp.zeros((CONV_DIM,), jnp.float32), 'hy_dt_bias': jnp.log(jnp.expm1(jnp.full((H,), 0.01, jnp.float32))), 'hy_A_log': jnp.log(jnp.linspace(1.0, 16.0, H)).astype(jnp.float32), 'hy_D': jnp.ones((H,), jnp.float32), 'hy_fcD_w': jax.random.normal(ks[6], (H, D_INNER), jnp.float32) * s, 'hy_norm_w': jnp.ones((D_INNER,), jnp.float32), 'hy_out_w': jax.random.normal(ks[7], (D_INNER, D_INNER), jnp.float32) * s, 'out_w': jax.random.normal(ks[8], (dim, D_INNER), jnp.float32) * s, 'out_b': jnp.zeros((dim,), jnp.float32)}
    _L1_ffn_all = _L1_ffn_setup()
    _L1_ffn_in = {k: v for k, v in _L1_ffn_all.items() if k in ('W_fx', 'b_fx', 'W_x', 'b_x', 'W_slice', 'b_slice', 'temperature', 'hy_in_w', 'hy_conv_w', 'hy_conv_b', 'hy_dt_bias', 'hy_A_log', 'hy_D', 'hy_fcD_w', 'hy_norm_w', 'hy_out_w', 'out_w', 'out_b')}
    del _L1_ffn_all
    return {'x': x, 'adj': adj, 'L0_gnn_W_t': _L0_gnn_in['W_t'], 'L0_gnn_b_t': _L0_gnn_in['b_t'], 'L0_gnn_W_h': _L0_gnn_in['W_h'], 'L0_gnn_theta': _L0_gnn_in['theta'], 'L0_ffn_Wr': _L0_ffn_in['Wr'], 'L0_ffn_W1s': _L0_ffn_in['W1s'], 'L0_ffn_b1s': _L0_ffn_in['b1s'], 'L0_ffn_W2s': _L0_ffn_in['W2s'], 'L0_ffn_b2s': _L0_ffn_in['b2s'], 'L0_ffn_W1p': _L0_ffn_in['W1p'], 'L0_ffn_b1p': _L0_ffn_in['b1p'], 'L0_ffn_W2p': _L0_ffn_in['W2p'], 'L0_ffn_b2p': _L0_ffn_in['b2p'], 'L1_gnn_W_lin': _L1_gnn_in['W_lin'], 'L1_gnn_b_lin': _L1_gnn_in['b_lin'], 'L1_gnn_W_q': _L1_gnn_in['W_q'], 'L1_gnn_W_k': _L1_gnn_in['W_k'], 'L1_gnn_ln_g': _L1_gnn_in['ln_g'], 'L1_gnn_ln_b': _L1_gnn_in['ln_b'], 'L1_ffn_W_fx': _L1_ffn_in['W_fx'], 'L1_ffn_b_fx': _L1_ffn_in['b_fx'], 'L1_ffn_W_x': _L1_ffn_in['W_x'], 'L1_ffn_b_x': _L1_ffn_in['b_x'], 'L1_ffn_W_slice': _L1_ffn_in['W_slice'], 'L1_ffn_b_slice': _L1_ffn_in['b_slice'], 'L1_ffn_temperature': _L1_ffn_in['temperature'], 'L1_ffn_hy_in_w': _L1_ffn_in['hy_in_w'], 'L1_ffn_hy_conv_w': _L1_ffn_in['hy_conv_w'], 'L1_ffn_hy_conv_b': _L1_ffn_in['hy_conv_b'], 'L1_ffn_hy_dt_bias': _L1_ffn_in['hy_dt_bias'], 'L1_ffn_hy_A_log': _L1_ffn_in['hy_A_log'], 'L1_ffn_hy_D': _L1_ffn_in['hy_D'], 'L1_ffn_hy_fcD_w': _L1_ffn_in['hy_fcD_w'], 'L1_ffn_hy_norm_w': _L1_ffn_in['hy_norm_w'], 'L1_ffn_hy_out_w': _L1_ffn_in['hy_out_w'], 'L1_ffn_out_w': _L1_ffn_in['out_w'], 'L1_ffn_out_b': _L1_ffn_in['out_b']}

def reference(x, adj, L0_gnn_W_t, L0_gnn_b_t, L0_gnn_W_h, L0_gnn_theta, L0_ffn_Wr, L0_ffn_W1s, L0_ffn_b1s, L0_ffn_W2s, L0_ffn_b2s, L0_ffn_W1p, L0_ffn_b1p, L0_ffn_W2p, L0_ffn_b2p, L1_gnn_W_lin, L1_gnn_b_lin, L1_gnn_W_q, L1_gnn_W_k, L1_gnn_ln_g, L1_gnn_ln_b, L1_ffn_W_fx, L1_ffn_b_fx, L1_ffn_W_x, L1_ffn_b_x, L1_ffn_W_slice, L1_ffn_b_slice, L1_ffn_temperature, L1_ffn_hy_in_w, L1_ffn_hy_conv_w, L1_ffn_hy_conv_b, L1_ffn_hy_dt_bias, L1_ffn_hy_A_log, L1_ffn_hy_D, L1_ffn_hy_fcD_w, L1_ffn_hy_norm_w, L1_ffn_hy_out_w, L1_ffn_out_w, L1_ffn_out_b):
    import jax
    import jax.numpy as jnp

    def _L0_gnn_ref(x, adj, W_t, b_t, W_h, theta):
        import jax, jax.numpy as jnp
        import numpy as np
        B, N, D = (4, 2048, 128)
        DENSITY = 0.02
        in_degrees = jnp.sum(adj, axis=-1)
        norm = jnp.power(in_degrees + 1e-06, -0.5)[..., None]
        f_hom = jnp.einsum('bnd,de->bne', x, theta) * norm
        f_hom = jnp.einsum('bnm,bmd->bnd', adj, f_hom) * norm
        f_het = jnp.einsum('bnd,de->bne', x, W_h)
        gate = jax.nn.sigmoid(jnp.einsum('bnd,de->bne', x, W_t) + b_t)
        out = gate * f_hom + (1.0 - gate) * f_het
        return jax.nn.elu(out)

    def _L0_ffn_ref(x, Wr, W1s, b1s, W2s, b2s, W1p, b1p, W2p, b2p):
        import jax, jax.numpy as jnp
        import numpy as np
        B, S, D, F, E, K = (8, 1024, 128, 512, 8, 2)
        gelu = lambda t: jax.nn.gelu(t, approximate=False)
        shared = gelu(x @ W1s + b1s) @ W2s + b2s
        rw = jax.nn.softmax(x @ Wr, axis=-1)
        topw, topi = jax.lax.top_k(rw, K)
        topw = topw / jnp.sum(topw, axis=-1, keepdims=True)
        mask = jnp.sum(jax.nn.one_hot(topi, E, dtype=topw.dtype) * topw[..., None], axis=-2)
        h = gelu(jnp.einsum('bsd,edf->bsef', x, W1p) + b1p)
        priv = jnp.einsum('bsef,efd->bsed', h, W2p) + b2p
        routed = jnp.einsum('bsed,bse->bsd', priv, mask)
        return shared + routed

    def _L1_gnn_ref(node_feats, adj_matrix, W_lin, b_lin, W_q, W_k, ln_g, ln_b):
        import jax, jax.numpy as jnp
        import numpy as np
        H = 4
        LN_EPS = 1e-05

        def _heads(x, B, N):
            return x.reshape(B, N, H, -1).transpose(0, 2, 1, 3)
        B, N, _ = node_feats.shape
        out_dim = W_lin.shape[1]
        hd = out_dim // H
        scale = hd ** (-0.5)
        lrelu = lambda z: jax.nn.leaky_relu(z, 0.01)
        X = _heads(lrelu(node_feats @ W_lin + b_lin), B, N)
        q = _heads(lrelu(node_feats @ W_q), B, N)
        k = _heads(lrelu(node_feats @ W_k), B, N)
        att = jax.nn.sigmoid(jnp.einsum('bhxd,bhyd->bhxy', q, k) * scale)
        adj_h = adj_matrix[:, None] * att
        deg = jnp.sum(adj_h, axis=-1)
        dis = jnp.where(deg > 0, deg ** (-0.5), 0.0)
        A = dis[..., :, None] * adj_h * dis[..., None, :]
        Y = jnp.einsum('bhxy,bhyd->bhxd', A, X)
        Y = Y.transpose(0, 2, 1, 3).reshape(B, N, out_dim)
        mu = jnp.mean(Y, axis=-1, keepdims=True)
        var = jnp.mean((Y - mu) ** 2, axis=-1, keepdims=True)
        return (Y - mu) * jax.lax.rsqrt(var + LN_EPS) * ln_g + ln_b

    def _L1_ffn_ref(x, W_fx, b_fx, W_x, b_x, W_slice, b_slice, temperature, hy_in_w, hy_conv_w, hy_conv_b, hy_dt_bias, hy_A_log, hy_D, hy_fcD_w, hy_norm_w, hy_out_w, out_w, out_b):
        import jax, jax.numpy as jnp
        import numpy as np
        H, P, G, NS, K = (8, 64, 64, 64, 3)
        D_INNER = H * P
        CONV_DIM = D_INNER + 2 * NS
        D_IN_PROJ = 2 * D_INNER + 2 * NS + 2 * H

        def _hydra(u, in_w, conv_w, conv_b, dt_bias, A_log, Dp, fcD_w, norm_w, out_w):
            Bt, L, _ = u.shape
            zxbcdt = u @ in_w.T
            z = zxbcdt[..., :D_INNER]
            xBC = zxbcdt[..., D_INNER:D_INNER + CONV_DIM]
            dt = zxbcdt[..., -2 * H:]
            dt = jnp.concatenate([dt[..., :H], jnp.flip(dt[..., H:], axis=1)], axis=0)
            dt = jax.nn.softplus(dt + dt_bias)
            xp = jnp.pad(xBC, ((0, 0), (K - 1, 0), (0, 0)))
            xBC = sum((xp[:, k:k + L, :] * conv_w[:, k] for k in range(K))) + conv_b
            xBC = jax.nn.silu(xBC)
            x = xBC[..., :D_INNER]
            Bm = xBC[..., D_INNER:D_INNER + NS]
            Cm = xBC[..., D_INNER + NS:]
            x_og = x
            x2 = jnp.concatenate([x, jnp.flip(x, 1)], 0).reshape(2 * Bt, L, H, P)
            B2 = jnp.concatenate([Bm, jnp.flip(Bm, 1)], 0)
            C2 = jnp.concatenate([Cm, jnp.flip(Cm, 1)], 0)
            dA = jnp.exp(dt * -jnp.exp(A_log))
            dBx = jnp.einsum('blh,bln,blhp->blhpn', dt, B2, x2)

            def step(h, inp):
                dA_t, dBx_t, C_t = inp
                h = h * dA_t[:, :, None, None] + dBx_t
                return (h, jnp.einsum('bhpn,bn->bhp', h, C_t))
            h0 = jnp.zeros((2 * Bt, H, P, NS), u.dtype)
            _, ys = jax.lax.scan(step, h0, (dA.transpose(1, 0, 2), dBx.transpose(1, 0, 2, 3, 4), C2.transpose(1, 0, 2)))
            y = ys.transpose(1, 0, 2, 3).reshape(2 * Bt, L, D_INNER)
            y_fw, y_bw = (y[:Bt], jnp.flip(y[Bt:], 1))
            y = jnp.pad(y_fw[:, :-1], ((0, 0), (1, 0), (0, 0))) + jnp.pad(y_bw[:, 1:], ((0, 0), (0, 1), (0, 0)))
            y = y + x_og * jnp.repeat(x_og @ fcD_w.T + Dp, P, axis=-1)
            yg = y * jax.nn.silu(z)
            yg = yg * jax.lax.rsqrt(jnp.mean(jnp.square(yg), -1, keepdims=True) + 1e-05) * norm_w
            return yg @ out_w.T
        B, N, _ = x.shape
        fx = (x @ W_fx.T + b_fx).reshape(B, N, H, P).transpose(0, 2, 1, 3)
        xm = (x @ W_x.T + b_x).reshape(B, N, H, P).transpose(0, 2, 1, 3)
        temp = jnp.maximum(temperature, 1e-06)
        sw = jax.nn.softmax((xm @ W_slice.T + b_slice) / temp, axis=-1)
        snorm = sw.sum(2)
        st = jnp.einsum('bhnc,bhng->bhgc', fx, sw) / (snorm + 1e-05)[..., None]
        st = st.transpose(0, 2, 1, 3).reshape(B, G, D_INNER)
        ot = _hydra(st, hy_in_w, hy_conv_w, hy_conv_b, hy_dt_bias, hy_A_log, hy_D, hy_fcD_w, hy_norm_w, hy_out_w)
        ot = ot.reshape(B, G, H, P).transpose(0, 2, 1, 3)
        out = jnp.einsum('bhgc,bhng->bhnc', ot, sw).transpose(0, 2, 1, 3).reshape(B, N, D_INNER)
        return out @ out_w.T + out_b
    x = x + _L0_gnn_ref(_layernorm(x, axis=-1), adj, L0_gnn_W_t, L0_gnn_b_t, L0_gnn_W_h, L0_gnn_theta)
    x = x + _L0_ffn_ref(_layernorm(x, axis=-1), L0_ffn_Wr, L0_ffn_W1s, L0_ffn_b1s, L0_ffn_W2s, L0_ffn_b2s, L0_ffn_W1p, L0_ffn_b1p, L0_ffn_W2p, L0_ffn_b2p)
    x = x + _L1_gnn_ref(_layernorm(x, axis=-1), adj, L1_gnn_W_lin, L1_gnn_b_lin, L1_gnn_W_q, L1_gnn_W_k, L1_gnn_ln_g, L1_gnn_ln_b)
    x = x + _L1_ffn_ref(_layernorm(x, axis=-1), L1_ffn_W_fx, L1_ffn_b_fx, L1_ffn_W_x, L1_ffn_b_x, L1_ffn_W_slice, L1_ffn_b_slice, L1_ffn_temperature, L1_ffn_hy_in_w, L1_ffn_hy_conv_w, L1_ffn_hy_conv_b, L1_ffn_hy_dt_bias, L1_ffn_hy_A_log, L1_ffn_hy_D, L1_ffn_hy_fcD_w, L1_ffn_hy_norm_w, L1_ffn_hy_out_w, L1_ffn_out_w, L1_ffn_out_b)
    return x

_drawn_inputs = setup_inputs


def setup_inputs(seed=0):
    import zlib

    import numpy as np

    out = dict(_drawn_inputs(seed))
    spreads = {'L0_ffn_b1s': (0.0, 0.8),
     'L0_ffn_b2s': (0.0, 0.372),
     'L0_ffn_b1p': (0.0, 0.8),
     'L0_ffn_b2p': (0.0, 0.582),
     'L1_gnn_b_lin': (0.0, 0.368),
     'L1_gnn_ln_g': (1.0, 0.6),
     'L1_gnn_ln_b': (0.0, 0.718),
     'L1_ffn_b_fx': (0.0, 0.8),
     'L1_ffn_b_x': (0.0, 0.8),
     'L1_ffn_b_slice': (0.0, 0.8),
     'L1_ffn_temperature': (0.5, 0.6),
     'L1_ffn_hy_conv_b': (0.0, 0.782),
     'L1_ffn_hy_dt_bias': (-4.600166320800781, 0.6),
     'L1_ffn_hy_D': (1.0, 0.6),
     'L1_ffn_hy_norm_w': (1.0, 0.6),
     'L1_ffn_out_b': (0.0, 0.667)}
    factors = {'L0_gnn_b_t': 5.631,
     'L0_gnn_W_h': 3.002,
     'L0_ffn_Wr': 4.479,
     'L0_ffn_W1s': 6.018,
     'L0_ffn_W2s': 5.242,
     'L0_ffn_W1p': 8.0,
     'L0_ffn_W2p': 7.715,
     'L1_gnn_W_q': 4.895,
     'L1_gnn_W_k': 4.779,
     'L1_ffn_W_fx': 8.0,
     'L1_ffn_W_x': 8.0,
     'L1_ffn_W_slice': 8.0,
     'L1_ffn_hy_in_w': 6.425,
     'L1_ffn_hy_conv_w': 8.0,
     'L1_ffn_hy_A_log': 8.0,
     'L1_ffn_hy_fcD_w': 8.0,
     'L1_ffn_hy_out_w': 6.792,
     'L1_ffn_out_w': 6.229}
    for name, (base, spread) in spreads.items():
        noise = np.random.default_rng([zlib.crc32(name.encode()), seed]).standard_normal(out[name].shape)
        drawn = base * np.exp(spread * noise) if base else spread * noise
        out[name] = jnp.asarray(drawn.astype(out[name].dtype))
    for name, factor in factors.items():
        out[name] = (out[name] * factor).astype(out[name].dtype)
    return out
```

```python
import concourse.bass as bass
from concourse import mybir
from contextlib import ExitStack

fp32 = mybir.dt.float32
fp32r = mybir.dt.float32r
ALU = mybir.AluOpType
ACT = mybir.ActivationFunctionType
AX = mybir.AxisListType

P = 128
B, N, D = 8, 1024, 128
T = N // P
HALF = 512
NH = N // HALF
LN_EPS = 1e-5


E_N, F_N = 8, 512
FT = F_N // P
G = 512
RT = G // P
TOK = B * N
TILES = TOK // P
SHARED = TOK // G
ROUTED = 2 * TOK // G + E_N - 1
GROUPS = SHARED + ROUTED
BLOB = F_N + FT + FT * D + 1
ROW = D + 2
SPARE = ROUTED * G // B
FP = 96
FILL = SPARE // FP
i32, u32 = mybir.dt.int32, mybir.dt.uint32


class Chain:

    def __init__(self, eng, sem):
        self.eng, self.sem, self.base, self.n = eng, sem, 0, 0

    def at(self, base):
        self.base, self.n = base, 0

    def step(self, ins):
        ins.then_inc(self.sem, 1)
        self.n += 1

    def wait(self):
        self.eng.wait_ge(self.sem, self.base + self.n)

    def link(self, ins):
        self.step(ins)
        self.wait()


def over_batches(eng, body):
    body(0, 0, True, False)
    body(1, 1, False, False)
    with eng.Fori(1, B // 2 - 1) as j:
        body(2 * j, 0, False, False)
        body(2 * j + 1, 1, False, False)
    body(B - 2, 0, False, False)
    body(B - 1, 1, False, True)


def exists(i):
    return not isinstance(i, int) or i < B


def wait(eng, sem, value):
    if not isinstance(value, int) or value > 0:
        eng.wait_ge(sem, value)


def tiled(x):
    return x.rearrange("(t p) d -> p t d", p=P)


def transposes(pe, out, src, ident):
    last = []
    for t in range(T):
        mm = pe.transpose(out[:, t, :], src[:, t, :], ident[:, :])
        if t % 4 == 3:
            last.append(mm)
    return last


class LayerNorm:

    def __init__(self, sb, sem):
        self.st = sb("st", [P, T, 6])
        self.sums = sb("sums", [P, T, 2])
        self.dm, self.dm2, self.var = sb("dm", [P, T]), sb("dm2", [P, T]), sb("var", [P, T])
        self.mean = [sb(f"mean{u}", [P, T]) for u in range(2)]
        self.ve = [sb(f"ve{u}", [P, T]) for u in range(2)]
        self.rstd = [sb(f"rstd{u}", [P, T]) for u in range(2)]
        self.var_ready, self.rstd_ready = sem("var_ready"), sem("rstd_ready")
        self.step = sem("norm_step")

    def stats(self, dve, x, i, u):
        chain = Chain(dve, self.step)
        chain.at(3 * i)
        st, sums = self.st, self.sums
        for t in range(T):
            ins = dve.bn_stats(st[:, t, :], x[:, t, :])
        chain.link(ins)
        dve.tensor_tensor(sums[:, :, :], st[:, :, 1:3], st[:, :, 4:6], ALU.add)
        chain.link(dve.tensor_tensor(self.dm[:, :], st[:, :, 1], st[:, :, 4], ALU.subtract))
        dve.tensor_scalar(self.mean[u][:, :], sums[:, :, 0], 0.5, None, ALU.mult)
        dve.scalar_tensor_tensor(out=self.dm2[:, :], in0=self.dm[:, :], scalar=0.25, in1=self.dm[:, :],
                                 op0=ALU.mult, op1=ALU.mult)
        chain.link(dve.tensor_scalar(self.var[:, :], sums[:, :, 1], 1.0 / D, LN_EPS, ALU.mult, ALU.add))
        dve.tensor_tensor(self.ve[u][:, :], self.var[:, :], self.dm2[:, :], ALU.add).then_inc(self.var_ready, 1)

    def power(self, pool, power, i, u):
        pool.wait_ge(self.var_ready, i + 1)
        pool.tensor_tensor(self.rstd[u][:, :], self.ve[u][:, :], power[:, 0:T], ALU.pow).then_inc(self.rstd_ready, 1)

    def apply(self, dve, x, xn, i, u):
        dve.wait_ge(self.rstd_ready, i + 1)
        for t in range(T):
            ins = dve.tensor_scalar(xn[:, t, :], x[:, t, :], self.mean[u][:, t:t + 1], self.rstd[u][:, t:t + 1],
                                    ALU.subtract, ALU.mult)
        return ins


def setup_stage(nc, ident):
    with ExitStack() as ctx:
        zeroed = ctx.enter_context(nc.semaphore("ident_zeroed"))
        block = ctx.enter_context(nc.Block())

        @block.gpsimd
        def _(pool):
            pool.memset(ident[:, :], 0.0).then_inc(zeroed, 1)
            pool.wait_ge(zeroed, 1)
            pool.affine_select(out=ident[:, :], in_=ident[:, :], compare_op=ALU.not_equal, fill=1.0,
                               base=0, pattern=[[-1, P]], channel_multiplier=1).then_inc(zeroed, 1)
            pool.wait_ge(zeroed, 2)


def gated_gnn_stage(nc, x_in, x_out, adjT, W_t, b_t, W_h, theta, ident, rows, sums):
    with ExitStack() as ctx:
        sb = lambda name, shape, dt=fp32: ctx.enter_context(nc.sbuf_tensor("a_" + name, shape, dt))
        ps = lambda name, shape: ctx.enter_context(nc.psum_tensor("a_" + name, shape, fp32))
        sem = lambda name: ctx.enter_context(nc.semaphore("a_" + name))

        W = sb("W", [P, 3, D])
        bias = sb("bias", [P, D])
        ones = sb("ones", [P, 32])
        power = sb("power", [P, T])
        fill = sb("fill", [FP, FILL, ROW])
        spare_i = sb("spare_i", [FP, FILL], i32)
        X = [sb(f"X{u}", [P, T, D]) for u in range(2)]
        R = [sb(f"R{u}", [P, T, D]) for u in range(2)]
        A = [sb(f"A{u}", [P, T, N]) for u in range(2)]
        xn = sb("xn", [P, T, D])
        xnT = sb("xnT", [P, N])
        dpart = sb("dpart", [P, N])
        dsum = sb("dsum", [P, T])
        deg = sb("deg", [P, T])
        norm = [sb(f"norm{u}", [P, T]) for u in range(2)]
        F = sb("F", [P, T, D])
        Hh = [sb(f"H{u}", [P, T, D]) for u in range(2)]
        Z = [sb(f"Z{u}", [P, T, D]) for u in range(2)]
        aggT = sb("aggT", [P, N])
        dif = sb("dif", [P, T, D])
        O = sb("O", [P, T, D])
        E = sb("E", [P, T, D])

        TP = ps("TP", [P, T, P])
        DG = ps("DG", [P, N])
        FG = ps("FG", [P, 2, HALF])
        AG = ps("AG", [P, N])

        w_loaded, consts, filled = sem("w_loaded"), sem("consts"), sem("filled")
        x_loaded = [sem(f"x_loaded{u}") for u in range(2)]
        r_loaded = [sem(f"r_loaded{u}") for u in range(2)]
        adj_loaded = [sem(f"adj_loaded{u}") for u in range(2)]
        xn_ready = sem("xn_ready")
        norm_in = LayerNorm(sb, sem)
        xnT_psum, xnT_ready = sem("xnT_psum"), sem("xnT_ready")
        dpart_psum, dpart_ready, degT_psum = sem("dpart_psum"), sem("dpart_ready"), sem("degT_psum")
        deg_ready, norm_ready = sem("deg_ready"), sem("norm_ready")
        fgh_psum, H_ready, FZ_ready = sem("fgh_psum"), sem("H_ready"), sem("FZ_ready")
        th_ready = sem("th_ready")
        agg_psum, agg_ready, out_psum = sem("agg_psum"), sem("agg_ready"), sem("out_psum")
        dif_ready, O_min, E_ready = sem("dif_ready"), sem("O_min"), sem("E_ready")
        out_ready, stored = sem("out_ready"), sem("stored")
        dve_step = sem("dve_step")
        block = ctx.enter_context(nc.Block())

        @block.sync
        def _(sp):
            sp.dma_start(W[:, 0, :], theta).then_inc(w_loaded, 16)
            sp.dma_start(W[:, 1, :], W_h).then_inc(w_loaded, 16)
            sp.dma_start(W[:, 2, :], W_t).then_inc(w_loaded, 16)
            sp.dma_start(bias[:, :], b_t.rearrange("(a n) -> a n", a=1).to_broadcast([P, D])).then_inc(w_loaded, 16)

            def load_x(i, u):
                wait(sp, xn_ready, i - 1)
                sp.dma_start(X[u][:, :, :], tiled(x_in[i])).then_inc(x_loaded[u], 16)

            def load_adj(i, u):
                wait(sp, agg_psum, NH * (i - 1))
                for q in range(4):
                    sp.dma_start(A[u][:, 2 * q:2 * q + 2, :], adjT[i, bass.ts(q, 2 * P), :].rearrange(
                        "(t p) n -> p t n", p=P)).then_inc(adj_loaded[u], 16)

            def body(i, u, first, last):
                if exists(i + 2):
                    load_x(i + 2, u)
                if exists(i + 1):
                    load_adj(i + 1, 1 - u)
                wait(sp, stored, 16 * i - 16)
                sp.dma_start(R[u][:, :, :], tiled(x_in[i])).then_inc(r_loaded[u], 16)
                if not first:
                    store(i - 1, 1 - u)
                if last:
                    store(i, u)
                sp.dma_start(rows[bass.ds(i * SPARE + TOK, SPARE), :].rearrange("(p r) d -> p r d", p=FP),
                             fill[:, :, :]).then_inc(filled, 16)

            def store(i, u):
                sp.wait_ge(out_ready, i + 1)
                sp.dma_start(tiled(x_out[i]), R[u][:, :, :]).then_inc(stored, 16)

            load_x(0, 0)
            load_x(1, 1)
            load_adj(0, 0)
            sp.wait_ge(consts, 5)
            sp.dma_start(sums[TOK:TOK + SPARE, :].rearrange("(p r) d -> p r d", p=FP), fill[:, :, 0:D]).then_inc(filled, 16)
            over_batches(sp, body)
            sp.wait_ge(stored, 16 * B)
            sp.wait_ge(filled, 16 * (B + 1))

        @block.gpsimd
        def _(pool):
            pool.memset(ones[:, :], 1.0).then_inc(consts, 1)
            pool.memset(power[:, :], -0.5).then_inc(consts, 1)
            pool.memset(fill[:, :, :], 0.0).then_inc(consts, 1)
            pool.iota(spare_i[:, :], pattern=[[1, FILL]], base=TOK, channel_multiplier=FILL).then_inc(consts, 1)
            pool.wait_ge(consts, 4)
            pool.tensor_copy(fill[:, :, D + 1], spare_i[:, :]).then_inc(consts, 1)

            def body(i, u, first, last):
                if exists(i + 2):
                    norm_in.power(pool, power, i + 2, u)
                pool.wait_ge(deg_ready, i + 1)
                pool.tensor_tensor(norm[u][:, :], deg[:, :], power[:, :], ALU.pow).then_inc(norm_ready, 1)

            norm_in.power(pool, power, 0, 0)
            norm_in.power(pool, power, 1, 1)
            over_batches(pool, body)

        @block.tensor
        def _(pe):
            pe.wait_ge(w_loaded, 64)
            pe.wait_ge(consts, 2)

            def out_transposes(i, u):
                pe.wait_ge(agg_ready, NH * i + NH)
                pe_last = transposes(pe, TP, aggT[:, :].rearrange("p (t n) -> p t n", t=T), ident)[-1]
                pe_last.then_inc(out_psum, 1)

            def body(i, u, first, last):
                pe.wait_ge(xn_ready, i + 1)
                wait(pe, dif_ready, i - 1)
                for mm in transposes(pe, TP, xn, ident):
                    mm.then_inc(xnT_psum, 1)
                pe.wait_ge(adj_loaded[u], 32 * (i - u) + 64)
                if not first:
                    pe.wait_ge(dpart_ready, NH * i)
                for h in range(NH):
                    for t in range(T):
                        g = 32 * (t % 4)
                        mm = pe.matmul(DG[g:g + 32, h * HALF:(h + 1) * HALF], ones[:, :],
                                       A[u][:, t, h * HALF:(h + 1) * HALF], start=(t < 4), stop=(t >= 4))
                    mm.then_inc(dpart_psum, 1)
                pe.wait_ge(xnT_ready, NH * i + NH)
                pe.wait_ge(dpart_ready, NH * i + NH)
                transposes(pe, TP, dpart[:, :].rearrange("p (t n) -> p t n", t=T), ident)[-1].then_inc(degT_psum, 1)
                for t in range(T):
                    if t >= 2:
                        pe.wait_ge(H_ready, T * i + t - 1)
                    pe.matmul(FG[:, t % 2, 0:3 * D], xnT[:, t * P:(t + 1) * P],
                              W[:, :, :].rearrange("p a n -> p (a n)"), start=True, stop=True).then_inc(fgh_psum, 1)
                if not first:
                    pe.wait_ge(norm_ready, i + 1)
                    out_transposes(i - 1, 1 - u)
                pe.wait_ge(FZ_ready, T * i + T)
                for h in range(NH):
                    if not first:
                        pe.wait_ge(agg_ready, NH * (i - 1) + h + 1)
                    for t in range(T):
                        mm = pe.matmul(AG[:, h * HALF:(h + 1) * HALF], F[:, t, :],
                                       A[u][:, t, h * HALF:(h + 1) * HALF], start=(t == 0), stop=(t == T - 1))
                    mm.then_inc(agg_psum, 1)
                if last:
                    pe.wait_ge(dif_ready, i)
                    out_transposes(i, u)

            over_batches(pe, body)

        @block.scalar
        def _(act):
            def elu_exp(i):
                act.wait_ge(O_min, i + 1)
                act.activation(E[:, :, :], E[:, :, :], ACT.Exp).then_inc(E_ready, 1)

            def body(i, u, first, last):
                for h in range(NH):
                    act.wait_ge(xnT_psum, NH * i + h + 1)
                    act.activation(xnT[:, h * HALF:(h + 1) * HALF],
                                   TP[:, 4 * h:4 * h + 4, :].rearrange("p t n -> p (t n)"), ACT.Copy).then_inc(xnT_ready, 1)
                for h in range(NH):
                    act.wait_ge(dpart_psum, NH * i + h + 1)
                    act.activation(dpart[:, h * HALF:(h + 1) * HALF], DG[:, h * HALF:(h + 1) * HALF],
                                   ACT.Copy).then_inc(dpart_ready, 1)
                for t in range(T):
                    act.wait_ge(FZ_ready, T * i + t + 1)
                    act.activation(Hh[u][:, t, :], FG[:, t % 2, D:2 * D], ACT.Copy).then_inc(H_ready, 1)
                act.activation(Z[u][:, :, :], Z[u][:, :, :], ACT.Tanh, scale=0.5).then_inc(th_ready, 1)
                if not first:
                    elu_exp(i - 1)
                for h in range(NH):
                    act.wait_ge(agg_psum, NH * i + h + 1)
                    if not first:
                        act.wait_ge(out_psum, i)
                    act.activation(aggT[:, h * HALF:(h + 1) * HALF], AG[:, h * HALF:(h + 1) * HALF],
                                   ACT.Copy).then_inc(agg_ready, 1)
                if last:
                    elu_exp(i)

            over_batches(act, body)

        @block.vector
        def _(dve):
            chain = Chain(dve, dve_step)
            dve.wait_ge(w_loaded, 64)
            dve.wait_ge(consts, 2)

            def stats(i, u):
                dve.wait_ge(x_loaded[u], 8 * (i - u) + 16)
                norm_in.stats(dve, X[u], i, u)

            def norm_x(i, u):
                norm_in.apply(dve, X[u], xn, i, u).then_inc(xn_ready, 1)

            def finish(i, u):
                dve.wait_ge(out_psum, i + 1)
                dve.wait_ge(H_ready, T * i + T)
                for t in range(T):
                    ins = dve.scalar_tensor_tensor(out=dif[:, t, :], in0=TP[:, t, :], scalar=norm[u][:, t:t + 1],
                                                   in1=Hh[u][:, t, :], op0=ALU.mult, op1=ALU.subtract)
                ins.then_inc(dif_ready, 1)
                dve.wait_ge(dif_ready, i + 1)
                dve.wait_ge(th_ready, i + 1)
                dve.wait_ge(r_loaded[u], 8 * (i - u) + 16)
                chain.link(dve.scalar_tensor_tensor(out=dif[:, :, :], in0=Z[u][:, :, :], scalar=1.0,
                                                    in1=dif[:, :, :], op0=ALU.add, op1=ALU.mult))
                chain.link(dve.scalar_tensor_tensor(out=O[:, :, :], in0=dif[:, :, :], scalar=0.5,
                                                    in1=Hh[u][:, :, :], op0=ALU.mult, op1=ALU.add))
                dve.tensor_scalar(E[:, :, :], O[:, :, :], 0.0, None, ALU.min).then_inc(O_min, 1)
                chain.link(dve.scalar_tensor_tensor(out=R[u][:, :, :], in0=O[:, :, :], scalar=0.0,
                                                    in1=R[u][:, :, :], op0=ALU.max, op1=ALU.add))
                dve.wait_ge(E_ready, i + 1)
                dve.scalar_tensor_tensor(out=R[u][:, :, :], in0=E[:, :, :], scalar=-1.0,
                                         in1=R[u][:, :, :], op0=ALU.add, op1=ALU.add).then_inc(out_ready, 1)

            def body(i, u, first, last):
                chain.at(0 if first else 4 * i - 3)
                if exists(i + 1):
                    dve.wait_ge(xnT_psum, NH * i + NH)
                    norm_x(i + 1, 1 - u)
                if exists(i + 2):
                    stats(i + 2, u)
                dve.wait_ge(degT_psum, i + 1)
                chain.link(dve.tensor_reduce(dsum[:, :], TP[:, :, :].rearrange("p t (g c) -> p t c g", c=32)[:, :, 0, :],
                                             AX.X, ALU.add))
                dve.tensor_scalar(deg[:, :], dsum[:, :], 1e-6, None, ALU.add).then_inc(deg_ready, 1)
                dve.wait_ge(norm_ready, i + 1)
                for t in range(T):
                    dve.wait_ge(fgh_psum, T * i + t + 1)
                    dve.tensor_scalar(F[:, t, :], FG[:, t % 2, 0:D], norm[u][:, t:t + 1], None, ALU.mult)
                    dve.tensor_tensor(Z[u][:, t, :], FG[:, t % 2, 2 * D:3 * D], bias[:, :], ALU.add).then_inc(FZ_ready, 1)
                if not first:
                    finish(i - 1, 1 - u)
                if last:
                    finish(i, u)

            stats(0, 0)
            stats(1, 1)
            norm_x(0, 0)
            over_batches(dve, body)


def over_groups(eng, body):
    assert GROUPS % 2 == 1
    body(0, 0, True, False)
    body(1, 1, False, False)
    with eng.Fori(1, GROUPS // 2) as j:
        body(2 * j, 0, False, False)
        body(2 * j + 1, 1, False, False)
    body(GROUPS - 1, 0, False, True)


def routing_stage(nc, x_in, rows, Wr, ident, slots, w_top, expert_of):
    with ExitStack() as ctx:
        sb = lambda name, shape, dt=fp32: ctx.enter_context(nc.sbuf_tensor("r_" + name, shape, dt))
        ps = lambda name, shape: ctx.enter_context(nc.psum_tensor("r_" + name, shape, fp32))
        sem = lambda name: ctx.enter_context(nc.semaphore("r_" + name))
        K = TOK // G

        W = sb("W", [P, E_N])
        power = sb("power", [P, T])
        ones = sb("ones", [P, P])
        before = sb("before", [P, P])
        order_i, order = sb("order_i", [P, TILES, E_N], i32), sb("order", [P, TILES, E_N])
        steps_i, steps = sb("steps_i", [P, E_N, K], i32), sb("steps", [P, E_N, K])
        group_i, group = sb("group_i", [P, ROUTED, E_N], i32), sb("group", [P, ROUTED, E_N])
        keep = sb("keep", [P, E_N, TILES])
        X = [sb(f"X{u}", [P, T, D]) for u in range(2)]
        xn = [sb(f"xn{u}", [P, T, D]) for u in range(2)]
        xnT = sb("xnT", [P, N])
        Lg = sb("Lg", [P, TILES, E_N])
        eq, sc = sb("eq", [P, TILES, E_N]), sb("sc", [P, TILES, E_N])
        hot = [sb(f"hot{k}", [P, TILES, E_N]) for k in range(2)]
        top = [sb(f"top{k}", [P, TILES]) for k in range(2)]
        best = sb("best", [P, TILES])
        gap, th = sb("gap", [P, TILES]), sb("th", [P, TILES])
        both, total = sb("both", [P, E_N, TILES]), sb("total", [P, E_N, TILES])
        upto, pos = sb("upto", [P, E_N, TILES]), sb("pos", [P, E_N, TILES])
        hit = sb("hit", [P, E_N, K])
        n_groups, group_end, start = sb("n_groups", [P, E_N]), sb("group_end", [P, E_N]), sb("start", [P, E_N])
        first_row = sb("first_row", [P, E_N])
        past = sb("past", [P, ROUTED, E_N])
        expert_f = sb("expert_f", [P, ROUTED])
        slot_f = sb("slot_f", [P, 2, TILES])

        TP = ps("TP", [P, T, P])
        LG = [ps(f"LG{u}", [P, T, E_N]) for u in range(2)]
        RK = ps("RK", [P, E_N, TILES])
        TT = ps("TT", [P, E_N, TILES])

        w_loaded, consts = sem("w_loaded"), sem("consts")
        x_loaded = [sem(f"x_loaded{u}") for u in range(2)]
        norm_in = LayerNorm(sb, sem)
        xn_ready = sem("xn_ready")
        rows_stored = [sem(f"rows_stored{u}") for u in range(2)]
        xnT_psum, xnT_ready = sem("xnT_psum"), sem("xnT_ready")
        logits_psum, logits_read = sem("logits_psum"), sem("logits_read")
        gap_ready, th_ready = sem("gap_ready"), sem("th_ready")
        both_ready, rank_psum, dve_step = sem("both_ready"), sem("rank_psum"), sem("dve_step")
        block = ctx.enter_context(nc.Block())
        N_CONST = 8

        @block.sync
        def _(sp):
            def load(i, u):
                wait(sp, xn_ready, i - 1)
                sp.dma_start(X[u][:, :, :], tiled(x_in[i])).then_inc(x_loaded[u], 16)

            def body(i, u, first, last):
                if exists(i + 2):
                    load(i + 2, u)
                sp.wait_ge(xn_ready, i + 1)
                sp.dma_start(tiled(rows[bass.ts(i, N), 0:D]), xn[u][:, :, :]).then_inc(rows_stored[u], 16)

            sp.dma_start(W[:, :], Wr).then_inc(w_loaded, 16)
            load(0, 0)
            load(1, 1)
            over_batches(sp, body)
            for u in range(2):
                sp.wait_ge(rows_stored[u], 16 * B // 2)

        @block.gpsimd
        def _(pool):
            pool.memset(power[:, :], -0.5).then_inc(consts, 1)
            pool.memset(ones[:, :], 1.0).then_inc(consts, 1)
            pool.memset(keep[:, :, :], 1.0).then_inc(consts, 1)
            pool.iota(order_i[:, :, :], pattern=[[0, TILES], [-1, E_N]], base=E_N, channel_multiplier=0).then_inc(consts, 1)
            pool.iota(steps_i[:, :, :], pattern=[[0, E_N], [G, K]], base=0, channel_multiplier=0).then_inc(consts, 1)
            pool.iota(group_i[:, :, :], pattern=[[1, ROUTED], [0, E_N]], base=0, channel_multiplier=0).then_inc(consts, 1)
            pool.wait_ge(consts, 6)
            pool.affine_select(out=before[:, :], in_=ones[:, :], compare_op=ALU.is_gt, fill=0.0, base=0,
                               pattern=[[1, P]], channel_multiplier=-1).then_inc(consts, 1)
            pool.memset(keep[:, :, 0:1], 0.0).then_inc(consts, 1)
            norm_in.power(pool, power, 0, 0)
            norm_in.power(pool, power, 1, 1)

            def body(i, u, first, last):
                if exists(i + 2):
                    norm_in.power(pool, power, i + 2, u)

            over_batches(pool, body)

        @block.tensor
        def _(pe):
            pe.wait_ge(w_loaded, 16)

            def body(i, u, first, last):
                pe.wait_ge(xn_ready, i + 1)
                wait(pe, xnT_ready, NH * i)
                for mm in transposes(pe, TP, xn[u], ident):
                    mm.then_inc(xnT_psum, 1)
                pe.wait_ge(xnT_ready, NH * i + NH)
                wait(pe, logits_read, i - 1)
                for t in range(T):
                    mm = pe.matmul(LG[u][:, t, :], xnT[:, t * P:(t + 1) * P], W[:, :], start=True, stop=True)
                mm.then_inc(logits_psum, 1)

            over_batches(pe, body)
            pe.wait_ge(both_ready, 1)
            pe.wait_ge(consts, N_CONST)
            pe.matmul(RK[:, :, :], before[:, :], both[:, :, :], start=True, stop=True).then_inc(rank_psum, 1)
            pe.matmul(TT[:, :, :], ones[:, :], both[:, :, :], start=True, stop=True).then_inc(rank_psum, 1)

        @block.scalar
        def _(act):
            def body(i, u, first, last):
                for h in range(NH):
                    act.wait_ge(xnT_psum, NH * i + h + 1)
                    wait(act, logits_psum, i)
                    act.activation(xnT[:, h * HALF:(h + 1) * HALF],
                                   TP[:, 4 * h:4 * h + 4, :].rearrange("p t n -> p (t n)"), ACT.Copy).then_inc(xnT_ready, 1)

            over_batches(act, body)
            act.wait_ge(gap_ready, 1)
            act.activation(th[:, :], gap[:, :], ACT.Tanh, scale=0.5).then_inc(th_ready, 1)

        @block.vector
        def _(dve):
            chain = Chain(dve, dve_step)
            by_tile = lambda a: a.rearrange("p t e -> p e t")
            flat = lambda a: a.rearrange("p e t -> p (e t)")
            wide = lambda a: a.unsqueeze(2).to_broadcast([P, TILES, E_N])

            def stats(i, u):
                dve.wait_ge(x_loaded[u], 8 * (i - u) + 16)
                norm_in.stats(dve, X[u], i, u)

            def norm_x(i, u):
                wait(dve, rows_stored[u], 8 * (i - u))
                norm_in.apply(dve, X[u], xn[u], i, u).then_inc(xn_ready, 1)

            def body(i, u, first, last):
                if exists(i + 1):
                    norm_x(i + 1, 1 - u)
                if exists(i + 2):
                    stats(i + 2, u)
                dve.wait_ge(logits_psum, i + 1)
                dve.tensor_copy(Lg[:, bass.ts(i, T), :], LG[u][:, :, :]).then_inc(logits_read, 1)

            stats(0, 0)
            stats(1, 1)
            norm_x(0, 0)
            over_batches(dve, body)
            dve.wait_ge(consts, N_CONST)
            dve.tensor_copy(steps[:, :, :], steps_i[:, :, :])
            dve.tensor_copy(group[:, :, :], group_i[:, :, :])
            chain.link(dve.tensor_copy(order[:, :, :], order_i[:, :, :]))
            dve.wait_ge(logits_read, B)
            for k in range(2):
                chain.link(dve.tensor_reduce(top[k][:, :], Lg[:, :, :], AX.X, ALU.max))
                chain.link(dve.tensor_tensor(eq[:, :, :], Lg[:, :, :], wide(top[k][:, :]), ALU.is_equal))
                chain.link(dve.tensor_tensor(sc[:, :, :], eq[:, :, :], order[:, :, :], ALU.mult))
                chain.link(dve.tensor_reduce(best[:, :], sc[:, :, :], AX.X, ALU.max))
                chain.link(dve.tensor_tensor(hot[k][:, :, :], sc[:, :, :], wide(best[:, :]), ALU.is_equal))
                if k == 0:
                    chain.link(dve.scalar_tensor_tensor(out=Lg[:, :, :], in0=hot[0][:, :, :], scalar=-3e38,
                                                        in1=Lg[:, :, :], op0=ALU.mult, op1=ALU.add))
            dve.tensor_tensor(both[:, :, :], by_tile(hot[0][:, :, :]), by_tile(hot[1][:, :, :]),
                              ALU.add).then_inc(both_ready, 1)
            dve.tensor_tensor(gap[:, :], top[0][:, :], top[1][:, :], ALU.subtract).then_inc(gap_ready, 1)
            dve.wait_ge(th_ready, 1)
            dve.tensor_scalar(w_top[:, 0, :], th[:, :], 0.5, 0.5, ALU.mult, ALU.add)
            chain.link(dve.tensor_scalar(w_top[:, 1, :], th[:, :], -0.5, 0.5, ALU.mult, ALU.add))
            dve.wait_ge(rank_psum, 2)
            dve.tensor_tensor_scan(flat(upto[:, :, :]), flat(keep[:, :, :]), flat(TT[:, :, :]), 0.0, ALU.mult, ALU.add)
            chain.link(dve.tensor_copy(total[:, :, :], TT[:, :, :]))
            chain.link(dve.tensor_tensor(hit[:, :, :], upto[:, :, TILES - 1:TILES].to_broadcast([P, E_N, K]),
                                         steps[:, :, :], ALU.is_gt))
            chain.link(dve.tensor_reduce(n_groups[:, :], hit[:, :, :], AX.X, ALU.add))
            dve.tensor_tensor(pos[:, :, :], upto[:, :, :], total[:, :, :], ALU.subtract)
            chain.link(dve.tensor_tensor_scan(group_end[:, :], ones[:, 0:E_N], n_groups[:, :], 0.0, ALU.mult, ALU.add))
            dve.tensor_tensor(start[:, :], group_end[:, :], n_groups[:, :], ALU.subtract)
            dve.tensor_tensor(past[:, :, :], group_end[:, :].unsqueeze(1).to_broadcast([P, ROUTED, E_N]),
                              group[:, :, :], ALU.is_le)
            chain.link(dve.tensor_tensor(total[:, :, :], RK[:, :, :], pos[:, :, :], ALU.add))
            dve.tensor_scalar(first_row[:, :], start[:, :], float(G), float(TOK), ALU.mult, ALU.add)
            chain.link(dve.tensor_reduce(expert_f[:, :], past[:, :, :], AX.X, ALU.add))
            dve.tensor_scalar(expert_of[:, :], expert_f[:, :], float(E_N - 1), None, ALU.min)
            chain.link(dve.tensor_tensor(pos[:, :, :], total[:, :, :],
                                         first_row[:, :].unsqueeze(2).to_broadcast([P, E_N, TILES]), ALU.add))
            for k in range(2):
                chain.link(dve.tensor_tensor(total[:, :, :], by_tile(hot[k][:, :, :]), pos[:, :, :], ALU.mult))
                chain.link(dve.tensor_reduce(slot_f[:, k, :], total[:, :, :].rearrange("p e t -> p t e"), AX.X, ALU.add))
            chain.link(dve.tensor_copy(slots[:, :, :], slot_f[:, :, :]))


def experts_stage(nc, x_in, rows, sums, blobs, ident, slots, w_top, expert_of):
    with ExitStack() as ctx:
        sb = lambda name, shape, dt=fp32: ctx.enter_context(nc.sbuf_tensor("e_" + name, shape, dt))
        ps = lambda name, shape: ctx.enter_context(nc.psum_tensor("e_" + name, shape, fp32))
        sem = lambda name: ctx.enter_context(nc.semaphore("e_" + name))

        S = [[sb(f"S{u}{k}", [P, T, ROW]) for k in range(2)] for u in range(2)]
        to = [sb(f"to{u}", [P, 2, T], u32) for u in range(2)]
        token_i, token = sb("token_i", [P, TILES], i32), sb("token", [P, TILES])
        Wb = [sb(f"W{u}", [P, BLOB]) for u in range(2)]
        X = [sb(f"X{u}", [P, RT, ROW]) for u in range(2)]
        R = [sb(f"R{u}", [P, RT, D]) for u in range(2)]
        meta = [sb(f"meta{u}", [P, RT, 2]) for u in range(2)]
        result = [sb(f"result{u}", [P, RT], u32) for u in range(2)]
        xT = [sb(f"xT{u}", [P, G]) for u in range(2)]
        hT = sb("hT", [P, FT, G])
        yT = [sb(f"yT{u}", [P, RT, P]) for u in range(2)]
        Y = [sb(f"Y{u}", [P, RT, D]) for u in range(2)]
        TX, TY = ps("TX", [P, RT, P]), ps("TY", [P, RT, P])
        UP = ps("UP", [P, FT, G])
        DN = ps("DN", [P, 2, G])

        s_loaded = [sem(f"s_loaded{u}") for u in range(2)]
        token_ready, to_ready, sent = sem("token_ready"), sem("to_ready"), [sem(f"sent{u}") for u in range(2)]
        w_loaded = [sem(f"w_loaded{u}") for u in range(2)]
        x_loaded = [sem(f"x_loaded{u}") for u in range(2)]
        r_loaded = [sem(f"r_loaded{u}") for u in range(2)]
        xT_psum, xT_ready = sem("xT_psum"), sem("xT_ready")
        up_psum, h_ready = sem("up_psum"), sem("h_ready")
        dn_psum, yT_ready = sem("dn_psum"), sem("yT_ready")
        y_psum, y_ready = sem("y_psum"), sem("y_ready")
        y_stored = [sem(f"y_stored{u}") for u in range(2)]
        added, meta_ready, rounds = sem("added"), sem("meta_ready"), sem("rounds")
        block = ctx.enter_context(nc.Block())

        def w1(u, f):
            return Wb[u][:, f * P:(f + 1) * P]

        def b1(u, f):
            return Wb[u][:, F_N + f:F_N + f + 1]

        def w2(u, f):
            return Wb[u][:, F_N + FT + f * D:F_N + FT + (f + 1) * D]

        def b2(u):
            return Wb[u][:, BLOB - 1:BLOB]

        x_rows = x_in.rearrange("b n d -> (b n) d")

        @block.sync
        def _(sp):
            def load_w(g, u, expert):
                wait(sp, yT_ready, g - 1)
                sp.dma_start(Wb[u][:, :], blobs[expert]).then_inc(w_loaded[u], 16)

            def routed_expert(g):
                return sp.value_load(expert_of[0:1, bass.ds(g - SHARED, 1)], min_val=0, max_val=E_N - 1)

            def load_x(g, u, cols):
                wait(sp, xT_ready, g - 1)
                sp.dma_start(X[u][:, :, 0:cols], tiled(rows[bass.ts(g, G), 0:cols])).then_inc(x_loaded[u], 16)

            def load_r(g, u):
                wait(sp, y_ready, g - 1)
                sp.dma_start(R[u][:, :, :], tiled(x_rows[bass.ts(g, G), :])).then_inc(r_loaded[u], 16)

            def store(g, u):
                sp.wait_ge(y_ready, g + 1)
                sp.dma_start(tiled(sums[bass.ts(g, G), :]), Y[u][:, :, :]).then_inc(y_stored[u], 16)

            load_x(0, 0, D)
            load_w(0, 0, E_N)
            load_x(1, 1, D)
            load_w(1, 1, E_N)
            load_r(0, 0)
            load_x(2, 0, D)
            load_r(1, 1)
            load_x(3, 1, D)
            with sp.Fori(1, SHARED // 2 - 1) as j:
                for u in range(2):
                    g = 2 * j + u
                    load_w(g, u, E_N)
                    load_x(g + 2, u, D)
                    store(g - 2, u)
                    load_r(g, u)
            for g in (SHARED - 2, SHARED - 1):
                load_w(g, g % 2, E_N)
                store(g - 2, g % 2)
                load_r(g, g % 2)
            for u in range(2):
                sp.wait_ge(sent[u], 16 * TILES)
            for g in (SHARED, SHARED + 1):
                load_x(g, g % 2, ROW)
            for g in (SHARED, SHARED + 1):
                load_w(g, g % 2, routed_expert(g))
                load_x(g + 2, g % 2, ROW)
                store(g - 2, g % 2)
            with sp.Fori(SHARED // 2 + 1, GROUPS // 2 - 1) as j:
                for u in range(2):
                    g = 2 * j + u
                    load_w(g, u, routed_expert(g))
                    load_x(g + 2, u, ROW)
            for g in range(GROUPS - 3, GROUPS):
                load_w(g, g % 2, routed_expert(g))
                if g + 2 < GROUPS:
                    load_x(g + 2, g % 2, ROW)

        @block.gpsimd
        def _(pool):
            limit = pool.to_reg(TOK + ROUTED * G - 1)
            sums_limit = pool.to_reg(TOK + SPARE - 1)
            pool.iota(token_i[:, :], pattern=[[P, TILES]], base=0, channel_multiplier=1).then_inc(token_ready, 1)
            pool.wait_ge(token_ready, 1)
            pool.tensor_copy(token[:, :], token_i[:, :]).then_inc(token_ready, 1)

            def load(i, u):
                wait(pool, sent[u], 128 * (i - u))
                for k in range(2):
                    pool.dma_start(S[u][k][:, :, 0:D], tiled(rows[bass.ts(i, N), 0:D])).then_inc(s_loaded[u], 16)

            def send(i, u, first, last):
                if not last:
                    load(i + 1, 1 - u)
                pool.wait_ge(token_ready, 2)
                wait(pool, sent[u], 128 * (i - u))
                for k in range(2):
                    pool.tensor_copy(S[u][k][:, :, D], w_top[:, k, bass.ts(i, T)])
                    pool.tensor_copy(S[u][k][:, :, D + 1], token[:, bass.ts(i, T)])
                pool.tensor_copy(to[u][:, :, :], slots[:, :, bass.ts(i, T)]).then_inc(to_ready, 1)
                pool.wait_ge(to_ready, i + 1)
                pool.wait_ge(s_loaded[u], 16 * (i - u) + 32)
                pool.sem_inc(rounds, 1)
                for k in range(2):
                    for t in range(T):
                        pool.indirect_dma_start(
                            rows, bass.IndirectOffsetOnAxis(ap=to[u][:, k, t:t + 1], axis=0),
                            S[u][k][:, t, :], None, bounds_check=limit).then_inc(sent[u], 16)

            load(0, 0)
            over_batches(pool, send)
            for u in range(2):
                pool.wait_ge(y_stored[u], 16 * SHARED // 2)

            def add(g, u):
                pool.wait_ge(y_ready, g + 1)
                wait(pool, added, 16 * RT * (g - SHARED))
                pool.sem_inc(rounds, 1)
                for t in range(RT):
                    pool.indirect_dma_start(
                        sums, bass.IndirectOffsetOnAxis(ap=result[u][:, t:t + 1], axis=0),
                        Y[u][:, t, :], None, bounds_check=sums_limit, compute_op=ALU.add).then_inc(added, 16)

            add(SHARED, 0)
            with pool.Fori(SHARED // 2, (GROUPS - 1) // 2) as j:
                add(2 * j + 1, 1)
                add(2 * j + 2, 0)
            pool.wait_ge(added, 16 * RT * ROUTED)

        @block.tensor
        def _(pe):
            def x_transposes(g, u):
                pe.wait_ge(x_loaded[u], 8 * (g - u) + 16)
                wait(pe, xT_ready, g)
                for t in range(RT):
                    mm = pe.transpose(TX[:, t, :], X[u][:, t, 0:D], ident[:, :])
                mm.then_inc(xT_psum, 1)

            def y_transposes(g, u):
                pe.wait_ge(yT_ready, g + 1)
                wait(pe, y_ready, g)
                for t in range(RT):
                    mm = pe.transpose(TY[:, t, :], yT[u][:, t, :], ident[:, :])
                mm.then_inc(y_psum, 1)

            def body(g, u, first, last):
                pe.wait_ge(xT_ready, g + 1)
                pe.wait_ge(w_loaded[u], 8 * (g - u) + 16)
                for f in range(FT):
                    wait(pe, h_ready, FT * g - FT + f + 1)
                    pe.matmul(UP[:, f, :], w1(u, f), xT[u][:, :], start=True, stop=True).then_inc(up_psum, 1)
                if not first:
                    y_transposes(g - 1, 1 - u)
                if not last:
                    x_transposes(g + 1, 1 - u)
                for f in range(FT):
                    pe.wait_ge(h_ready, FT * g + f + 1)
                    mm = pe.matmul(DN[:, u, :], w2(u, f), hT[:, f, :], start=(f == 0), stop=(f == FT - 1))
                mm.then_inc(dn_psum, 1)
                if last:
                    y_transposes(g, u)

            x_transposes(0, 0)
            over_groups(pe, body)

        @block.scalar
        def _(act):
            def body(g, u, first, last):
                act.wait_ge(w_loaded[u], 8 * (g - u) + 16)
                wait(act, dn_psum, g)
                for f in range(FT):
                    act.wait_ge(up_psum, FT * g + f + 1)
                    act.activation(hT[:, f, :], UP[:, f, :], ACT.Gelu, bias=b1(u, f)).then_inc(h_ready, 1)
                act.wait_ge(dn_psum, g + 1)
                wait(act, y_psum, g - 1)
                act.activation(yT[u][:, :, :], DN[:, u, :].rearrange("p (t n) -> p t n", t=RT),
                               ACT.Identity, bias=b2(u)).then_inc(yT_ready, 1)

            over_groups(act, body)

        @block.vector
        def _(dve):
            def copy_x(g, u, routed):
                dve.wait_ge(xT_psum, g + 1)
                wait(dve, up_psum, FT * (g - 1))
                if routed:
                    dve.wait_ge(y_ready, g - 1)
                    dve.tensor_copy(meta[u][:, :, :], X[u][:, :, D:D + 2]).then_inc(meta_ready, 1)
                dve.tensor_copy(xT[u][:, :], TX[:, :, :].rearrange("p t n -> p (t n)")).then_inc(xT_ready, 1)

            def shared_y(g, u):
                dve.wait_ge(y_psum, g + 1)
                dve.wait_ge(r_loaded[u], 8 * (g - u) + 16)
                wait(dve, y_stored[u], 8 * (g - u))
                dve.tensor_tensor(Y[u][:, :, :], TY[:, :, :], R[u][:, :, :], ALU.add).then_inc(y_ready, 1)

            def routed_y(g, u):
                dve.wait_ge(y_psum, g + 1)
                dve.wait_ge(meta_ready, g - SHARED + 1)
                dve.wait_ge(y_stored[u], 16 * SHARED // 2)
                wait(dve, added, 16 * RT * (g - SHARED - 1))
                dve.tensor_copy(result[u][:, :], meta[u][:, :, 1])
                for t in range(RT):
                    ins = dve.tensor_scalar(Y[u][:, t, :], TY[:, t, :], meta[u][:, t, 0:1], None, ALU.mult)
                ins.then_inc(y_ready, 1)

            def step(g, u, y=routed_y, routed=True):
                y(g - 1, 1 - u)
                copy_x(g + 1, 1 - u, routed)

            copy_x(0, 0, False)
            copy_x(1, 1, False)
            step(1, 1, shared_y, False)
            with dve.Fori(1, SHARED // 2 - 1) as j:
                for u in range(2):
                    step(2 * j + u, u, shared_y, False)
            step(SHARED - 2, 0, shared_y, False)
            step(SHARED - 1, 1, shared_y, True)
            step(SHARED, 0, shared_y, True)
            for g in range(SHARED + 1, SHARED + 4):
                step(g, g % 2)
            with dve.Fori(SHARED // 2 + 2, GROUPS // 2) as j:
                for u in range(2):
                    step(2 * j + u, u)
            routed_y(GROUPS - 2, 1)
            routed_y(GROUPS - 1, 0)


HEADS, HD = 4, D // 4
ADJ_BUFS = 3
BUF_TILES = [len(range(b, T, ADJ_BUFS)) for b in range(ADJ_BUFS)]


def over_graphs(eng, body):
    body(0, True, False)
    with eng.Fori(1, B - 1) as i:
        body(i, False, False)
    body(B - 1, False, True)


def attention_gnn_stage(nc, x_in, x_out, adjT, W_lin, b_lin, W_q, W_k, ln_g, ln_b, ident):
    with ExitStack() as ctx:
        sb = lambda name, shape, dt=fp32: ctx.enter_context(nc.sbuf_tensor("c_" + name, shape, dt))
        ps = lambda name, shape: ctx.enter_context(nc.psum_tensor("c_" + name, shape, fp32))
        sem = lambda name: ctx.enter_context(nc.semaphore("c_" + name))

        W = sb("W", [P, 3, D])
        bias, gain, shift = sb("bias", [P, D]), sb("gain", [P, D]), sb("shift", [P, D])
        ones = sb("ones", [P, HD])
        power = sb("power", [P, T * HEADS])
        AH = sb("AH", [P, T, HEADS, N])
        QS, KS = sb("QS", [P, HEADS, N], fp32r), sb("KS", [P, HEADS, N], fp32r)
        A = [sb(f"A{b}", [P, N]) for b in range(ADJ_BUFS)]
        X = sb("X", [P, T, D])
        xnT = sb("xnT", [P, N])
        L = sb("L", [P, N])
        F = sb("F", [P, N])
        H = sb("H", [P, N], fp32r)
        XT = sb("XT", [P, T, D])
        R = sb("R", [P, T, D])
        deg, mask = sb("deg", [P, T, HEADS]), sb("mask", [P, T, HEADS])
        pw, dis = sb("pw", [P, T, HEADS]), sb("dis", [P, T, HEADS])

        S = [ps(f"S{u}", [P, N]) for u in range(2)]
        DG, YA = ps("DG", [P, N]), ps("YA", [P, N])

        w_loaded, consts = sem("w_loaded"), sem("consts")
        x_loaded, r_loaded, stored = sem("x_loaded"), sem("r_loaded"), sem("stored")
        adj_loaded = [sem(f"adj_loaded{b}") for b in range(ADJ_BUFS)]
        norm_in = LayerNorm(lambda n, s: sb("i" + n, s), lambda n: sem("i" + n))
        norm_y = LayerNorm(lambda n, s: sb("y" + n, s), lambda n: sem("y" + n))
        xn_ready, xnT_psum, xnT_ready, proj_psum = sem("xn_ready"), sem("xnT_psum"), sem("xnT_ready"), sem("proj_psum")
        l_ready, f_ready, h_ready, lo_ready = sem("l_ready"), sem("f_ready"), sem("h_ready"), sem("lo_ready")
        stacked = [sem("q_stacked"), sem("k_stacked")]
        xb_ready, XT_ready = sem("xb_ready"), sem("XT_ready")
        s_psum, att_ready, ah_ready = sem("s_psum"), sem("att_ready"), sem("ah_ready")
        dg_psum, dT_ready, degT_psum = sem("dg_psum"), sem("dT_ready"), sem("degT_psum")
        deg_ready, pow_ready, xs_ready = sem("deg_ready"), sem("pow_ready"), sem("xs_ready")
        y_psum, yT_ready, yTr_psum = sem("y_psum"), sem("yT_ready"), sem("yTr_psum")
        ys_ready, Rb_ready, out_ready = sem("ys_ready"), sem("Rb_ready"), sem("out_ready")
        dve_step = sem("dve_step")
        block = ctx.enter_context(nc.Block())

        by_head = lambda a: a.rearrange("p t (h c) -> p t h c", h=HEADS)
        tiles = lambda a: a[:, :].rearrange("p (t n) -> p t n", t=T)
        Yn = tiles(xnT)
        PARTS = 2

        @block.sync
        def _(sp):
            row = lambda b: b.rearrange("(a n) -> a n", a=1).to_broadcast([P, D])
            for k, w in enumerate((W_q, W_k, W_lin)):
                sp.dma_start(W[:, k, :], w).then_inc(w_loaded, 16)
            for dst, src in ((bias, b_lin), (gain, ln_g), (shift, ln_b)):
                sp.dma_start(dst[:, :], row(src)).then_inc(w_loaded, 16)

            def load_x(i):
                wait(sp, xnT_psum, i)
                sp.dma_start(X[:, :, :], tiled(x_in[i])).then_inc(x_loaded, 16)

            def load_adj(i, t):
                b = t % ADJ_BUFS
                before = t - ADJ_BUFS if t >= ADJ_BUFS else max(range(b, T, ADJ_BUFS)) - T
                wait(sp, ah_ready, 2 * T * i + 2 * before + 2)
                sp.dma_start(A[b][:, :], adjT[i, t * P:(t + 1) * P, :]).then_inc(adj_loaded[b], 16)

            def stack(i, k):
                sp.wait_ge(lo_ready, PARTS * i + k + 1)
                dst, parts = ((QS, (H, F, H, F)), (KS, (H, H, F, F)))[k]
                for h in range(HEADS):
                    for q, src in enumerate(parts):
                        part = src[h * HD:(h + 1) * HD, :]
                        sp.dma_start(dst[q * HD:(q + 1) * HD, h, :].bitcast(fp32),
                                     part.bitcast(fp32) if src is H else part).then_inc(stacked[k], 16)

            def body(i, first, last):
                for t in range(ADJ_BUFS, T):
                    load_adj(i, t)
                if not first:
                    store(i - 1)
                sp.dma_start(R[:, :, :], tiled(x_in[i])).then_inc(r_loaded, 16)
                if not last:
                    for t in range(ADJ_BUFS):
                        load_adj(i + 1, t)
                    for k in range(2):
                        stack(i + 1, k)
                    if not isinstance(i, int) or i + 2 < B:
                        load_x_after(i + 2)

            def load_x_after(i):
                load_x(i)

            def store(i):
                sp.wait_ge(out_ready, i + 1)
                sp.dma_start(tiled(x_out[i]), R[:, :, :]).then_inc(stored, 16)
                sp.wait_ge(stored, 16 * i + 16)

            load_x(0)
            for t in range(ADJ_BUFS):
                load_adj(0, t)
            for k in range(2):
                stack(0, k)
            load_x(1)
            body(0, True, False)
            with sp.Fori(1, B - 2) as i:
                body(i, False, False)
            body(B - 2, False, False)
            body(B - 1, False, True)
            store(B - 1)

        @block.gpsimd
        def _(pool):
            pool.memset(ones[:, :], 1.0).then_inc(consts, 1)
            pool.memset(power[:, :], -0.5).then_inc(consts, 1)
            pool.wait_ge(consts, 2)
            pool.wait_ge(w_loaded, 96)
            norm_in.power(pool, power, 0, 0)

            def body(i, first, last):
                if not first:
                    norm_y.power(pool, power, i - 1, 0)
                if not last:
                    norm_in.power(pool, power, i + 1, 0)
                pool.wait_ge(deg_ready, i + 1)
                pool.tensor_tensor(pw[:, :, :].rearrange("p t h -> p (t h)"), deg[:, :, :].rearrange("p t h -> p (t h)"),
                                   power[:, :], ALU.pow).then_inc(pow_ready, 1)
                pool.wait_ge(r_loaded, 16 * i + 16)
                pool.tensor_tensor(R[:, :, :], R[:, :, :], shift[:, :].unsqueeze(1).to_broadcast([P, T, D]),
                                   ALU.add).then_inc(Rb_ready, 1)

            over_graphs(pool, body)
            norm_y.power(pool, power, B - 1, 0)

        @block.tensor
        def _(pe):
            pe.wait_ge(w_loaded, 96)
            pe.wait_ge(consts, 2)

            def xn_transposes(i):
                pe.wait_ge(xn_ready, i + 1)
                wait(pe, att_ready, HEADS * T * i)
                transposes(pe, tiles(S[0]), X, ident)[-1].then_inc(xnT_psum, 1)

            def projections(i):
                pe.wait_ge(xnT_ready, i + 1)
                for k in range(2):
                    if k == 1:
                        wait(pe, deg_ready, i)
                    for h in range(NH):
                        cols = slice(h * HALF, (h + 1) * HALF)
                        mm = pe.matmul(S[k][:, cols], W[:, k, :], xnT[:, cols], start=True, stop=True)
                    mm.then_inc(proj_psum, 1)
                for t in range(T):
                    mm = pe.matmul(DG[:, t * P:(t + 1) * P], xnT[:, t * P:(t + 1) * P], W[:, 2, :], start=True, stop=True)
                mm.then_inc(proj_psum, 1)

            def scores(i, t, h):
                wait(pe, att_ready, HEADS * T * i + HEADS * t + h - 1)
                if t == 0 and h < 2:
                    pe.wait_ge(f_ready, 2 * i + h + 1)
                    wait(pe, ys_ready, i)
                for half in range(NH):
                    cols = slice(half * HALF, (half + 1) * HALF)
                    mm = pe.matmul(S[h % 2][:, cols], KS[:, h, t * P:(t + 1) * P], QS[:, h, cols], start=True, stop=True)
                mm.then_inc(s_psum, 1)

            def by_columns(out, t, lhsT):
                for half in range(NH):
                    cols = slice(half * HALF, (half + 1) * HALF)
                    for h in range(HEADS):
                        mm = pe.matmul(out[h * HD:(h + 1) * HD, cols], lhsT(h), AH[:, t, h, cols],
                                       start=(t == 0), stop=(t == T - 1))
                return mm

            def degrees(i, t):
                if t == 0:
                    pe.wait_ge(xb_ready, i + 1)
                pe.wait_ge(ah_ready, 2 * T * i + 2 * t + 2)
                return by_columns(DG, t, lambda h: ones[:, :])

            def body(i, first, last):
                for k in range(2):
                    pe.wait_ge(stacked[k], 16 * 16 * i + 16 * 16)
                for t in range(T):
                    for h in range(HEADS):
                        scores(i, t, h)
                    if t > 0:
                        degrees(i, t - 1)
                degrees(i, T - 1).then_inc(dg_psum, 1)
                if not last:
                    xn_transposes(i + 1)
                pe.wait_ge(dT_ready, i + 1)
                pe.wait_ge(att_ready, HEADS * T * i + HEADS * T)
                transposes(pe, tiles(S[1]), tiles(L), ident)[-1].then_inc(degT_psum, 1)
                if not last:
                    projections(i + 1)
                pe.wait_ge(xs_ready, i + 1)
                for t in range(T):
                    mm = by_columns(YA, t, lambda h: XT[:, t, h * HD:(h + 1) * HD])
                mm.then_inc(y_psum, 1)
                pe.wait_ge(yT_ready, i + 1)
                if not last:
                    pe.wait_ge(f_ready, 2 * i + 3)
                transposes(pe, tiles(S[0]), tiles(L), ident)[-1].then_inc(yTr_psum, 1)

            xn_transposes(0)
            projections(0)
            over_graphs(pe, body)

        @block.scalar
        def _(act):
            def copy_xnT(i):
                act.wait_ge(xnT_psum, i + 1)
                wait(act, out_ready, i - 1)
                act.activation(xnT[:, :], S[0][:, :], ACT.Copy).then_inc(xnT_ready, 1)

            def split(i, k):
                act.wait_ge(proj_psum, 3 * i + k + 1)
                if k == 0:
                    wait(act, degT_psum, i)
                    wait(act, yTr_psum, i - 1)
                else:
                    act.wait_ge(f_ready, 2 * i + 1)
                act.activation(L[:, :], S[k][:, :], ACT.Copy, scale=0.01).then_inc(l_ready, 1)
                act.wait_ge(f_ready, 2 * i + k + 1)
                act.activation(H[:, :], F[:, :], ACT.Copy).then_inc(h_ready, 1)

            def leak_X(i):
                act.wait_ge(xb_ready, i + 1)
                act.activation(L[:, :], XT[:, :, :].rearrange("p t d -> p (t d)"), ACT.Copy,
                               scale=0.01).then_inc(l_ready, 1)

            def copy_YT(i):
                act.wait_ge(XT_ready, i + 2) if exists(i + 1) else None
                act.activation(L[:, :], YA[:, :], ACT.Copy).then_inc(yT_ready, 1)

            def body(i, first, last):
                for t in range(T):
                    for h in range(HEADS):
                        act.wait_ge(s_psum, HEADS * T * i + HEADS * t + h + 1)
                        if t == 0 and h == 0:
                            wait(act, y_psum, i)
                        act.activation(AH[:, t, h, :], S[h % 2][:, :], ACT.Sigmoid, scale=HD ** -0.5).then_inc(att_ready, 1)
                act.wait_ge(dg_psum, i + 1)
                wait(act, yTr_psum, i)
                act.activation(L[:, :], DG[:, :], ACT.Copy).then_inc(dT_ready, 1)
                if not last:
                    copy_xnT(i + 1)
                    for k in range(2):
                        split(i + 1, k)
                    leak_X(i + 1)
                act.wait_ge(y_psum, i + 1)
                if last:
                    act.activation(L[:, :], YA[:, :], ACT.Copy).then_inc(yT_ready, 1)
                else:
                    copy_YT(i)

            copy_xnT(0)
            for k in range(2):
                split(0, k)
            leak_X(0)
            over_graphs(act, body)

        @block.vector
        def _(dve):
            chain = Chain(dve, dve_step)
            dve.wait_ge(w_loaded, 96)
            dve.wait_ge(consts, 2)

            def norm_x(i):
                dve.wait_ge(x_loaded, 16 * i + 16)
                norm_in.stats(dve, X, i, 0)
                norm_in.apply(dve, X, X, i, 0).then_inc(xn_ready, 1)

            def split(i, k):
                dve.wait_ge(l_ready, 3 * i + k + 1)
                if k == 1:
                    dve.wait_ge(stacked[0], 256 * i + 256)
                else:
                    wait(dve, stacked[1], 256 * i)
                dve.tensor_tensor(F[:, :], S[k][:, :], L[:, :], ALU.max).then_inc(f_ready, 1)
                dve.wait_ge(h_ready, 2 * i + k + 1)
                dve.tensor_tensor(F[:, :].bitcast(fp32r), F[:, :], H[:, :].bitcast(fp32), ALU.subtract).then_inc(lo_ready, 1)

            def lift_X(i):
                dve.wait_ge(proj_psum, 3 * i + 3)
                wait(dve, y_psum, i)
                dve.tensor_tensor(XT[:, :, :], tiles(DG), bias[:, :].unsqueeze(1).to_broadcast([P, T, D]),
                                  ALU.add).then_inc(xb_ready, 1)
                dve.wait_ge(l_ready, 3 * i + 3)
                dve.tensor_tensor(XT[:, :, :], XT[:, :, :], tiles(L), ALU.max).then_inc(XT_ready, 1)

            def scale_Y(i):
                dve.wait_ge(yTr_psum, i + 1)
                dve.tensor_tensor(by_head(Yn), by_head(tiles(S[0])), dis[:, :, :].unsqueeze(3).to_broadcast([P, T, HEADS, HD]),
                                  ALU.mult).then_inc(ys_ready, 1)

            def finish(i):
                dve.wait_ge(ys_ready, i + 1)
                norm_y.stats(dve, Yn, i, 0)
                chain.at(3 * i + 1)
                chain.link(norm_y.apply(dve, Yn, Yn, i, 0))
                chain.link(dve.tensor_tensor(Yn, Yn, gain[:, :].unsqueeze(1).to_broadcast([P, T, D]), ALU.mult))
                dve.wait_ge(Rb_ready, i + 1)
                dve.tensor_tensor(R[:, :, :], Yn, R[:, :, :], ALU.add).then_inc(out_ready, 1)

            def body(i, first, last):
                for t in range(T):
                    b = t % ADJ_BUFS
                    dve.wait_ge(adj_loaded[b], 16 * (BUF_TILES[b] * i + t // ADJ_BUFS + 1))
                    for p in range(2):
                        dve.wait_ge(att_ready, HEADS * T * i + HEADS * t + 2 * p + 2)
                        dve.tensor_tensor(AH[:, t, 2 * p:2 * p + 2, :], AH[:, t, 2 * p:2 * p + 2, :],
                                          A[b][:, :].unsqueeze(1).to_broadcast([P, 2, N]), ALU.mult).then_inc(ah_ready, 1)
                    if t == 0 and not first:
                        finish(i - 1)
                    if t == 1 and not last:
                        norm_x(i + 1)
                dve.wait_ge(degT_psum, i + 1)
                chain.at(3 * i)
                degT = S[1][:, :].rearrange("p (t h c) -> p t h c", t=T, h=HEADS)[:, :, :, 0]
                dve.tensor_scalar(mask[:, :, :], degT, 0.0, None, ALU.is_gt)
                dve.tensor_scalar(deg[:, :, :], degT, 1.1754944e-38, None, ALU.max).then_inc(deg_ready, 1)
                dve.wait_ge(pow_ready, i + 1)
                chain.link(dve.tensor_tensor(dis[:, :, :], pw[:, :, :], mask[:, :, :], ALU.mult))
                dve.wait_ge(XT_ready, i + 1)
                dve.tensor_tensor(by_head(XT[:, :, :]), by_head(XT[:, :, :]),
                                  dis[:, :, :].unsqueeze(3).to_broadcast([P, T, HEADS, HD]), ALU.mult).then_inc(xs_ready, 1)
                if not last:
                    for k in range(2):
                        split(i + 1, k)
                    lift_X(i + 1)
                scale_Y(i)

            norm_x(0)
            for k in range(2):
                split(0, k)
            lift_X(0)
            over_graphs(dve, body)
            finish(B - 1)


SH, SP_, G_N = 8, 64, 64
INNER = SH * SP_
KT = INNER // P
NS = 64
CONV_K = 3
IN_PROJ = 2 * INNER + 2 * NS + 2 * SH
LAG = 2
SW_BUFS = 4


def slicing_stage(nc, x_in, W_x, b_xT, W_sliceT, b_slice, temperature, W_fxT, b_fx, ident, SWT, ST, scratch):
    with ExitStack() as ctx:
        sb = lambda name, shape, dt=fp32: ctx.enter_context(nc.sbuf_tensor("s_" + name, shape, dt))
        ps = lambda name, shape: ctx.enter_context(nc.psum_tensor("s_" + name, shape, fp32))
        sem = lambda name: ctx.enter_context(nc.semaphore("s_" + name))

        wx = scratch[0:SP_, 0:SH * P].rearrange("c (h d) -> c h d", h=SH)
        bx = scratch[0:SP_, SH * P:2 * SH * P].rearrange("c (h d) -> c h d", h=SH)
        bxc, wsl = sb("bxc", [SP_, SH]), sb("wsl", [SP_, G_N])
        bsl, temp = sb("bsl", [P, G_N]), sb("temp", [P, SH])
        Wc, bias = sb("Wc", [P, INNER]), sb("bias", [P, INNER])
        wfx, bfx = sb("wfx", [P, INNER]), sb("bfx", [1, INNER])
        power = sb("power", [P, T])
        X = sb("X", [P, T, D])
        xn = [sb(f"xn{u}", [P, T, D + 1]) for u in range(2)]
        xnT = [sb(f"xnT{u}", [P, N]) for u in range(2)]
        SW = [sb(f"SW{k}", [P, SH, G_N]) for k in range(SW_BUFS)]
        top, total, inv = sb("top", [P, SH]), sb("total", [P, SH]), [sb(f"inv{u}", [P, SH]) for u in range(2)]
        sn, xs = sb("sn", [P, KT]), sb("xs", [P, KT, D + 1])
        xsT, snT = sb("xsT", [P, KT, P]), sb("snT", [1, KT, P])
        zeros = scratch[:, 2 * SH * P:2 * SH * P + 512]

        TP = ps("TP", [P, T, P])
        LG = [ps(f"LG{u}", [P, INNER]) for u in range(2)]
        XS = ps("XS", [P, KT, 256])
        SP_T = [ps(f"SPT{u}", [P, KT, P]) for u in range(2)]

        w_loaded, consts, x_loaded = sem("w_loaded"), sem("consts"), sem("x_loaded")
        norm_in = LayerNorm(sb, sem)
        xn_ready, xnT_psum, xnT_ready = sem("xn_ready"), sem("xnT_psum"), sem("xnT_ready")
        lg_psum, lg_read, centred = sem("lg_psum"), sem("lg_read"), sem("centred")
        exp_ready, inv_ready, sw_ready = sem("exp_ready"), sem("inv_ready"), sem("sw_ready")
        sw_used, swT_ready = sem("sw_used"), sem("swT_ready")
        xs_ready, xsT_psum, xsT_ready, st_psum, st_ready = (
            sem("xs_ready"), sem("xsT_psum"), sem("xsT_ready"), sem("st_psum"), sem("st_ready"))
        dve_step = sem("dve_step")
        block = ctx.enter_context(nc.Block())
        LOADS = 7
        SETUP_STEPS = 4

        @block.sync
        def _(sp):
            row = lambda b, parts: b.rearrange("(a n) -> a n", a=1).to_broadcast([parts, b.shape[0]])
            sp.dma_start(wx, W_x.rearrange("(h c) d -> c h d", c=SP_)).then_inc(w_loaded, 16)
            sp.dma_start(bxc[:, :], b_xT).then_inc(w_loaded, 16)
            sp.dma_start(wsl[:, :], W_sliceT).then_inc(w_loaded, 16)
            sp.dma_start(bsl[:, :], row(b_slice, P)).then_inc(w_loaded, 16)
            sp.dma_start(temp[:, :], row(temperature.rearrange("a h b c -> (a h b c)"), P)).then_inc(w_loaded, 16)
            sp.dma_start(wfx[:, :], W_fxT).then_inc(w_loaded, 16)
            sp.dma_start(bfx[:, :], row(b_fx, 1)).then_inc(w_loaded, 16)

            def load_x(i):
                wait(sp, xn_ready, i)
                sp.dma_start(X[:, :, :], tiled(x_in[i])).then_inc(x_loaded, 16)

            load_x(0)
            load_x(1)
            with sp.Fori(2, B) as i:
                load_x(i)

        @block.gpsimd
        def _(pool):
            pool.memset(power[:, :], -0.5).then_inc(consts, 1)
            pool.memset(top[:, :], -1.0)
            pool.memset(zeros, 0.0).then_inc(consts, 1)
            for u in range(2):
                pool.memset(xn[u][:, :, D:D + 1], 1.0).then_inc(consts, 1)
            pool.wait_ge(dve_step, 2)
            pool.wait_ge(consts, 4)
            pool.tensor_tensor(temp[:, :], temp[:, :], top[:, :], ALU.pow).then_inc(consts, 1)
            norm_in.power(pool, power, 0, 0)

            def body(i, u, first, last):
                for t in range(T):
                    pool.wait_ge(inv_ready, T * i + t + 1)
                    k = t % SW_BUFS
                    pool.tensor_tensor(SW[k][:, :, :], SW[k][:, :, :], inv[t % 2][:, :].unsqueeze(2).to_broadcast([P, SH, G_N]),
                                       ALU.mult).then_inc(sw_ready, 1)
                    if t == 3 and not last:
                        norm_in.power(pool, power, i + 1, 1 - u)

            over_batches(pool, body)

        @block.tensor
        def _(pe):
            pe.wait_ge(w_loaded, 16 * LOADS)
            pe.wait_ge(consts, 4)
            for h in range(SH):
                pe.matmul(LG[0][:, h * G_N:(h + 1) * G_N], wx[:, h, :], wsl[:, :], start=True, stop=True)
            pe.wait_ge(dve_step, 1)
            for h in range(SH):
                mm = pe.matmul(LG[1][:, h * G_N:(h + 1) * G_N], bx[:, h, :], wsl[:, :], start=True, stop=True)
            mm.then_inc(lg_psum, 1)

            def xn_transposes(i, u):
                pe.wait_ge(xn_ready, i + 1)
                wait(pe, st_ready, i - 1)
                transposes(pe, TP, xn[u][:, :, 0:D], ident)[-1].then_inc(xnT_psum, 1)

            def logits(i, u, t):
                if t == 0:
                    pe.wait_ge(xnT_ready, i + 1)
                if t >= 2:
                    pe.wait_ge(lg_read, T * i + t)
                else:
                    pe.wait_ge(lg_read, T * i + t) if not isinstance(i, int) or i > 0 else pe.wait_ge(lg_read, 1)
                pe.matmul(LG[t % 2][:, :], xnT[u][:, t * P:(t + 1) * P], Wc[:, :], start=True, stop=True).then_inc(lg_psum, 1)

            def use(i, u, t, first=False):
                n = T * i + t
                pe.wait_ge(sw_ready, n + 1)
                if t == 0:
                    wait(pe, xs_ready, i)
                    for b in range(2):
                        pe.matmul(XS[:, 2 * b:2 * b + 2, :], zeros[:, 0:P], zeros, start=True, stop=False)
                flat = SW[t % SW_BUFS][:, :, :].rearrange("p h g -> p (h g)")
                for k in range(KT):
                    pe.matmul(XS[:, k, 0:D + 1], flat[:, k * P:(k + 1) * P], xn[u][:, t, :], start=False,
                              stop=(t == T - 1 and k % 2 == 1))
                wait(pe, swT_ready, n - 1)
                for k in range(KT):
                    mm = pe.transpose(SP_T[t % 2][:, k, :], flat[:, k * P:(k + 1) * P], ident[:, :])
                mm.then_inc(sw_used, 1)

            def xs_transposes(i):
                pe.wait_ge(xs_ready, i + 1)
                if exists(i + 1):
                    pe.wait_ge(xnT_ready, i + 2)
                for k in range(KT):
                    pe.transpose(TP[:, k, :], xs[:, k, 0:D], ident[:, :])
                for k in range(KT):
                    mm = pe.transpose(TP[0:1, KT + k, :], xs[:, k, D:D + 1], ident[:, :])
                mm.then_inc(xsT_psum, 1)

            def slice_tokens(i):
                pe.wait_ge(xsT_ready, i + 1)
                for h in range(SH):
                    k, q = h // 2, h % 2
                    cols, heads = slice(q * G_N, (q + 1) * G_N), slice(h * SP_, (h + 1) * SP_)
                    out = TP[q * SP_:(q + 1) * SP_, k, 0:G_N]
                    pe.matmul(out, wfx[:, heads], xsT[:, k, cols], start=True, stop=False)
                    mm = pe.matmul(out, bfx[:, heads], snT[:, k, cols], start=False, stop=True)
                mm.then_inc(st_psum, 1)

            def body(i, u, first, last):
                for t in range(T):
                    logits(i, u, t)
                    if t >= LAG:
                        use(i, u, t - LAG)
                    elif not first:
                        use(i - 1, 1 - u, t - LAG + T)
                    if t == 3 and not first:
                        xs_transposes(i - 1)
                    if t == 4 and not first:
                        slice_tokens(i - 1)
                    if t == 5 and not last:
                        xn_transposes(i + 1, 1 - u)
                if last:
                    for t in range(T - LAG, T):
                        use(i, u, t)
                    xs_transposes(i)
                    slice_tokens(i)

            xn_transposes(0, 0)
            over_batches(pe, body)

        @block.scalar
        def _(act):
            def copy_xnT(i, u):
                act.wait_ge(xnT_psum, i + 1)
                act.activation(xnT[u][:, :], TP[:, :, :].rearrange("p t n -> p (t n)"), ACT.Copy).then_inc(xnT_ready, 1)

            def copy_swT(i, t):
                act.wait_ge(sw_used, T * i + t + 1)
                act.activation(SWT[:, i, t, :, :], SP_T[t % 2][:, :, :], ACT.Copy).then_inc(swT_ready, 1)

            def copy_xsT(i):
                act.wait_ge(xsT_psum, i + 1)
                act.activation(xsT[:, :, :], TP[:, 0:KT, :], ACT.Copy)
                act.activation(snT[:, :, :], TP[0:1, KT:2 * KT, :], ACT.Copy).then_inc(xsT_ready, 1)

            def copy_st(i):
                act.wait_ge(st_psum, i + 1)
                act.activation(ST[:, :, i, :], TP[:, 0:KT, 0:G_N], ACT.Copy).then_inc(st_ready, 1)

            def body(i, u, first, last):
                for t in range(T):
                    act.wait_ge(centred, T * i + t + 1)
                    act.activation(SW[t % SW_BUFS][:, :, :], SW[t % SW_BUFS][:, :, :], ACT.Exp).then_inc(exp_ready, 1)
                    if t >= LAG:
                        copy_swT(i, t - LAG)
                    elif not first:
                        copy_swT(i - 1, t - LAG + T)
                    if t == 3 and not first:
                        copy_xsT(i - 1)
                    if t == 4 and not first:
                        copy_st(i - 1)
                    if t == 5 and not last:
                        copy_xnT(i + 1, 1 - u)
                if last:
                    for t in range(T - LAG, T):
                        copy_swT(i, t)
                    copy_xsT(i)
                    copy_st(i)

            copy_xnT(0, 0)
            over_batches(act, body)

        @block.vector
        def _(dve):
            chain = Chain(dve, dve_step)
            dve.wait_ge(w_loaded, 16 * LOADS)
            chain.link(dve.tensor_copy(bx, bxc[:, :].unsqueeze(2).to_broadcast([SP_, SH, P])))
            chain.link(dve.tensor_scalar(temp[:, :], temp[:, :], 1e-6, None, ALU.max))
            dve.wait_ge(consts, 5)
            dve.wait_ge(lg_psum, 1)
            by_head = lambda a: a.rearrange("p (h g) -> p h g", h=SH)
            over_slices = temp[:, :].unsqueeze(2).to_broadcast([P, SH, G_N])
            dve.tensor_tensor(by_head(Wc[:, :]), by_head(LG[0][:, :]), over_slices, ALU.mult)
            chain.link(dve.tensor_tensor(by_head(bias[:, :]), by_head(LG[1][:, :]),
                                         bsl[:, :].unsqueeze(1).to_broadcast([P, SH, G_N]), ALU.add))
            chain.link(dve.tensor_tensor(by_head(bias[:, :]), by_head(bias[:, :]), over_slices, ALU.mult))
            dve.sem_inc(lg_read, 1)

            def norm_x(i, u):
                dve.wait_ge(x_loaded, 16 * i + 16)
                norm_in.stats(dve, X, i, u)

            def apply(i, u):
                norm_in.apply(dve, X, xn[u][:, :, 0:D], i, u).then_inc(xn_ready, 1)

            def centre(i, t):
                n, k = T * i + t, t % SW_BUFS
                dve.wait_ge(lg_psum, n + 2)
                wait(dve, sw_used, n + 1 - SW_BUFS)
                dve.tensor_tensor(SW[k][:, :, :], by_head(LG[t % 2][:, :]), by_head(bias[:, :]), ALU.add).then_inc(lg_read, 1)
                dve.wait_ge(lg_read, n + 2)
                chain.link(dve.tensor_reduce(top[:, :], SW[k][:, :, :], AX.X, ALU.max))
                dve.tensor_tensor(SW[k][:, :, :], SW[k][:, :, :], top[:, :].unsqueeze(2).to_broadcast([P, SH, G_N]),
                                  ALU.subtract).then_inc(centred, 1)

            def invert(i, t):
                n, k = T * i + t, t % SW_BUFS
                dve.wait_ge(exp_ready, n + 1)
                wait(dve, inv_ready, n)
                chain.link(dve.tensor_reduce(total[:, :], SW[k][:, :, :], AX.X, ALU.add))
                wait(dve, sw_ready, n - 1)
                dve.reciprocal(inv[t % 2][:, :], total[:, :]).then_inc(inv_ready, 1)

            def slice_sums(i):
                dve.wait_ge(sw_used, T * i + T)
                wait(dve, xsT_psum, i)
                chain.link(dve.tensor_scalar(sn[:, :], XS[:, :, D], 1e-5, None, ALU.add))
                chain.link(dve.reciprocal(sn[:, :], sn[:, :]))
                dve.tensor_tensor(xs[:, :, :], XS[:, :, 0:D + 1], sn[:, :].unsqueeze(2).to_broadcast([P, KT, D + 1]),
                                  ALU.mult).then_inc(xs_ready, 1)

            def body(i, u, first, last):
                chain.at(SETUP_STEPS if first else 2 * T * i + 2 * (i - 1) - 1 + SETUP_STEPS)
                for t in range(T):
                    centre(i, t)
                    if t > 0:
                        invert(i, t - 1)
                    elif not first:
                        invert(i - 1, T - 1)
                    if t == 2 and not first:
                        slice_sums(i - 1)
                    if t == 3 and not last:
                        norm_x(i + 1, 1 - u)
                    if t == 4 and not last:
                        apply(i + 1, 1 - u)
                if last:
                    invert(i, T - 1)
                    slice_sums(i)

            norm_x(0, 0)
            apply(0, 0)
            over_batches(dve, body)


ROWS_ALL = B * G_N
BP = B // 2
DTS = 2 * SH


def hydra_stage(nc, in_wT, conv_w, conv_b, dt_bias, A_log, Dp, fcD_wT, norm_w, hy_out_wT, out_wT, dA_rows, ident, ST, M):
    with ExitStack() as ctx:
        sb = lambda name, shape, dt=fp32: ctx.enter_context(nc.sbuf_tensor("h_" + name, shape, dt))
        sem = lambda name: ctx.enter_context(nc.semaphore("h_" + name))

        inw = sb("inw", [P, KT * IN_PROJ])
        in_w = inw[:, :].rearrange("p (k j) -> p k j", k=KT)
        outw = sb("outw", [P, KT, INNER])
        foldw = sb("foldw", [P, KT, D])
        cw, cb = sb("cw", [P, KT, CONV_K]), sb("cb", [P, KT])
        cwn, cbn = sb("cwn", [NS, 2, CONV_K]), sb("cbn", [NS, 2])
        fcD, Dc, nw = sb("fcD", [P, KT, SH]), sb("Dc", [P, KT]), sb("nw", [P, KT])
        dtb, A = sb("dtb", [DTS, 1]), sb("A", [DTS, 1])
        power, ones = sb("power", [P, B]), sb("ones", [P, P])
        diag = sb("diag", [P, G_N])
        XC = sb("XC", [P, KT, ROWS_ALL])
        Z = sb("Z", [P, KT, ROWS_ALL])
        BC = sb("BC", [NS, 2, ROWS_ALL])
        TH = [sb(f"TH{u}", [P, ROWS_ALL]) for u in range(2)]
        dts = TH[1][0:DTS, :]
        m2, rstd = sb("m2", [P, B]), sb("rstd", [P, B])
        tmp = [M[0:DTS, k * ROWS_ALL:(k + 1) * ROWS_ALL] for k in range(6)]
        dA = tmp[5]
        decay = M[:, :].rearrange("p (j b l) -> p j b l", j=DTS, b=BP)
        mix = M[:, 0:SH * BP * G_N].rearrange("p (h b l) -> p h b l", h=SH, b=BP)
        reach = inw[:, 0:DTS * BP * G_N].rearrange("p (j b l) -> p j b l", j=DTS, b=BP)
        OT = inw[:, 0:KT * ROWS_ALL].rearrange("p (k r) -> p k r", k=KT)
        xtok = ST[:, :, :, :].rearrange("p k b g -> p (k b g)").rearrange("p (b c) -> p b c", b=BP)
        YN = ST[:, :, :, :].rearrange("p k b g -> p k (b g)")
        st = YN

        K_ = [ctx.enter_context(nc.psum_tensor(f"h_K{k}", [P, ROWS_ALL], fp32)) for k in range(8)]

        loaded, dA_stored, decay_loaded = sem("loaded"), sem("dA_stored"), sem("decay_loaded")
        pe_done, act_done, dve_done, pool_done = sem("pe_done"), sem("act_done"), sem("dve_done"), sem("pool_done")
        dve_step = sem("dve_step")
        block = ctx.enter_context(nc.Block())

        (PE_X, PE_B, PE_C, PE_DT, PE_Z, PE_XTOK, PE_G, PE_DTTOK, PE_FCD, PE_Y, PE_SUM, PE_OUT, PE_M
         ) = (1, 5, 6, 7, 8, 12, 16, 17, 18, 22, 23, 24, 28)
        (ACT_A, ACT_TX, ACT_TB, ACT_TC, ACT_E, ACT_TZ, ACT_LN, ACT_DA, ACT_XTOK, ACT_YG, ACT_OUT, ACT_M
         ) = (1, 2, 6, 7, 8, 9, 13, 14, 15, 19, 27, 31)
        (DVE_CX, DVE_CB, DVE_CC, DVE_ABS, DVE_X, DVE_B, DVE_C, DVE_U, DVE_Z, DVE_DT, DVE_DELTA, DVE_MIX, DVE_YG,
         DVE_VAR) = (1, 5, 6, 7, 8, 12, 13, 14, 15, 19, 20, 21, 22, 26)
        LOADS = 17
        POOL_CONST, POOL_ENDS, POOL_RSTD = 2, 4, 5

        @block.sync
        def _(sp):
            def load(dst, src):
                sp.dma_start(dst, src).then_inc(loaded, 16)

            col = lambda a: a.rearrange("(n a) -> n a", a=1)
            for k in range(KT):
                load(in_w[:, k, :], in_wT[k * P:(k + 1) * P, :])
            load(cw[:, :, :], conv_w[0:INNER, :].rearrange("(k p) t -> p k t", p=P))
            load(cwn[:, :, :], conv_w[INNER:INNER + 2 * NS, :].rearrange("(k p) t -> p k t", p=NS))
            load(cb[:, :], conv_b[:, 0:KT])
            load(cbn[:, :], conv_b[0:NS, KT:KT + 2])
            for h in range(2):
                load(dtb[h * SH:(h + 1) * SH, :], col(dt_bias))
                load(A[h * SH:(h + 1) * SH, :], col(A_log))
            load(fcD[:, :, :], fcD_wT.rearrange("(k p) h -> p k h", p=P))
            load(nw[:, :], norm_w)
            load(Dc[:, :], Dp)
            load(outw[:, :, :], hy_out_wT.rearrange("(k p) j -> p k j", p=P))
            load(foldw[:, :, :], out_wT.rearrange("(k p) d -> p k d", p=P))
            sp.wait_ge(act_done, ACT_DA)
            sp.dma_start(dA_rows, dA).then_inc(dA_stored, 16)
            sp.wait_ge(dA_stored, 16)
            sp.wait_ge(dve_done, DVE_DT)
            by_pair = dA_rows.rearrange("j (b q l) -> q j b l", b=BP, q=2)
            for q in range(2):
                sp.dma_start(decay[q * G_N:(q + 1) * G_N, :, :, :],
                             by_pair[q:q + 1, :, :, :].to_broadcast([G_N, DTS, BP, G_N])).then_inc(decay_loaded, 16)

        @block.gpsimd
        def _(pool):
            pool.memset(power[:, :], -0.5).then_inc(pool_done, 1)
            pool.memset(ones[:, :], 1.0).then_inc(pool_done, 1)
            pool.wait_ge(decay_loaded, 32)
            pool.memset(decay[:, 0:SH, :, 0:1], 0.0).then_inc(pool_done, 1)
            pool.memset(decay[:, SH:DTS, :, G_N - 1:G_N], 0.0).then_inc(pool_done, 1)
            pool.wait_ge(dve_done, DVE_VAR)
            pool.tensor_tensor(rstd[:, :], m2[:, :], power[:, :], ALU.pow).then_inc(pool_done, 1)

        @block.tensor
        def _(pe):
            pe.wait_ge(loaded, 16 * LOADS)
            pe.wait_ge(pool_done, POOL_CONST)

            def project(out, j0, width):
                for k in range(KT):
                    mm = pe.matmul(out, in_w[:, k, j0:j0 + width], st[:, k, :], start=(k == 0), stop=(k == KT - 1))
                mm.then_inc(pe_done, 1)

            for k in range(KT):
                project(K_[k][:, :], INNER + k * P, P)
            project(K_[4][0:NS, :], 2 * INNER, NS)
            project(K_[5][0:NS, :], 2 * INNER + NS, NS)
            project(K_[6][0:DTS, :], 2 * INNER + 2 * NS, DTS)
            for k, bank in enumerate((7, 0, 1, 2)):
                if k > 0:
                    pe.wait_ge(dve_done, DVE_CX + k - 1)
                project(K_[bank][:, :], k * P, P)
            pe.wait_ge(dve_done, DVE_X + KT - 1)
            for b in range(BP):
                if b >= 2:
                    pe.wait_ge(act_done, ACT_XTOK + b - 2)
                for k in range(KT):
                    mm = pe.transpose(K_[5 + b % 2][:, k * P:(k + 1) * P], XC[:, k, b * P:(b + 1) * P], ident[:, :])
                mm.then_inc(pe_done, 1)
            pe.wait_ge(dve_done, DVE_C)
            for b in range(B):
                cols = slice(b * G_N, (b + 1) * G_N)
                q = b % 2 * G_N
                mm = pe.matmul(K_[4][q:q + G_N, b // 2 * G_N:(b // 2 + 1) * G_N], BC[:, 0, cols], BC[:, 1, cols],
                               start=True, stop=True)
            mm.then_inc(pe_done, 1)
            pe.wait_ge(dve_done, DVE_DT)
            for b in range(BP):
                mm = pe.transpose(K_[3][:, b * DTS:(b + 1) * DTS], dts[:, b * P:(b + 1) * P], ident[0:DTS, 0:DTS])
            mm.then_inc(pe_done, 1)
            for k, bank in enumerate((7, 0, 1, 2)):
                pe.wait_ge(dve_done, DVE_Z + k)
                for q in range(2):
                    for c in range(KT):
                        mm = pe.matmul(K_[bank][q * SP_:(q + 1) * SP_, :],
                                       fcD[:, c, 2 * k + q:2 * k + q + 1].to_broadcast([P, SP_]), XC[:, c, :],
                                       start=(c == 0), stop=(c == KT - 1))
                mm.then_inc(pe_done, 1)
            pe.wait_ge(dve_done, DVE_MIX)
            pe.wait_ge(act_done, ACT_XTOK + BP - 1)
            for k in range(KT):
                for q in range(2):
                    h = 2 * k + q
                    for b in range(B):
                        part = slice(b % 2 * G_N, (b % 2 + 1) * G_N)
                        at = (k % 2 * BP + b // 2) * G_N
                        mm = pe.matmul(K_[3 + k // 2 * 2 + b % 2][q * SP_:(q + 1) * SP_, at:at + G_N],
                                       xtok[part, b // 2, h * SP_:(h + 1) * SP_], mix[part, h, b // 2, :],
                                       start=True, stop=True)
            mm.then_inc(pe_done, 1)
            pe.wait_ge(act_done, ACT_YG + 2 * KT - 1)
            for k in range(KT):
                mm = pe.matmul(K_[7][:, :], ones[:, :], Z[:, k, :], start=(k == 0), stop=(k == KT - 1))
            mm.then_inc(pe_done, 1)
            for j in range(KT):
                for k in range(KT):
                    mm = pe.matmul(K_[j][:, :], outw[:, k, j * P:(j + 1) * P], YN[:, k, :], start=(k == 0), stop=(k == KT - 1))
                mm.then_inc(pe_done, 1)
            pe.wait_ge(act_done, ACT_OUT + KT - 1)
            pe.wait_ge(dve_done, DVE_VAR)
            for b in range(B):
                bank = (4 + b) % 8
                for k in range(KT):
                    for q in range(2):
                        part = slice(q * SP_, (q + 1) * SP_)
                        mm = pe.matmul(K_[bank][part, k * D:(k + 1) * D], OT[part, k, b * G_N:(b + 1) * G_N],
                                       foldw[part, k, :], start=True, stop=True)
                mm.then_inc(pe_done, 1)

        @block.scalar
        def _(act):
            act.wait_ge(loaded, 16 * LOADS)

            def tanh_half(out, src):
                act.activation(out, src, ACT.Tanh, scale=0.5).then_inc(act_done, 1)

            act.activation(A[:, :], A[:, :], ACT.Exp).then_inc(act_done, 1)
            for k in range(KT):
                act.wait_ge(dve_done, DVE_CX + k)
                if k >= 2:
                    act.wait_ge(dve_done, DVE_X + k - 2)
                act.activation(TH[k % 2][:, :], XC[:, k, :], ACT.Tanh).then_inc(act_done, 1)
            for k, ready in enumerate((DVE_CB, DVE_CC)):
                act.wait_ge(dve_done, ready)
                act.wait_ge(dve_done, DVE_X + 2 + k)
                act.activation(TH[k][0:NS, :], BC[:, k, :], ACT.Tanh).then_inc(act_done, 1)
            act.wait_ge(dve_done, DVE_ABS)
            act.activation(tmp[1], tmp[1], ACT.Exp, scale=-1.0).then_inc(act_done, 1)
            for k, bank in enumerate((7, 0, 1, 2)):
                act.wait_ge(pe_done, PE_Z + k)
                act.wait_ge(dve_done, (DVE_B, DVE_C, DVE_Z, DVE_Z + 1)[k])
                act.activation(TH[k % 2][:, :], K_[bank][:, :], ACT.Tanh, scale=0.5).then_inc(act_done, 1)
            act.wait_ge(dve_done, DVE_U)
            act.activation(tmp[3], tmp[2], ACT.Ln).then_inc(act_done, 1)
            act.wait_ge(dve_done, DVE_DT)
            act.activation(dA, dts, ACT.Exp, scale=A[:, :]).then_inc(act_done, 1)
            for b in range(BP):
                act.wait_ge(pe_done, PE_XTOK + b)
                act.activation(xtok[:, b, :], K_[5 + b % 2][:, :], ACT.Copy).then_inc(act_done, 1)
            for k in range(KT):
                act.wait_ge(dve_done, DVE_YG + k)
                act.activation(Z[:, k, :], XC[:, k, :], ACT.Square).then_inc(act_done, 1)
                act.activation(YN[:, k, :], XC[:, k, :], ACT.Copy, scale=nw[:, k:k + 1]).then_inc(act_done, 1)
            for j in range(KT):
                act.wait_ge(pe_done, PE_OUT + j)
                act.activation(OT[:, j, :], K_[j][:, :], ACT.Copy).then_inc(act_done, 1)
            act.wait_ge(pool_done, POOL_RSTD)
            for b in range(B):
                act.wait_ge(pe_done, PE_M + b)
                act.activation(M[:, b * KT * D:(b + 1) * KT * D], K_[(4 + b) % 8][:, :], ACT.Copy,
                               scale=rstd[:, b:b + 1]).then_inc(act_done, 1)
            act.wait_ge(act_done, ACT_M + B - 1)

        @block.vector
        def _(dve):
            chain = Chain(dve, dve_step)
            link = chain.link
            done = lambda ins: ins.then_inc(dve_done, 1)
            by_graph = lambda a: a.rearrange("p (b l) -> p b l", b=B)
            dve.wait_ge(loaded, 16 * LOADS)
            dve.tensor_tensor(diag[:, :], ident[:, 0:G_N], ident[:, G_N:P], ALU.add)
            for w in (cw[:, :, :], cb[:, :], cwn[:, :, :], cbn[:, :]):
                ins = dve.tensor_scalar(w, w, 0.5, None, ALU.mult)
            link(ins)

            def convolve(out, src, w, bias):
                link(dve.tensor_scalar(out, src, w[:, 2:3], bias, ALU.mult, ALU.add))
                o, x = by_graph(out), by_graph(src)
                link(dve.scalar_tensor_tensor(out=o[:, :, 1:], in0=x[:, :, :G_N - 1], scalar=w[:, 1:2], in1=o[:, :, 1:],
                                              op0=ALU.mult, op1=ALU.add))
                done(dve.scalar_tensor_tensor(out=o[:, :, 2:], in0=x[:, :, :G_N - 2], scalar=w[:, 0:1], in1=o[:, :, 2:],
                                              op0=ALU.mult, op1=ALU.add))

            for k in range(KT):
                dve.wait_ge(pe_done, PE_X + k)
                convolve(XC[:, k, :], K_[k][:, :], cw[:, k, :], cb[:, k:k + 1])
            for k in range(2):
                dve.wait_ge(pe_done, (PE_B, PE_C)[k])
                convolve(BC[:, k, :], K_[4 + k][0:NS, :], cwn[:, k, :], cbn[:, k:k + 1])
            dve.wait_ge(pe_done, PE_DT)
            link(dve.tensor_scalar(tmp[0], K_[6][0:DTS, :], dtb[:, :], None, ALU.add))
            link(dve.tensor_scalar(tmp[2], tmp[0], -1.0, None, ALU.mult))
            done(dve.tensor_tensor(tmp[1], tmp[0], tmp[2], ALU.max))

            def gate(out, x, th, count):
                dve.wait_ge(act_done, count)
                done(dve.scalar_tensor_tensor(out=out, in0=th, scalar=1.0, in1=x, op0=ALU.add, op1=ALU.mult))

            for k in range(KT):
                gate(XC[:, k, :], XC[:, k, :], TH[k % 2][:, :], ACT_TX + k)
            for k in range(2):
                gate(BC[:, k, :], BC[:, k, :], TH[k][0:NS, :], (ACT_TB, ACT_TC)[k])
            dve.wait_ge(act_done, ACT_E)
            dve.tensor_scalar(A[:, :], A[:, :], -1.0, None, ALU.mult)
            done(dve.tensor_scalar(tmp[2], tmp[1], 1.0, None, ALU.add))
            for k, bank in enumerate((7, 0, 1, 2)):
                gate(Z[:, k, :], K_[bank][:, :], TH[k % 2][:, :], ACT_TZ + k)
            dve.wait_ge(act_done, ACT_LN)
            link(dve.tensor_scalar(tmp[4], tmp[2], -1.0, 2.0 ** -23, ALU.add, ALU.max))
            link(dve.reciprocal(tmp[4], tmp[4]))
            link(dve.tensor_tensor(tmp[3], tmp[3], tmp[4], ALU.mult))
            link(dve.scalar_tensor_tensor(out=tmp[4], in0=tmp[2], scalar=1.0, in1=tmp[3], op0=ALU.is_equal, op1=ALU.add))
            link(dve.tensor_tensor(tmp[4], tmp[4], tmp[1], ALU.mult))
            done(dve.scalar_tensor_tensor(out=dts, in0=tmp[0], scalar=0.0, in1=tmp[4], op0=ALU.max, op1=ALU.add))
            dve.wait_ge(pe_done, PE_DTTOK)
            done(dve.tensor_tensor(reach, K_[3][:, 0:BP * DTS].rearrange("p (b j) -> p j b", j=DTS).unsqueeze(3).to_broadcast(
                [P, DTS, BP, G_N]), diag[:, :].unsqueeze(1).unsqueeze(1).to_broadcast([P, DTS, BP, G_N]), ALU.mult))
            dve.wait_ge(dve_done, DVE_DELTA)
            dve.wait_ge(pool_done, POOL_ENDS)
            half = SH * BP * G_N
            for lo, step in ((0, 1), (half, -1)):
                r, d = inw[:, lo:lo + half], M[:, lo:lo + half]
                ins = dve.tensor_tensor_scan(r[:, ::step], d[:, ::step], r[:, ::step], 0.0, ALU.mult, ALU.add)
            link(ins)
            dve.wait_ge(pe_done, PE_G)
            for j in range(DTS):
                ins = dve.tensor_tensor(reach[:, j, :, :], reach[:, j, :, :],
                                        K_[4][:, 0:BP * G_N].rearrange("p (b l) -> p b l", b=BP), ALU.mult)
            link(ins)
            fw, bw = reach[:, 0:SH, :, :], reach[:, SH:DTS, :, :]
            by_hb = lambda a, lo, hi: a.rearrange("p h b l -> p (h b) l")[:, :, lo:hi]
            dve.tensor_tensor(by_hb(mix, 1, G_N - 1), by_hb(fw, 0, G_N - 2), by_hb(bw, 2, G_N), ALU.add)
            dve.tensor_copy(by_hb(mix, 0, 1), by_hb(bw, 1, 2))
            done(dve.tensor_copy(by_hb(mix, G_N - 1, G_N), by_hb(fw, G_N - 2, G_N - 1)))
            dve.wait_ge(pe_done, PE_Y)
            for k, bank in enumerate((7, 0, 1, 2)):
                link(dve.scalar_tensor_tensor(out=XC[:, k, :], in0=K_[bank][:, :], scalar=Dc[:, k:k + 1], in1=XC[:, k, :],
                                              op0=ALU.add, op1=ALU.mult))
                for odd in range(2):
                    part = XC[:, k, :].rearrange("p (b q l) -> p b q l", b=BP, q=2)[:, :, odd, :]
                    y = K_[3 + k // 2 * 2 + odd][:, k % 2 * BP * G_N:(k % 2 + 1) * BP * G_N]
                    ins = dve.tensor_tensor(part, y.rearrange("p (b l) -> p b l", b=BP), part, ALU.add)
                link(ins)
                done(dve.scalar_tensor_tensor(out=XC[:, k, :], in0=XC[:, k, :], scalar=0.5, in1=Z[:, k, :],
                                              op0=ALU.mult, op1=ALU.mult))
            dve.wait_ge(pe_done, PE_SUM)
            sq = TH[0][:, :]
            link(dve.tensor_tensor(by_graph(sq), by_graph(K_[7][:, :]), diag[:, :].unsqueeze(1).to_broadcast([P, B, G_N]), ALU.mult))
            link(dve.tensor_reduce(m2[:, :], by_graph(sq), AX.X, ALU.add))
            done(dve.tensor_scalar(m2[:, :], m2[:, :], 1.0 / INNER, 1e-5, ALU.mult, ALU.add))


def deslicing_stage(nc, x_in, x_out, out_b, SWT, M):
    with ExitStack() as ctx:
        sb = lambda name, shape, dt=fp32: ctx.enter_context(nc.sbuf_tensor("o_" + name, shape, dt))
        sem = lambda name: ctx.enter_context(nc.semaphore("o_" + name))

        bias = sb("bias", [P, D])
        R = [sb(f"R{u}", [P, T, D]) for u in range(2)]
        OUT = [ctx.enter_context(nc.psum_tensor(f"o_OUT{u}", [P, T, D], fp32)) for u in range(2)]
        b_loaded, r_loaded = sem("b_loaded"), [sem(f"r_loaded{u}") for u in range(2)]
        out_psum, summed = sem("out_psum"), sem("summed")
        stored = sem("stored")
        block = ctx.enter_context(nc.Block())

        @block.sync
        def _(sp):
            sp.dma_start(bias[:, :], out_b.rearrange("(a n) -> a n", a=1).to_broadcast([P, D])).then_inc(b_loaded, 16)

            def load(i, u):
                sp.dma_start(R[u][:, :, :], tiled(x_in[i])).then_inc(r_loaded[u], 16)

            def body(i, u, first, last):
                sp.wait_ge(summed, 2 * i + 2)
                sp.dma_start(tiled(x_out[i]), R[u][:, :, :]).then_inc(stored, 16)
                if exists(i + 2):
                    sp.wait_ge(stored, 16 * i + 16)
                    load(i + 2, u)

            load(0, 0)
            load(1, 1)
            over_batches(sp, body)
            sp.wait_ge(stored, 16 * B)

        @block.tensor
        def _(pe):
            mixed = M[:, :].rearrange("p (b k d) -> p b k d", b=B, k=KT)
            for i in range(B):
                if i >= 2:
                    pe.wait_ge(summed, 2 * i - 2)
                for t in range(T):
                    for k in range(KT):
                        mm = pe.matmul(OUT[i % 2][:, t, :], SWT[:, i, t, k, :], mixed[:, i, k, :],
                                       start=(k == 0), stop=(k == KT - 1))
                mm.then_inc(out_psum, 1)

        @block.vector
        def _(dve):
            dve.wait_ge(b_loaded, 16)

            def body(i, u, first, last):
                dve.wait_ge(r_loaded[u], 8 * (i - u) + 16)
                dve.tensor_tensor(R[u][:, :, :], R[u][:, :, :], bias[:, :].unsqueeze(1).to_broadcast([P, T, D]),
                                  ALU.add).then_inc(summed, 1)
                dve.wait_ge(out_psum, i + 1)
                dve.wait_ge(summed, 2 * i + 1)
                dve.tensor_tensor(R[u][:, :, :], R[u][:, :, :], OUT[u][:, :, :], ALU.add).then_inc(summed, 1)

            over_batches(dve, body)


def graph_transformer(nc, x, adjT, g0_W_t, g0_b_t, g0_W_h, g0_theta, Wr, expert_blobs,
                      g1_W_lin, g1_b_lin, g1_W_q, g1_W_k, g1_ln_g, g1_ln_b,
                      W_x, b_xT, W_sliceT, b_slice, temperature, W_fxT, b_fx,
                      hy_in_wT, hy_conv_w, hy_conv_b, hy_dt_bias, hy_A_log, hy_D, hy_fcD_wT, hy_norm_w, hy_out_wT,
                      out_wT, out_b, out):
    stream = [nc.dram_tensor(f"stream{k}", [B, N, D], fp32).ap() for k in range(2)]
    rows = nc.dram_tensor("rows", [TOK + ROUTED * G, ROW], fp32).ap()
    sums = nc.dram_tensor("sums", [TOK + SPARE, D], fp32).ap()
    dA_rows = nc.dram_tensor("dA_rows", [DTS, ROWS_ALL], fp32).ap()
    with ExitStack() as ctx:
        ident = ctx.enter_context(nc.sbuf_tensor("ident", [P, P], fp32))
        setup_stage(nc, ident)
        gated_gnn_stage(nc, x, stream[0], adjT, g0_W_t, g0_b_t, g0_W_h, g0_theta, ident, rows, sums)
        with ExitStack() as routing:
            sb = lambda name, shape, dt: routing.enter_context(nc.sbuf_tensor(name, shape, dt))
            slots, w_top = sb("slots", [P, 2, TILES], u32), sb("w_top", [P, 2, TILES], fp32)
            expert_of = sb("expert_of", [P, ROUTED], i32)
            routing_stage(nc, stream[0], rows, Wr, ident, slots, w_top, expert_of)
            experts_stage(nc, stream[0], rows, sums, expert_blobs, ident, slots, w_top, expert_of)
        after_experts = sums[0:TOK, :].rearrange("(b n) d -> b n d", b=B)
        attention_gnn_stage(nc, after_experts, stream[1], adjT, g1_W_lin, g1_b_lin, g1_W_q, g1_W_k, g1_ln_g, g1_ln_b, ident)
        SWT = ctx.enter_context(nc.sbuf_tensor("SWT", [P, B, T, KT, P], fp32))
        M = ctx.enter_context(nc.sbuf_tensor("M", [P, B * KT * D], fp32))
        ST = ctx.enter_context(nc.sbuf_tensor("ST", [P, KT, B, G_N], fp32))
        slicing_stage(nc, stream[1], W_x, b_xT, W_sliceT, b_slice, temperature, W_fxT, b_fx, ident, SWT, ST, M)
        hydra_stage(nc, hy_in_wT, hy_conv_w, hy_conv_b, hy_dt_bias, hy_A_log, hy_D, hy_fcD_wT, hy_norm_w, hy_out_wT,
                    out_wT, dA_rows, ident, ST, M)
        deslicing_stage(nc, stream[1], out, out_b, SWT, M)


def laid_out(a):
    import numpy as np

    def expert_blob(W1, b1, W2, b2):
        E = len(W1)
        return np.concatenate([W1, b1.reshape(E, FT, P).transpose(0, 2, 1),
                               W2.reshape(E, FT, P, D).transpose(0, 2, 1, 3).reshape(E, P, FT * D),
                               b2.reshape(E, P, 1)], axis=2)

    f = lambda name: a["L0_ffn_" + name]
    h = lambda name: a["L1_ffn_hy_" + name]
    blobs = np.concatenate([expert_blob(f("W1p"), f("b1p"), f("W2p"), f("b2p")),
                            expert_blob(f("W1s")[None], f("b1s")[None], f("W2s")[None], f("b2s")[None])])
    by_tile = lambda v: v.reshape(KT, P).T
    conv_bn = h("conv_b")[INNER:].reshape(2, NS).T
    return [
        a["x"], a["adj"].transpose(0, 2, 1),
        a["L0_gnn_W_t"], a["L0_gnn_b_t"], a["L0_gnn_W_h"], a["L0_gnn_theta"],
        f("Wr"), blobs,
        a["L1_gnn_W_lin"], a["L1_gnn_b_lin"], a["L1_gnn_W_q"], a["L1_gnn_W_k"], a["L1_gnn_ln_g"], a["L1_gnn_ln_b"],
        a["L1_ffn_W_x"], a["L1_ffn_b_x"].reshape(SH, SP_).T, a["L1_ffn_W_slice"].T, a["L1_ffn_b_slice"],
        a["L1_ffn_temperature"], a["L1_ffn_W_fx"].T, a["L1_ffn_b_fx"],
        h("in_w").T, h("conv_w"),
        np.concatenate([by_tile(h("conv_b")[:INNER]), np.concatenate([conv_bn, conv_bn])], axis=1),
        h("dt_bias"), h("A_log"), by_tile(np.repeat(h("D"), SP_)), h("fcD_w").T, by_tile(h("norm_w")), h("out_w").T,
        a["L1_ffn_out_w"].T, a["L1_ffn_out_b"],
    ]


def kernel(**inputs):
    import numpy as _np
    import concourse.bacc as _bacc
    from concourse import mybir as _mybir
    from concourse.bass_utils import run_bass_kernel_spmd as _run

    nc = _bacc.Bacc("TRN2", target_bir_lowering=False, num_devices=1)
    arrays, args = {}, []
    for i, a in enumerate(laid_out({name: _np.asarray(v) for name, v in inputs.items()})):
        a = _np.ascontiguousarray(a)
        arrays[f"in_{i}_dram"] = a
        args.append(nc.dram_tensor(f"in_{i}_dram", a.shape, _mybir.dt.from_np(a.dtype), kind="ExternalInput").ap())
    out = nc.dram_tensor("out_0_dram", (B, N, D), _mybir.dt.float32, kind="ExternalOutput").ap()
    graph_transformer(nc, *args, out)
    r = _run(nc, [arrays], core_ids=[0])
    return r.results[0]["out_0_dram"]
```

```python
import concourse.bass as bass
from concourse import mybir
from contextlib import ExitStack

fp32 = mybir.dt.float32
fp32r = mybir.dt.float32r
ALU = mybir.AluOpType
ACT = mybir.ActivationFunctionType
AX = mybir.AxisListType

P = 128
B, N, D = 8, 1024, 128
T = N // P
HALF = 512
NH = N // HALF
LN_EPS = 1e-5


E_N, F_N = 8, 512
FT = F_N // P
G = 512
RT = G // P
TOK = B * N
TILES = TOK // P
SHARED = TOK // G
ROUTED = 2 * TOK // G + E_N - 1
GROUPS = SHARED + ROUTED
BLOB = F_N + FT + FT * D + 1
ROW = D + 2
SPARE = ROUTED * G // B
FP = 96
FILL = SPARE // FP
i32, u32 = mybir.dt.int32, mybir.dt.uint32


class Chain:

    def __init__(self, eng, sem):
        self.eng, self.sem, self.base, self.n = eng, sem, 0, 0

    def at(self, base):
        self.base, self.n = base, 0

    def step(self, ins):
        ins.then_inc(self.sem, 1)
        self.n += 1

    def wait(self):
        self.eng.wait_ge(self.sem, self.base + self.n)

    def link(self, ins):
        self.step(ins)
        self.wait()


def over_batches(eng, body):
    body(0, 0, True, False)
    body(1, 1, False, False)
    with eng.Fori(1, B // 2 - 1) as j:
        body(2 * j, 0, False, False)
        body(2 * j + 1, 1, False, False)
    body(B - 2, 0, False, False)
    body(B - 1, 1, False, True)


def exists(i):
    return not isinstance(i, int) or i < B


def wait(eng, sem, value):
    if not isinstance(value, int) or value > 0:
        eng.wait_ge(sem, value)


def tiled(x):
    return x.rearrange("(t p) d -> p t d", p=P)


def transposes(pe, out, src, ident):
    last = []
    for t in range(T):
        mm = pe.transpose(out[:, t, :], src[:, t, :], ident[:, :])
        if t % 4 == 3:
            last.append(mm)
    return last


class LayerNorm:

    def __init__(self, sb, sem):
        self.st = sb("st", [P, T, 6])
        self.sums = sb("sums", [P, T, 2])
        self.dm, self.dm2, self.var = sb("dm", [P, T]), sb("dm2", [P, T]), sb("var", [P, T])
        self.mean = [sb(f"mean{u}", [P, T]) for u in range(2)]
        self.ve = [sb(f"ve{u}", [P, T]) for u in range(2)]
        self.rstd = [sb(f"rstd{u}", [P, T]) for u in range(2)]
        self.var_ready, self.rstd_ready = sem("var_ready"), sem("rstd_ready")
        self.step = sem("norm_step")

    def stats(self, dve, x, i, u):
        chain = Chain(dve, self.step)
        chain.at(3 * i)
        st, sums = self.st, self.sums
        for t in range(T):
            ins = dve.bn_stats(st[:, t, :], x[:, t, :])
        chain.link(ins)
        dve.tensor_tensor(sums[:, :, :], st[:, :, 1:3], st[:, :, 4:6], ALU.add)
        chain.link(dve.tensor_tensor(self.dm[:, :], st[:, :, 1], st[:, :, 4], ALU.subtract))
        dve.tensor_scalar(self.mean[u][:, :], sums[:, :, 0], 0.5, None, ALU.mult)
        dve.scalar_tensor_tensor(out=self.dm2[:, :], in0=self.dm[:, :], scalar=0.25, in1=self.dm[:, :],
                                 op0=ALU.mult, op1=ALU.mult)
        chain.link(dve.tensor_scalar(self.var[:, :], sums[:, :, 1], 1.0 / D, LN_EPS, ALU.mult, ALU.add))
        dve.tensor_tensor(self.ve[u][:, :], self.var[:, :], self.dm2[:, :], ALU.add).then_inc(self.var_ready, 1)

    def power(self, pool, power, i, u):
        pool.wait_ge(self.var_ready, i + 1)
        pool.tensor_tensor(self.rstd[u][:, :], self.ve[u][:, :], power[:, 0:T], ALU.pow).then_inc(self.rstd_ready, 1)

    def apply(self, dve, x, xn, i, u):
        dve.wait_ge(self.rstd_ready, i + 1)
        for t in range(T):
            ins = dve.tensor_scalar(xn[:, t, :], x[:, t, :], self.mean[u][:, t:t + 1], self.rstd[u][:, t:t + 1],
                                    ALU.subtract, ALU.mult)
        return ins


def setup_stage(nc, ident):
    with ExitStack() as ctx:
        zeroed = ctx.enter_context(nc.semaphore("ident_zeroed"))
        block = ctx.enter_context(nc.Block())

        @block.gpsimd
        def _(pool):
            pool.memset(ident[:, :], 0.0).then_inc(zeroed, 1)
            pool.wait_ge(zeroed, 1)
            pool.affine_select(out=ident[:, :], in_=ident[:, :], compare_op=ALU.not_equal, fill=1.0,
                               base=0, pattern=[[-1, P]], channel_multiplier=1).then_inc(zeroed, 1)
            pool.wait_ge(zeroed, 2)


def gated_gnn_stage(nc, x_in, x_out, adjT, W_t, b_t, W_h, theta, ident, rows, sums):
    with ExitStack() as ctx:
        sb = lambda name, shape, dt=fp32: ctx.enter_context(nc.sbuf_tensor("a_" + name, shape, dt))
        ps = lambda name, shape: ctx.enter_context(nc.psum_tensor("a_" + name, shape, fp32))
        sem = lambda name: ctx.enter_context(nc.semaphore("a_" + name))

        W = sb("W", [P, 3, D])
        bias = sb("bias", [P, D])
        ones = sb("ones", [P, 32])
        power = sb("power", [P, T])
        fill = sb("fill", [FP, FILL, ROW])
        spare_i = sb("spare_i", [FP, FILL], i32)
        X = [sb(f"X{u}", [P, T, D]) for u in range(2)]
        R = [sb(f"R{u}", [P, T, D]) for u in range(2)]
        A = [sb(f"A{u}", [P, T, N]) for u in range(2)]
        xn = sb("xn", [P, T, D])
        xnT = sb("xnT", [P, N])
        dpart = sb("dpart", [P, N])
        dsum = sb("dsum", [P, T])
        deg = sb("deg", [P, T])
        norm = [sb(f"norm{u}", [P, T]) for u in range(2)]
        F = sb("F", [P, T, D])
        Hh = [sb(f"H{u}", [P, T, D]) for u in range(2)]
        Z = [sb(f"Z{u}", [P, T, D]) for u in range(2)]
        aggT = sb("aggT", [P, N])
        dif = sb("dif", [P, T, D])
        O = sb("O", [P, T, D])
        E = sb("E", [P, T, D])

        TP = ps("TP", [P, T, P])
        DG = ps("DG", [P, N])
        FG = ps("FG", [P, 2, HALF])
        AG = ps("AG", [P, N])

        w_loaded, consts, filled = sem("w_loaded"), sem("consts"), sem("filled")
        x_loaded = [sem(f"x_loaded{u}") for u in range(2)]
        r_loaded = [sem(f"r_loaded{u}") for u in range(2)]
        adj_loaded = [sem(f"adj_loaded{u}") for u in range(2)]
        xn_ready = sem("xn_ready")
        norm_in = LayerNorm(sb, sem)
        xnT_psum, xnT_ready = sem("xnT_psum"), sem("xnT_ready")
        dpart_psum, dpart_ready, degT_psum = sem("dpart_psum"), sem("dpart_ready"), sem("degT_psum")
        deg_ready, norm_ready = sem("deg_ready"), sem("norm_ready")
        fgh_psum, H_ready, FZ_ready = sem("fgh_psum"), sem("H_ready"), sem("FZ_ready")
        th_ready = sem("th_ready")
        agg_psum, agg_ready, out_psum = sem("agg_psum"), sem("agg_ready"), sem("out_psum")
        dif_ready, O_min, E_ready = sem("dif_ready"), sem("O_min"), sem("E_ready")
        out_ready, stored = sem("out_ready"), sem("stored")
        dve_step = sem("dve_step")
        block = ctx.enter_context(nc.Block())

        def fgh(t, part):
            bank = FG[:, t % 2, :] if t % 4 < 2 else DG[:, t % 2 * HALF:(t % 2 + 1) * HALF]
            return bank[:, part.start * D:part.stop * D]

        def one(k):
            return slice(k, k + 1)

        @block.sync
        def _(sp):
            sp.dma_start(W[:, 0, :], theta).then_inc(w_loaded, 16)
            sp.dma_start(W[:, 1, :], W_h).then_inc(w_loaded, 16)
            sp.dma_start(W[:, 2, :], W_t).then_inc(w_loaded, 16)
            sp.dma_start(bias[:, :], b_t.rearrange("(a n) -> a n", a=1).to_broadcast([P, D])).then_inc(w_loaded, 16)

            def load_x(i, u):
                wait(sp, xn_ready, i - 1)
                sp.dma_start(X[u][:, :, :], tiled(x_in[i])).then_inc(x_loaded[u], 16)

            def load_adj(i, u):
                wait(sp, agg_psum, NH * (i - 1))
                for q in range(4):
                    sp.dma_start(A[u][:, 2 * q:2 * q + 2, :], adjT[i, bass.ts(q, 2 * P), :].rearrange(
                        "(t p) n -> p t n", p=P)).then_inc(adj_loaded[u], 16)

            def body(i, u, first, last):
                if exists(i + 2):
                    load_x(i + 2, u)
                if exists(i + 1):
                    load_adj(i + 1, 1 - u)
                wait(sp, stored, 16 * i - 16)
                sp.dma_start(R[u][:, :, :], tiled(x_in[i])).then_inc(r_loaded[u], 16)
                if not first:
                    store(i - 1, 1 - u)
                if last:
                    store(i, u)
                sp.dma_start(rows[bass.ds(i * SPARE + TOK, SPARE), :].rearrange("(p r) d -> p r d", p=FP),
                             fill[:, :, :]).then_inc(filled, 16)

            def store(i, u):
                sp.wait_ge(out_ready, i + 1)
                sp.dma_start(tiled(x_out[i]), R[u][:, :, :]).then_inc(stored, 16)

            load_x(0, 0)
            load_x(1, 1)
            load_adj(0, 0)
            sp.wait_ge(consts, 5)
            sp.dma_start(sums[TOK:TOK + SPARE, :].rearrange("(p r) d -> p r d", p=FP), fill[:, :, 0:D]).then_inc(filled, 16)
            over_batches(sp, body)
            sp.wait_ge(stored, 16 * B)
            sp.wait_ge(filled, 16 * (B + 1))

        @block.gpsimd
        def _(pool):
            pool.memset(ones[:, :], 1.0).then_inc(consts, 1)
            pool.memset(power[:, :], -0.5).then_inc(consts, 1)
            pool.memset(fill[:, :, :], 0.0).then_inc(consts, 1)
            pool.iota(spare_i[:, :], pattern=[[1, FILL]], base=TOK, channel_multiplier=FILL).then_inc(consts, 1)
            pool.wait_ge(consts, 4)
            pool.tensor_copy(fill[:, :, D + 1], spare_i[:, :]).then_inc(consts, 1)

            def body(i, u, first, last):
                pool.wait_ge(deg_ready, i + 1)
                pool.tensor_tensor(norm[u][:, :], deg[:, :], power[:, :], ALU.pow).then_inc(norm_ready, 1)
                if exists(i + 2):
                    norm_in.power(pool, power, i + 2, u)

            norm_in.power(pool, power, 0, 0)
            norm_in.power(pool, power, 1, 1)
            over_batches(pool, body)

        @block.tensor
        def _(pe):
            pe.wait_ge(w_loaded, 64)
            pe.wait_ge(consts, 2)

            def out_transposes(i, u):
                pe.wait_ge(agg_ready, NH * i + NH)
                pe_last = transposes(pe, TP, aggT[:, :].rearrange("p (t n) -> p t n", t=T), ident)[-1]
                pe_last.then_inc(out_psum, 1)

            def body(i, u, first, last):
                pe.wait_ge(xn_ready, i + 1)
                wait(pe, dif_ready, i - 1)
                for mm in transposes(pe, TP, xn, ident):
                    mm.then_inc(xnT_psum, 1)
                pe.wait_ge(adj_loaded[u], 32 * (i - u) + 64)
                if not first:
                    pe.wait_ge(H_ready, T * i)
                for h in range(NH):
                    for t in range(T):
                        g = 32 * (t % 4)
                        mm = pe.matmul(DG[g:g + 32, h * HALF:(h + 1) * HALF], ones[:, :],
                                       A[u][:, t, h * HALF:(h + 1) * HALF], start=(t < 4), stop=(t >= 4))
                    mm.then_inc(dpart_psum, 1)
                pe.wait_ge(xnT_ready, NH * i + NH)
                pe.wait_ge(dpart_ready, NH * i + NH)
                transposes(pe, TP, dpart[:, :].rearrange("p (t n) -> p t n", t=T), ident)[-1].then_inc(degT_psum, 1)
                for t in range(T):
                    if t == 2 and not first:
                        pe.wait_ge(deg_ready, i + 1)
                        out_transposes(i - 1, 1 - u)
                    if t >= 4:
                        pe.wait_ge(H_ready, T * i + t - 3)
                    pe.matmul(fgh(t, slice(0, 3)), xnT[:, t * P:(t + 1) * P],
                              W[:, :, :].rearrange("p a n -> p (a n)"), start=True, stop=True).then_inc(fgh_psum, 1)
                pe.wait_ge(FZ_ready, T * i + T)
                for h in range(NH):
                    if not first:
                        pe.wait_ge(agg_ready, NH * (i - 1) + h + 1)
                    for t in range(T):
                        mm = pe.matmul(AG[:, h * HALF:(h + 1) * HALF], F[:, t, :],
                                       A[u][:, t, h * HALF:(h + 1) * HALF], start=(t == 0), stop=(t == T - 1))
                    mm.then_inc(agg_psum, 1)
                if last:
                    pe.wait_ge(dif_ready, i)
                    out_transposes(i, u)

            over_batches(pe, body)

        @block.scalar
        def _(act):
            def elu_exp(i):
                act.wait_ge(O_min, i + 1)
                act.activation(E[:, :, :], E[:, :, :], ACT.Exp).then_inc(E_ready, 1)

            def body(i, u, first, last):
                for h in range(NH):
                    act.wait_ge(xnT_psum, NH * i + h + 1)
                    act.activation(xnT[:, h * HALF:(h + 1) * HALF],
                                   TP[:, 4 * h:4 * h + 4, :].rearrange("p t n -> p (t n)"), ACT.Copy).then_inc(xnT_ready, 1)
                for h in range(NH):
                    act.wait_ge(dpart_psum, NH * i + h + 1)
                    act.activation(dpart[:, h * HALF:(h + 1) * HALF], DG[:, h * HALF:(h + 1) * HALF],
                                   ACT.Copy).then_inc(dpart_ready, 1)
                for t in range(T):
                    act.wait_ge(FZ_ready, T * i + t + 1)
                    act.activation(Hh[u][:, t, :], fgh(t, one(1)), ACT.Copy).then_inc(H_ready, 1)
                act.activation(Z[u][:, :, :], Z[u][:, :, :], ACT.Tanh, scale=0.5).then_inc(th_ready, 1)
                if not first:
                    elu_exp(i - 1)
                for h in range(NH):
                    act.wait_ge(agg_psum, NH * i + h + 1)
                    if not first:
                        act.wait_ge(out_psum, i)
                    act.activation(aggT[:, h * HALF:(h + 1) * HALF], AG[:, h * HALF:(h + 1) * HALF],
                                   ACT.Copy).then_inc(agg_ready, 1)
                if last:
                    elu_exp(i)

            over_batches(act, body)

        @block.vector
        def _(dve):
            chain = Chain(dve, dve_step)
            dve.wait_ge(w_loaded, 64)
            dve.wait_ge(consts, 2)

            def stats(i, u):
                dve.wait_ge(x_loaded[u], 8 * (i - u) + 16)
                norm_in.stats(dve, X[u], i, u)

            def norm_x(i, u):
                norm_in.apply(dve, X[u], xn, i, u).then_inc(xn_ready, 1)

            def finish(i, u):
                dve.wait_ge(out_psum, i + 1)
                dve.wait_ge(H_ready, T * i + T)
                for t in range(T):
                    ins = dve.scalar_tensor_tensor(out=dif[:, t, :], in0=TP[:, t, :], scalar=norm[u][:, t:t + 1],
                                                   in1=Hh[u][:, t, :], op0=ALU.mult, op1=ALU.subtract)
                ins.then_inc(dif_ready, 1)
                dve.wait_ge(dif_ready, i + 1)
                dve.wait_ge(th_ready, i + 1)
                dve.wait_ge(r_loaded[u], 8 * (i - u) + 16)
                chain.link(dve.scalar_tensor_tensor(out=dif[:, :, :], in0=Z[u][:, :, :], scalar=1.0,
                                                    in1=dif[:, :, :], op0=ALU.add, op1=ALU.mult))
                chain.link(dve.scalar_tensor_tensor(out=O[:, :, :], in0=dif[:, :, :], scalar=0.5,
                                                    in1=Hh[u][:, :, :], op0=ALU.mult, op1=ALU.add))
                dve.tensor_scalar(E[:, :, :], O[:, :, :], 0.0, None, ALU.min).then_inc(O_min, 1)
                chain.link(dve.scalar_tensor_tensor(out=R[u][:, :, :], in0=O[:, :, :], scalar=0.0,
                                                    in1=R[u][:, :, :], op0=ALU.max, op1=ALU.add))
                dve.wait_ge(E_ready, i + 1)
                dve.scalar_tensor_tensor(out=R[u][:, :, :], in0=E[:, :, :], scalar=-1.0,
                                         in1=R[u][:, :, :], op0=ALU.add, op1=ALU.add).then_inc(out_ready, 1)

            def body(i, u, first, last):
                chain.at(0 if first else 4 * i - 3)
                if exists(i + 1):
                    dve.wait_ge(xnT_psum, NH * i + NH)
                    norm_x(i + 1, 1 - u)
                if exists(i + 2):
                    stats(i + 2, u)
                dve.wait_ge(degT_psum, i + 1)
                chain.link(dve.tensor_reduce(dsum[:, :], TP[:, :, :].rearrange("p t (g c) -> p t c g", c=32)[:, :, 0, :],
                                             AX.X, ALU.add))
                dve.tensor_scalar(deg[:, :], dsum[:, :], 1e-6, None, ALU.add).then_inc(deg_ready, 1)
                dve.wait_ge(norm_ready, i + 1)
                for t in range(T):
                    dve.wait_ge(fgh_psum, T * i + t + 1)
                    dve.tensor_scalar(F[:, t, :], fgh(t, one(0)), norm[u][:, t:t + 1], None, ALU.mult)
                    dve.tensor_tensor(Z[u][:, t, :], fgh(t, one(2)), bias[:, :], ALU.add).then_inc(FZ_ready, 1)
                if not first:
                    finish(i - 1, 1 - u)
                if last:
                    finish(i, u)

            stats(0, 0)
            stats(1, 1)
            norm_x(0, 0)
            over_batches(dve, body)


def over_groups(eng, body):
    assert SHARED % 2 == 0 and GROUPS % 2 == 1
    body(0, 0, False, True, False)
    body(1, 1, False, False, False)
    for routed, (lo, hi) in enumerate(((1, SHARED // 2), (SHARED // 2, GROUPS // 2))):
        with eng.Fori(lo, hi) as j:
            body(2 * j, 0, bool(routed), False, False)
            body(2 * j + 1, 1, bool(routed), False, False)
    body(GROUPS - 1, 0, True, False, True)


def weights_count(g, u, routed):
    return 8 * (g - u) + (32 - 8 * SHARED) if routed else 16


def routing_stage(nc, x_in, rows, Wr, ident, slots, w_top, expert_of):
    with ExitStack() as ctx:
        sb = lambda name, shape, dt=fp32: ctx.enter_context(nc.sbuf_tensor("r_" + name, shape, dt))
        ps = lambda name, shape: ctx.enter_context(nc.psum_tensor("r_" + name, shape, fp32))
        sem = lambda name: ctx.enter_context(nc.semaphore("r_" + name))
        K = TOK // G

        W = sb("W", [P, E_N])
        power = sb("power", [P, T])
        ones = sb("ones", [P, P])
        before = sb("before", [P, P])
        order_i, order = sb("order_i", [P, TILES, E_N], i32), sb("order", [P, TILES, E_N])
        steps_i, steps = sb("steps_i", [P, E_N, K], i32), sb("steps", [P, E_N, K])
        group_i, group = sb("group_i", [P, ROUTED, E_N], i32), sb("group", [P, ROUTED, E_N])
        keep = sb("keep", [P, E_N, TILES])
        X = [sb(f"X{u}", [P, T, D]) for u in range(2)]
        xn = [sb(f"xn{u}", [P, T, D]) for u in range(2)]
        xnT = sb("xnT", [P, N])
        Lg = sb("Lg", [P, TILES, E_N])
        eq, sc = sb("eq", [P, TILES, E_N]), sb("sc", [P, TILES, E_N])
        hot = [sb(f"hot{k}", [P, TILES, E_N]) for k in range(2)]
        top = [sb(f"top{k}", [P, TILES]) for k in range(2)]
        best = sb("best", [P, TILES])
        gap, th = sb("gap", [P, TILES]), sb("th", [P, TILES])
        both, total = sb("both", [P, E_N, TILES]), sb("total", [P, E_N, TILES])
        upto, pos = sb("upto", [P, E_N, TILES]), sb("pos", [P, E_N, TILES])
        hit = sb("hit", [P, E_N, K])
        n_groups, group_end, start = sb("n_groups", [P, E_N]), sb("group_end", [P, E_N]), sb("start", [P, E_N])
        first_row = sb("first_row", [P, E_N])
        past = sb("past", [P, ROUTED, E_N])
        expert_f = sb("expert_f", [P, ROUTED])
        slot_f = sb("slot_f", [P, 2, TILES])

        TP = ps("TP", [P, T, P])
        LG = [ps(f"LG{u}", [P, T, E_N]) for u in range(2)]
        RK = ps("RK", [P, E_N, TILES])
        TT = ps("TT", [P, E_N, TILES])

        w_loaded, consts = sem("w_loaded"), sem("consts")
        x_loaded = [sem(f"x_loaded{u}") for u in range(2)]
        norm_in = LayerNorm(sb, sem)
        xn_ready = sem("xn_ready")
        rows_stored = [sem(f"rows_stored{u}") for u in range(2)]
        xnT_psum, xnT_ready = sem("xnT_psum"), sem("xnT_ready")
        logits_psum, logits_read = sem("logits_psum"), sem("logits_read")
        gap_ready, th_ready = sem("gap_ready"), sem("th_ready")
        both_ready, rank_psum, dve_step = sem("both_ready"), sem("rank_psum"), sem("dve_step")
        block = ctx.enter_context(nc.Block())
        N_CONST = 8

        @block.sync
        def _(sp):
            def load(i, u):
                wait(sp, xn_ready, i - 1)
                sp.dma_start(X[u][:, :, :], tiled(x_in[i])).then_inc(x_loaded[u], 16)

            def body(i, u, first, last):
                if exists(i + 2):
                    load(i + 2, u)
                sp.wait_ge(xn_ready, i + 1)
                sp.dma_start(tiled(rows[bass.ts(i, N), 0:D]), xn[u][:, :, :]).then_inc(rows_stored[u], 16)

            sp.dma_start(W[:, :], Wr).then_inc(w_loaded, 16)
            load(0, 0)
            load(1, 1)
            over_batches(sp, body)
            for u in range(2):
                sp.wait_ge(rows_stored[u], 16 * B // 2)

        @block.gpsimd
        def _(pool):
            pool.memset(power[:, :], -0.5).then_inc(consts, 1)
            pool.memset(ones[:, :], 1.0).then_inc(consts, 1)
            pool.memset(keep[:, :, :], 1.0).then_inc(consts, 1)
            pool.iota(order_i[:, :, :], pattern=[[0, TILES], [-1, E_N]], base=E_N, channel_multiplier=0).then_inc(consts, 1)
            pool.iota(steps_i[:, :, :], pattern=[[0, E_N], [G, K]], base=0, channel_multiplier=0).then_inc(consts, 1)
            pool.iota(group_i[:, :, :], pattern=[[1, ROUTED], [0, E_N]], base=0, channel_multiplier=0).then_inc(consts, 1)
            pool.wait_ge(consts, 6)
            pool.affine_select(out=before[:, :], in_=ones[:, :], compare_op=ALU.is_gt, fill=0.0, base=0,
                               pattern=[[1, P]], channel_multiplier=-1).then_inc(consts, 1)
            pool.memset(keep[:, :, 0:1], 0.0).then_inc(consts, 1)
            norm_in.power(pool, power, 0, 0)
            norm_in.power(pool, power, 1, 1)

            def body(i, u, first, last):
                if exists(i + 2):
                    norm_in.power(pool, power, i + 2, u)

            over_batches(pool, body)

        @block.tensor
        def _(pe):
            pe.wait_ge(w_loaded, 16)

            def body(i, u, first, last):
                pe.wait_ge(xn_ready, i + 1)
                wait(pe, xnT_ready, NH * i)
                for mm in transposes(pe, TP, xn[u], ident):
                    mm.then_inc(xnT_psum, 1)
                pe.wait_ge(xnT_ready, NH * i + NH)
                wait(pe, logits_read, i - 1)
                for t in range(T):
                    mm = pe.matmul(LG[u][:, t, :], xnT[:, t * P:(t + 1) * P], W[:, :], start=True, stop=True)
                mm.then_inc(logits_psum, 1)

            over_batches(pe, body)
            pe.wait_ge(both_ready, 1)
            pe.wait_ge(consts, N_CONST)
            pe.matmul(RK[:, :, :], before[:, :], both[:, :, :], start=True, stop=True).then_inc(rank_psum, 1)
            pe.matmul(TT[:, :, :], ones[:, :], both[:, :, :], start=True, stop=True).then_inc(rank_psum, 1)

        @block.scalar
        def _(act):
            def body(i, u, first, last):
                for h in range(NH):
                    act.wait_ge(xnT_psum, NH * i + h + 1)
                    wait(act, logits_psum, i)
                    act.activation(xnT[:, h * HALF:(h + 1) * HALF],
                                   TP[:, 4 * h:4 * h + 4, :].rearrange("p t n -> p (t n)"), ACT.Copy).then_inc(xnT_ready, 1)

            over_batches(act, body)
            act.wait_ge(gap_ready, 1)
            act.activation(th[:, :], gap[:, :], ACT.Tanh, scale=0.5).then_inc(th_ready, 1)

        @block.vector
        def _(dve):
            chain = Chain(dve, dve_step)
            by_tile = lambda a: a.rearrange("p t e -> p e t")
            flat = lambda a: a.rearrange("p e t -> p (e t)")
            wide = lambda a: a.unsqueeze(2).to_broadcast([P, TILES, E_N])

            def stats(i, u):
                dve.wait_ge(x_loaded[u], 8 * (i - u) + 16)
                norm_in.stats(dve, X[u], i, u)

            def norm_x(i, u):
                wait(dve, rows_stored[u], 8 * (i - u))
                norm_in.apply(dve, X[u], xn[u], i, u).then_inc(xn_ready, 1)

            def body(i, u, first, last):
                if exists(i + 1):
                    norm_x(i + 1, 1 - u)
                if exists(i + 2):
                    stats(i + 2, u)
                dve.wait_ge(logits_psum, i + 1)
                dve.tensor_copy(Lg[:, bass.ts(i, T), :], LG[u][:, :, :]).then_inc(logits_read, 1)

            stats(0, 0)
            stats(1, 1)
            norm_x(0, 0)
            over_batches(dve, body)
            dve.wait_ge(consts, N_CONST)
            dve.tensor_copy(steps[:, :, :], steps_i[:, :, :])
            dve.tensor_copy(group[:, :, :], group_i[:, :, :])
            chain.link(dve.tensor_copy(order[:, :, :], order_i[:, :, :]))
            dve.wait_ge(logits_read, B)
            for k in range(2):
                chain.link(dve.tensor_reduce(top[k][:, :], Lg[:, :, :], AX.X, ALU.max))
                chain.link(dve.tensor_tensor(eq[:, :, :], Lg[:, :, :], wide(top[k][:, :]), ALU.is_equal))
                chain.link(dve.tensor_tensor(sc[:, :, :], eq[:, :, :], order[:, :, :], ALU.mult))
                chain.link(dve.tensor_reduce(best[:, :], sc[:, :, :], AX.X, ALU.max))
                chain.link(dve.tensor_tensor(hot[k][:, :, :], sc[:, :, :], wide(best[:, :]), ALU.is_equal))
                if k == 0:
                    chain.link(dve.scalar_tensor_tensor(out=Lg[:, :, :], in0=hot[0][:, :, :], scalar=-3e38,
                                                        in1=Lg[:, :, :], op0=ALU.mult, op1=ALU.add))
            dve.tensor_tensor(both[:, :, :], by_tile(hot[0][:, :, :]), by_tile(hot[1][:, :, :]),
                              ALU.add).then_inc(both_ready, 1)
            dve.tensor_tensor(gap[:, :], top[0][:, :], top[1][:, :], ALU.subtract).then_inc(gap_ready, 1)
            dve.wait_ge(th_ready, 1)
            dve.tensor_scalar(w_top[:, 0, :], th[:, :], 0.5, 0.5, ALU.mult, ALU.add)
            chain.link(dve.tensor_scalar(w_top[:, 1, :], th[:, :], -0.5, 0.5, ALU.mult, ALU.add))
            dve.wait_ge(rank_psum, 2)
            dve.tensor_tensor_scan(flat(upto[:, :, :]), flat(keep[:, :, :]), flat(TT[:, :, :]), 0.0, ALU.mult, ALU.add)
            chain.link(dve.tensor_copy(total[:, :, :], TT[:, :, :]))
            chain.link(dve.tensor_tensor(hit[:, :, :], upto[:, :, TILES - 1:TILES].to_broadcast([P, E_N, K]),
                                         steps[:, :, :], ALU.is_gt))
            chain.link(dve.tensor_reduce(n_groups[:, :], hit[:, :, :], AX.X, ALU.add))
            dve.tensor_tensor(pos[:, :, :], upto[:, :, :], total[:, :, :], ALU.subtract)
            chain.link(dve.tensor_tensor_scan(group_end[:, :], ones[:, 0:E_N], n_groups[:, :], 0.0, ALU.mult, ALU.add))
            dve.tensor_tensor(start[:, :], group_end[:, :], n_groups[:, :], ALU.subtract)
            dve.tensor_tensor(past[:, :, :], group_end[:, :].unsqueeze(1).to_broadcast([P, ROUTED, E_N]),
                              group[:, :, :], ALU.is_le)
            chain.link(dve.tensor_tensor(total[:, :, :], RK[:, :, :], pos[:, :, :], ALU.add))
            dve.tensor_scalar(first_row[:, :], start[:, :], float(G), float(TOK), ALU.mult, ALU.add)
            chain.link(dve.tensor_reduce(expert_f[:, :], past[:, :, :], AX.X, ALU.add))
            dve.tensor_scalar(expert_of[:, :], expert_f[:, :], float(E_N - 1), None, ALU.min)
            chain.link(dve.tensor_tensor(pos[:, :, :], total[:, :, :],
                                         first_row[:, :].unsqueeze(2).to_broadcast([P, E_N, TILES]), ALU.add))
            for k in range(2):
                chain.link(dve.tensor_tensor(total[:, :, :], by_tile(hot[k][:, :, :]), pos[:, :, :], ALU.mult))
                chain.link(dve.tensor_reduce(slot_f[:, k, :], total[:, :, :].rearrange("p e t -> p t e"), AX.X, ALU.add))
            chain.link(dve.tensor_copy(slots[:, :, :], slot_f[:, :, :]))


def experts_stage(nc, x_in, rows, sums, blobs, ident, slots, w_top, expert_of):
    with ExitStack() as ctx:
        sb = lambda name, shape, dt=fp32: ctx.enter_context(nc.sbuf_tensor("e_" + name, shape, dt))
        ps = lambda name, shape: ctx.enter_context(nc.psum_tensor("e_" + name, shape, fp32))
        sem = lambda name: ctx.enter_context(nc.semaphore("e_" + name))

        S = [[sb(f"S{u}{k}", [P, T, ROW]) for k in range(2)] for u in range(2)]
        to = [sb(f"to{u}", [P, 2, T], u32) for u in range(2)]
        token_i, token = sb("token_i", [P, TILES], i32), sb("token", [P, TILES])
        Wb = [sb(f"W{u}", [P, BLOB]) for u in range(2)]
        X = [sb(f"X{u}", [P, RT, ROW]) for u in range(2)]
        R = [sb(f"R{u}", [P, RT, D]) for u in range(2)]
        meta = [sb(f"meta{u}", [P, RT, 2]) for u in range(2)]
        result = [sb(f"result{u}", [P, RT], u32) for u in range(2)]
        xT = [sb(f"xT{u}", [P, G]) for u in range(2)]
        hT = sb("hT", [P, FT, G])
        yT = [sb(f"yT{u}", [P, RT, P]) for u in range(2)]
        Y = [sb(f"Y{u}", [P, RT, D]) for u in range(2)]
        TX, TY = ps("TX", [P, RT, P]), ps("TY", [P, RT, P])
        UP = ps("UP", [P, FT, G])
        DN = ps("DN", [P, 2, G])

        s_loaded = [sem(f"s_loaded{u}") for u in range(2)]
        token_ready, to_ready, sent = sem("token_ready"), sem("to_ready"), [sem(f"sent{u}") for u in range(2)]
        w_loaded = [sem(f"w_loaded{u}") for u in range(2)]
        x_loaded = [sem(f"x_loaded{u}") for u in range(2)]
        r_loaded = [sem(f"r_loaded{u}") for u in range(2)]
        xT_psum, xT_ready = sem("xT_psum"), sem("xT_ready")
        up_psum, h_ready = sem("up_psum"), sem("h_ready")
        dn_psum, yT_ready = sem("dn_psum"), sem("yT_ready")
        y_psum, y_ready = sem("y_psum"), sem("y_ready")
        y_stored = [sem(f"y_stored{u}") for u in range(2)]
        added, meta_ready, rounds = sem("added"), sem("meta_ready"), sem("rounds")
        block = ctx.enter_context(nc.Block())

        def w1(u, f):
            return Wb[u][:, f * P:(f + 1) * P]

        def b1(u, f):
            return Wb[u][:, F_N + f:F_N + f + 1]

        def w2(u, f):
            return Wb[u][:, F_N + FT + f * D:F_N + FT + (f + 1) * D]

        def b2(u):
            return Wb[u][:, BLOB - 1:BLOB]

        x_rows = x_in.rearrange("b n d -> (b n) d")

        @block.sync
        def _(sp):
            def load_w(g, u, expert):
                wait(sp, yT_ready, g - 1)
                sp.dma_start(Wb[u][:, :], blobs[expert]).then_inc(w_loaded[u], 16)

            def routed_expert(g):
                return sp.value_load(expert_of[0:1, bass.ds(g - SHARED, 1)], min_val=0, max_val=E_N - 1)

            def load_x(g, u, cols):
                wait(sp, xT_ready, g - 1)
                sp.dma_start(X[u][:, :, 0:cols], tiled(rows[bass.ts(g, G), 0:cols])).then_inc(x_loaded[u], 16)

            def load_r(g, u):
                wait(sp, y_ready, g - 1)
                sp.dma_start(R[u][:, :, :], tiled(x_rows[bass.ts(g, G), :])).then_inc(r_loaded[u], 16)

            def load_s(i, u):
                wait(sp, sent[u], 128 * (i - u))
                for k in range(2):
                    sp.dma_start(S[u][k][:, :, 0:D], tiled(rows[bass.ts(i, N), 0:D])).then_inc(s_loaded[u], 16)

            def store(g, u):
                sp.wait_ge(y_ready, g + 1)
                sp.dma_start(tiled(sums[bass.ts(g, G), :]), Y[u][:, :, :]).then_inc(y_stored[u], 16)

            load_x(0, 0, D)
            load_w(0, 0, E_N)
            load_s(0, 0)
            load_x(1, 1, D)
            load_w(1, 1, E_N)
            load_s(1, 1)
            load_r(0, 0)
            load_x(2, 0, D)
            load_r(1, 1)
            load_x(3, 1, D)
            with sp.Fori(0, (SHARED // 2 - 2) // 2) as j:
                for v in range(2):
                    for u in range(2):
                        g = 4 * j + (2 + 2 * v + u)
                        load_x(g + 2, u, D)
                        store(g - 2, u)
                        load_r(g, u)
                    load_s(2 * j + (2 + v), v)
            for g in (SHARED - 2, SHARED - 1):
                store(g - 2, g % 2)
                load_r(g, g % 2)
            for u in range(2):
                sp.wait_ge(sent[u], 16 * TILES)
            for g in (SHARED, SHARED + 1):
                load_x(g, g % 2, ROW)
            for g in (SHARED, SHARED + 1):
                load_w(g, g % 2, routed_expert(g))
                load_x(g + 2, g % 2, ROW)
                store(g - 2, g % 2)
            with sp.Fori(SHARED // 2 + 1, GROUPS // 2 - 1) as j:
                for u in range(2):
                    g = 2 * j + u
                    load_w(g, u, routed_expert(g))
                    load_x(g + 2, u, ROW)
            for g in range(GROUPS - 3, GROUPS):
                load_w(g, g % 2, routed_expert(g))
                if g + 2 < GROUPS:
                    load_x(g + 2, g % 2, ROW)

        @block.gpsimd
        def _(pool):
            limit = pool.to_reg(TOK + ROUTED * G - 1)
            sums_limit = pool.to_reg(TOK + SPARE - 1)
            pool.iota(token_i[:, :], pattern=[[P, TILES]], base=0, channel_multiplier=1).then_inc(token_ready, 1)
            pool.wait_ge(token_ready, 1)
            pool.tensor_copy(token[:, :], token_i[:, :]).then_inc(token_ready, 1)

            def send(i, u, first, last):
                pool.wait_ge(token_ready, 2)
                wait(pool, sent[u], 128 * (i - u))
                for k in range(2):
                    pool.tensor_copy(S[u][k][:, :, D], w_top[:, k, bass.ts(i, T)])
                    pool.tensor_copy(S[u][k][:, :, D + 1], token[:, bass.ts(i, T)])
                pool.tensor_copy(to[u][:, :, :], slots[:, :, bass.ts(i, T)]).then_inc(to_ready, 1)
                pool.wait_ge(to_ready, i + 1)
                pool.wait_ge(s_loaded[u], 16 * (i - u) + 32)
                pool.sem_inc(rounds, 1)
                for k in range(2):
                    for t in range(T):
                        pool.indirect_dma_start(
                            rows, bass.IndirectOffsetOnAxis(ap=to[u][:, k, t:t + 1], axis=0),
                            S[u][k][:, t, :], None, bounds_check=limit).then_inc(sent[u], 16)

            over_batches(pool, send)
            for u in range(2):
                pool.wait_ge(y_stored[u], 16 * SHARED // 2)

            def add(g, u):
                pool.wait_ge(y_ready, g + 1)
                wait(pool, added, 16 * RT * (g - SHARED))
                pool.sem_inc(rounds, 1)
                for t in range(RT):
                    pool.indirect_dma_start(
                        sums, bass.IndirectOffsetOnAxis(ap=result[u][:, t:t + 1], axis=0),
                        Y[u][:, t, :], None, bounds_check=sums_limit, compute_op=ALU.add).then_inc(added, 16)

            add(SHARED, 0)
            with pool.Fori(SHARED // 2, (GROUPS - 1) // 2) as j:
                add(2 * j + 1, 1)
                add(2 * j + 2, 0)
            pool.wait_ge(added, 16 * RT * ROUTED)

        @block.tensor
        def _(pe):
            def x_transposes(g, u):
                pe.wait_ge(x_loaded[u], 8 * (g - u) + 16)
                wait(pe, xT_ready, g)
                for t in range(RT):
                    mm = pe.transpose(TX[:, t, :], X[u][:, t, 0:D], ident[:, :])
                mm.then_inc(xT_psum, 1)

            def y_transposes(g, u):
                pe.wait_ge(yT_ready, g + 1)
                wait(pe, y_ready, g)
                for t in range(RT):
                    mm = pe.transpose(TY[:, t, :], yT[u][:, t, :], ident[:, :])
                mm.then_inc(y_psum, 1)

            def body(g, u, routed, first, last):
                pe.wait_ge(xT_ready, g + 1)
                pe.wait_ge(w_loaded[u], weights_count(g, u, routed))
                for f in range(FT):
                    wait(pe, h_ready, FT * g - FT + f + 1)
                    pe.matmul(UP[:, f, :], w1(u, f), xT[u][:, :], start=True, stop=True).then_inc(up_psum, 1)
                if not first:
                    y_transposes(g - 1, 1 - u)
                if not last:
                    x_transposes(g + 1, 1 - u)
                for f in range(FT):
                    pe.wait_ge(h_ready, FT * g + f + 1)
                    mm = pe.matmul(DN[:, u, :], w2(u, f), hT[:, f, :], start=(f == 0), stop=(f == FT - 1))
                mm.then_inc(dn_psum, 1)
                if last:
                    y_transposes(g, u)

            x_transposes(0, 0)
            over_groups(pe, body)

        @block.scalar
        def _(act):
            def body(g, u, routed, first, last):
                act.wait_ge(w_loaded[u], weights_count(g, u, routed))
                wait(act, dn_psum, g)
                for f in range(FT):
                    act.wait_ge(up_psum, FT * g + f + 1)
                    act.activation(hT[:, f, :], UP[:, f, :], ACT.Gelu, bias=b1(u, f)).then_inc(h_ready, 1)
                act.wait_ge(dn_psum, g + 1)
                wait(act, y_psum, g - 1)
                act.activation(yT[u][:, :, :], DN[:, u, :].rearrange("p (t n) -> p t n", t=RT),
                               ACT.Identity, bias=b2(u)).then_inc(yT_ready, 1)

            over_groups(act, body)

        @block.vector
        def _(dve):
            def copy_x(g, u, routed):
                dve.wait_ge(xT_psum, g + 1)
                wait(dve, up_psum, FT * (g - 1))
                if routed:
                    dve.wait_ge(y_ready, g - 1)
                    dve.tensor_copy(meta[u][:, :, :], X[u][:, :, D:D + 2]).then_inc(meta_ready, 1)
                dve.tensor_copy(xT[u][:, :], TX[:, :, :].rearrange("p t n -> p (t n)")).then_inc(xT_ready, 1)

            def shared_y(g, u):
                dve.wait_ge(y_psum, g + 1)
                dve.wait_ge(r_loaded[u], 8 * (g - u) + 16)
                wait(dve, y_stored[u], 8 * (g - u))
                dve.tensor_tensor(Y[u][:, :, :], TY[:, :, :], R[u][:, :, :], ALU.add).then_inc(y_ready, 1)

            def routed_y(g, u):
                dve.wait_ge(y_psum, g + 1)
                dve.wait_ge(meta_ready, g - SHARED + 1)
                dve.wait_ge(y_stored[u], 16 * SHARED // 2)
                wait(dve, added, 16 * RT * (g - SHARED - 1))
                dve.tensor_copy(result[u][:, :], meta[u][:, :, 1])
                for t in range(RT):
                    ins = dve.tensor_scalar(Y[u][:, t, :], TY[:, t, :], meta[u][:, t, 0:1], None, ALU.mult)
                ins.then_inc(y_ready, 1)

            def step(g, u, y=routed_y, routed=True):
                y(g - 1, 1 - u)
                copy_x(g + 1, 1 - u, routed)

            copy_x(0, 0, False)
            copy_x(1, 1, False)
            step(1, 1, shared_y, False)
            with dve.Fori(1, SHARED // 2 - 1) as j:
                for u in range(2):
                    step(2 * j + u, u, shared_y, False)
            step(SHARED - 2, 0, shared_y, False)
            step(SHARED - 1, 1, shared_y, True)
            step(SHARED, 0, shared_y, True)
            for g in range(SHARED + 1, SHARED + 4):
                step(g, g % 2)
            with dve.Fori(SHARED // 2 + 2, GROUPS // 2) as j:
                for u in range(2):
                    step(2 * j + u, u)
            routed_y(GROUPS - 2, 1)
            routed_y(GROUPS - 1, 0)


HEADS, HD = 4, D // 4
ADJ_BUFS = 3
ADJ_PIECES = NH * T
BUF_PIECES = [len(range(b, ADJ_PIECES, ADJ_BUFS)) for b in range(ADJ_BUFS)]


def attention_gnn_stage(nc, x_in, x_out, adjT, W_lin, b_lin, W_q, W_k, ln_g, ln_b, ident):
    with ExitStack() as ctx:
        sb = lambda name, shape, dt=fp32: ctx.enter_context(nc.sbuf_tensor("c_" + name, shape, dt))
        ps = lambda name, shape: ctx.enter_context(nc.psum_tensor("c_" + name, shape, fp32))
        sem = lambda name: ctx.enter_context(nc.semaphore("c_" + name))

        W = sb("W", [P, 3, D])
        bias, gain, shift = sb("bias", [P, D]), sb("gain", [P, D]), sb("shift", [P, D])
        ones = sb("ones", [P, HD])
        power = sb("power", [P, T])
        AH = sb("AH", [P, T, HEADS, N])
        QS, KS = sb("QS", [P, HEADS, N], fp32r), sb("KS", [P, HEADS, N], fp32r)
        A = [sb(f"A{b}", [P, HALF]) for b in range(ADJ_BUFS)]
        X = sb("X", [P, T, D])
        xnT = sb("xnT", [P, N])
        F = [sb(f"F{k}", [P, N]) for k in range(2)]
        H = [sb(f"H{k}", [P, N], fp32r) for k in range(2)]
        XR = sb("XR", [P, T, D])
        XT = sb("XT", [P, T, D])
        R = sb("R", [P, T, D])
        deg, mask = sb("deg", [P, T, HEADS]), sb("mask", [P, T, HEADS])
        warm = sb("warm", [P, 1])
        root, dis = sb("root", [P, T, HEADS]), sb("dis", [P, T, HEADS])

        S = [ps(f"S{u}", [P, N]) for u in range(2)]
        DG, YA = ps("DG", [P, N]), ps("YA", [P, N])

        w_loaded, consts = sem("w_loaded"), sem("consts")
        x_loaded, r_loaded, stored = sem("x_loaded"), sem("r_loaded"), sem("stored")
        adj_loaded = [sem(f"adj_loaded{b}") for b in range(ADJ_BUFS)]
        norm_in = LayerNorm(lambda n, s: sb("i" + n, s), lambda n: sem("i" + n))
        norm_y = LayerNorm(lambda n, s: sb("y" + n, s), lambda n: sem("y" + n))
        xn_ready, xnT_psum, xnT_ready, proj_psum = sem("xn_ready"), sem("xnT_psum"), sem("xnT_ready"), sem("proj_psum")
        copied, leaked, h_ready, lo_ready = sem("copied"), sem("leaked"), sem("h_ready"), sem("lo_ready")
        q_stacked, k_stacked = sem("q_stacked"), [sem(f"k_stacked{half}") for half in range(NH)]
        xb_ready = sem("xb_ready")
        s_psum, att_ready, ah_ready = sem("s_psum"), sem("att_ready"), sem("ah_ready")
        dg_psum, dT_ready, degT_psum = sem("dg_psum"), sem("dT_ready"), sem("degT_psum")
        deg_ready, root_ready, xs_ready = sem("deg_ready"), sem("root_ready"), sem("xs_ready")
        y_psum, yT_ready, yTr_psum = sem("y_psum"), sem("yT_ready"), sem("yTr_psum")
        ys_ready, Rb_ready, out_ready = sem("ys_ready"), sem("Rb_ready"), sem("out_ready")
        dve_step = sem("dve_step")
        block = ctx.enter_context(nc.Block())

        by_head = lambda a: a.rearrange("p t (h c) -> p t h c", h=HEADS)
        tiles = lambda a: a[:, :].rearrange("p (t n) -> p t n", t=T)
        XTt = XT[:, :, :].rearrange("p t d -> p (t d)")
        LN_AT, TR_AT, QK_AT, SPLIT_AT = 0, 2, 3, 4

        def over_rounds(eng, body):
            body(0)
            body(1)
            with eng.Fori(2, B - 1) as i:
                body(i)
            body(B - 1)
            body(B)

        STACK_AT = ADJ_PIECES - HEADS
        is_graph = lambda i: not isinstance(i, int) or 0 <= i < B

        @block.sync
        def _(sp):
            row = lambda b: b.rearrange("(a n) -> a n", a=1).to_broadcast([P, D])
            for k, w in enumerate((W_q, W_k, W_lin)):
                sp.dma_start(W[:, k, :], w).then_inc(w_loaded, 16)
            for dst, src in ((bias, b_lin), (gain, ln_g), (shift, ln_b)):
                sp.dma_start(dst[:, :], row(src)).then_inc(w_loaded, 16)

            def load_x(i):
                if is_graph(i - 3):
                    sp.wait_ge(out_ready, i - 2)
                else:
                    wait(sp, xnT_psum, i)
                sp.dma_start(X[:, :, :], tiled(x_in[i])).then_inc(x_loaded, 16)

            def load_adj(i, n):
                b, t, half = n % ADJ_BUFS, n // NH, n % NH
                before = n - ADJ_BUFS if n >= ADJ_BUFS else max(range(b, ADJ_PIECES, ADJ_BUFS)) - ADJ_PIECES
                wait(sp, ah_ready, ADJ_PIECES * i + before + 1)
                sp.dma_start(A[b][:, :], adjT[i, t * P:(t + 1) * P, half * HALF:(half + 1) * HALF]).then_inc(adj_loaded[b], 16)

            def stack(dst, parts, cols, done, heads):
                for h in heads:
                    for q, src in enumerate(parts):
                        part = src[h * HD:(h + 1) * HD, cols]
                        sp.dma_start(dst[q * HD:(q + 1) * HD, h, cols].bitcast(fp32),
                                     part if src in F else part.bitcast(fp32)).then_inc(done, 16)

            def stack_q(i):
                wait(sp, s_psum, HEADS * T * i)
                stack(QS, (H[0], F[0], H[0], F[0]), slice(0, N), q_stacked, range(HEADS))

            def stack_k(i, half, heads):
                if half == 0 and heads[0] == 0:
                    sp.wait_ge(lo_ready, 2 * i + 2)
                stack(KS, (H[1], H[1], F[1], F[1]), slice(half * HALF, (half + 1) * HALF), k_stacked[half], heads)

            def store(i):
                sp.wait_ge(out_ready, i + 1)
                sp.dma_start(tiled(x_out[i]), R[:, :, :]).then_inc(stored, 16)

            def body(i):
                if is_graph(i + 1):
                    load_x(i + 1)
                if is_graph(i):
                    for h in range(HEADS):
                        stack_k(i, 1, [h])
                        load_adj(i, ADJ_BUFS + h)
                if is_graph(i - 2):
                    store(i - 2)
                if is_graph(i - 1):
                    if is_graph(i - 2):
                        sp.wait_ge(stored, 16 * (i - 1))
                    sp.dma_start(R[:, :, :], tiled(x_in[i - 1])).then_inc(r_loaded, 16)
                if is_graph(i):
                    for n in range(ADJ_BUFS + HEADS, ADJ_PIECES):
                        load_adj(i, n)
                        h = n - STACK_AT
                        if 0 <= h < HEADS and is_graph(i + 1):
                            stack_k(i + 1, 0, [h])
                if is_graph(i + 1):
                    stack_q(i + 1)
                    for n in range(ADJ_BUFS):
                        load_adj(i + 1, n)

            load_x(0)
            for n in range(ADJ_BUFS):
                load_adj(0, n)
            sp.wait_ge(lo_ready, 1)
            stack_q(0)
            stack_k(0, 0, range(HEADS))
            over_rounds(sp, body)
            store(B - 1)
            sp.wait_ge(stored, 16 * B)

        @block.gpsimd
        def _(pool):
            pool.memset(ones[:, :], 1.0).then_inc(consts, 1)
            pool.memset(power[:, :], -0.5).then_inc(consts, 1)
            pool.wait_ge(consts, 2)
            pool.wait_ge(w_loaded, 96)
            norm_in.power(pool, power, 0, 0)

            def body(i):
                if is_graph(i + 1):
                    norm_in.power(pool, power, i + 1, 0)
                if is_graph(i - 1):
                    pool.wait_ge(r_loaded, 16 * i)
                    pool.tensor_tensor(R[:, :, :], R[:, :, :], shift[:, :].unsqueeze(1).to_broadcast([P, T, D]),
                                       ALU.add).then_inc(Rb_ready, 1)
                    norm_y.power(pool, power, i - 1, 0)

            over_rounds(pool, body)

        @block.tensor
        def _(pe):
            pe.wait_ge(w_loaded, 96)
            pe.wait_ge(consts, 2)

            def scores_read(i, t, h):
                wait(pe, att_ready, HEADS * T * i + HEADS * t + h + 1)

            def xn_transposes(i):
                pe.wait_ge(xn_ready, i + 1)
                scores_read(i - 1, TR_AT, 2)
                transposes(pe, tiles(S[0]), X, ident)[-1].then_inc(xnT_psum, 1)

            def project_qk(i):
                pe.wait_ge(xnT_ready, i + 1)
                for k in range(2):
                    scores_read(i - 1, QK_AT, 2 + k)
                    for h in range(NH):
                        cols = slice(h * HALF, (h + 1) * HALF)
                        mm = pe.matmul(S[k][:, cols], W[:, k, :], xnT[:, cols], start=True, stop=True)
                    mm.then_inc(proj_psum, 1)

            def project_X(i):
                if is_graph(i - 2):
                    pe.wait_ge(ys_ready, i - 1)
                elif is_graph(i - 1):
                    scores_read(i - 1, T - 1, HEADS - 1)
                else:
                    pe.wait_ge(copied, 2)
                for t in range(T):
                    mm = pe.matmul(S[1][:, t * P:(t + 1) * P], xnT[:, t * P:(t + 1) * P], W[:, 2, :], start=True, stop=True)
                mm.then_inc(proj_psum, 1)

            def scores(i, t, h):
                if t == 0 and h == 0:
                    if is_graph(i - 1):
                        pe.wait_ge(deg_ready, i)
                    pe.wait_ge(q_stacked, 256 * i + 256)
                    pe.wait_ge(k_stacked[0], 256 * i + 256)
                elif t == 0 and h == 1:
                    pe.wait_ge(xb_ready, i + 1)
                else:
                    scores_read(i, t, h - 2)
                if t == T // NH and h == 0:
                    pe.wait_ge(k_stacked[1], 256 * i + 256)
                if is_graph(i + 1):
                    if t == TR_AT + 1 and h == 0:
                        pe.wait_ge(xnT_ready, i + 2)
                    if t == QK_AT + 1 and h < 2:
                        pe.wait_ge(copied, 2 * i + 3 + h)
                for half in range(NH):
                    cols = slice(half * HALF, (half + 1) * HALF)
                    mm = pe.matmul(S[h % 2][:, cols], KS[:, h, t * P:(t + 1) * P], QS[:, h, cols], start=True, stop=True)
                mm.then_inc(s_psum, 1)

            def by_columns(out, t, lhsT):
                for half in range(NH):
                    cols = slice(half * HALF, (half + 1) * HALF)
                    for h in range(HEADS):
                        mm = pe.matmul(out[h * HD:(h + 1) * HD, cols], lhsT(h), AH[:, t, h, cols],
                                       start=(t == 0), stop=(t == T - 1))
                return mm

            def degrees(i, t):
                if t == 0 and is_graph(i - 1):
                    pe.wait_ge(dT_ready, i)
                pe.wait_ge(ah_ready, ADJ_PIECES * i + NH * t + NH)
                return by_columns(DG, t, lambda h: ones[:, :])

            def products(i, t):
                if t == 0:
                    pe.wait_ge(xs_ready, i + 1)
                    wait(pe, yT_ready, i)
                by_columns(YA, t, lambda h: XT[:, t, h * HD:(h + 1) * HD]).then_inc(y_psum, 1)

            def body(i):
                if is_graph(i - 1):
                    products(i - 1, 0)
                for t in range(T):
                    if is_graph(i):
                        scores(i, t, 0)
                        scores(i, t, 1)
                    if is_graph(i - 1) and t + 1 < T:
                        products(i - 1, t + 1)
                    if is_graph(i):
                        scores(i, t, 2)
                        scores(i, t, 3)
                        if t > 0:
                            degrees(i, t - 1)
                        if t == TR_AT and is_graph(i + 1):
                            xn_transposes(i + 1)
                        if t == QK_AT and is_graph(i + 1):
                            project_qk(i + 1)
                if is_graph(i - 1):
                    pe.wait_ge(yT_ready, i)
                    if is_graph(i):
                        scores_read(i, T - 1, HEADS - 1)
                    transposes(pe, tiles(S[1]), XT, ident)[-1].then_inc(yTr_psum, 1)
                if is_graph(i):
                    degrees(i, T - 1).then_inc(dg_psum, 1)
                    if is_graph(i + 1):
                        project_X(i + 1)
                    pe.wait_ge(dT_ready, i + 1)
                    transposes(pe, tiles(S[0]), XT, ident)[-1].then_inc(degT_psum, 1)

            xn_transposes(0)
            project_qk(0)
            project_X(0)
            over_rounds(pe, body)

        @block.scalar
        def _(act):
            def copy_xnT(i):
                act.wait_ge(xnT_psum, i + 1)
                act.activation(xnT[:, :], S[0][:, :], ACT.Copy).then_inc(xnT_ready, 1)

            def copy_qk(i):
                for k in range(2):
                    act.wait_ge(proj_psum, 3 * i + k + 1)
                    wait(act, (q_stacked, k_stacked[1])[k], 256 * i)
                    act.activation(F[k][:, :], S[k][:, :], ACT.Copy).then_inc(copied, 1)

            def split_hi(i):
                for k in range(2):
                    act.wait_ge(leaked, 2 * i + k + 1)
                    act.activation(H[k][:, :], F[k][:, :], ACT.Copy).then_inc(h_ready, 1)

            def body(i):
                if is_graph(i):
                    for t in range(T):
                        for h in range(HEADS):
                            act.wait_ge(s_psum, HEADS * T * i + HEADS * t + h + 1)
                            if h == 0 and is_graph(i - 1):
                                act.wait_ge(y_psum, T * (i - 1) + t + 1)
                            act.activation(AH[:, t, h, :], S[h % 2][:, :], ACT.Sigmoid, scale=HD ** -0.5).then_inc(att_ready, 1)
                        if is_graph(i + 1):
                            if t == TR_AT:
                                copy_xnT(i + 1)
                            if t == QK_AT:
                                copy_qk(i + 1)
                            if t == SPLIT_AT:
                                split_hi(i + 1)
                if is_graph(i - 1):
                    act.wait_ge(y_psum, T * i)
                    act.activation(XTt, YA[:, :], ACT.Copy).then_inc(yT_ready, 1)
                if is_graph(i):
                    act.wait_ge(dg_psum, i + 1)
                    if is_graph(i - 1):
                        act.wait_ge(yTr_psum, i)
                    act.activation(XTt, DG[:, :], ACT.Copy).then_inc(dT_ready, 1)
                    act.wait_ge(deg_ready, i + 1)
                    act.activation(root[:, :, :], deg[:, :, :], ACT.Sqrt).then_inc(root_ready, 1)
                    act.activation(warm[:, :], power[:, 0:1], ACT.Sigmoid)

            act.wait_ge(consts, 2)
            copy_xnT(0)
            copy_qk(0)
            split_hi(0)
            over_rounds(act, body)

        @block.vector
        def _(dve):
            chain = Chain(dve, dve_step)
            dve.wait_ge(w_loaded, 96)
            dve.wait_ge(consts, 2)

            def leak(a):
                return dve.scalar_tensor_tensor(out=a, in0=a, scalar=0.01, in1=a, op0=ALU.mult, op1=ALU.max)

            def leak_qk(i):
                for k in range(2):
                    dve.wait_ge(copied, 2 * i + k + 1)
                    leak(F[k][:, :]).then_inc(leaked, 1)

            def split_lo(i):
                for k in range(2):
                    dve.wait_ge(h_ready, 2 * i + k + 1)
                    dve.tensor_tensor(F[k][:, :].bitcast(fp32r), F[k][:, :], H[k][:, :].bitcast(fp32),
                                      ALU.subtract).then_inc(lo_ready, 1)

            def make_X(i):
                dve.wait_ge(proj_psum, 3 * i + 3)
                wait(dve, xs_ready, i)
                dve.tensor_tensor(XR[:, :, :], tiles(S[1]), bias[:, :].unsqueeze(1).to_broadcast([P, T, D]),
                                  ALU.add).then_inc(xb_ready, 1)
                dve.wait_ge(xb_ready, i + 1)
                chain.step(leak(XR[:, :, :]))

            def scale_Y(i):
                dve.wait_ge(yTr_psum, i + 1)
                wait(dve, out_ready, i)
                dve.tensor_tensor(by_head(X[:, :, :]), by_head(tiles(S[1])), dis[:, :, :].unsqueeze(3).to_broadcast(
                    [P, T, HEADS, HD]), ALU.mult).then_inc(ys_ready, 1)
                dve.wait_ge(ys_ready, i + 1)
                norm_y.stats(dve, X, i, 0)

            def finish(i):
                chain.link(norm_y.apply(dve, X, X, i, 0))
                chain.link(dve.tensor_tensor(X[:, :, :], X[:, :, :], gain[:, :].unsqueeze(1).to_broadcast([P, T, D]), ALU.mult))
                dve.wait_ge(Rb_ready, i + 1)
                dve.tensor_tensor(R[:, :, :], X[:, :, :], R[:, :, :], ALU.add).then_inc(out_ready, 1)

            def body(i):
                chain.at({0: 1, B: 9 * B - 2}.get(i, 9 * i - 1) if isinstance(i, int) else 9 * i - 1)
                if is_graph(i):
                    for t in range(T):
                        for half in range(NH):
                            n = NH * t + half
                            b, cols = n % ADJ_BUFS, slice(half * HALF, (half + 1) * HALF)
                            dve.wait_ge(adj_loaded[b], 16 * (BUF_PIECES[b] * i + n // ADJ_BUFS + 1))
                            if half == 0:
                                dve.wait_ge(att_ready, HEADS * T * i + HEADS * t + HEADS)
                            dve.tensor_tensor(AH[:, t, :, cols], AH[:, t, :, cols],
                                              A[b][:, :].unsqueeze(1).to_broadcast([P, HEADS, HALF]),
                                              ALU.mult).then_inc(ah_ready, 1)
                        if is_graph(i + 1):
                            if t == LN_AT:
                                dve.wait_ge(x_loaded, 16 * i + 32)
                                norm_in.stats(dve, X, i + 1, 0)
                            if t == LN_AT + 1:
                                norm_in.apply(dve, X, X, i + 1, 0).then_inc(xn_ready, 1)
                            if t == QK_AT:
                                leak_qk(i + 1)
                            if t == SPLIT_AT:
                                split_lo(i + 1)
                if is_graph(i - 1):
                    scale_Y(i - 1)
                if is_graph(i):
                    dve.wait_ge(degT_psum, i + 1)
                    degT = S[0][:, :].rearrange("p (t h c) -> p t h c", t=T, h=HEADS)[:, :, :, 0]
                    dve.tensor_scalar(mask[:, :, :], degT, 0.0, None, ALU.is_gt)
                    dve.tensor_scalar(deg[:, :, :], degT, 1.1754944e-38, None, ALU.max).then_inc(deg_ready, 1)
                    dve.wait_ge(root_ready, i + 1)
                    chain.link(dve.reciprocal(dis[:, :, :], root[:, :, :]))
                    chain.link(dve.tensor_tensor(root[:, :, :], deg[:, :, :], dis[:, :, :], ALU.mult))
                    chain.link(dve.tensor_tensor(root[:, :, :], root[:, :, :], dis[:, :, :], ALU.mult))
                    chain.link(dve.tensor_scalar(root[:, :, :], root[:, :, :], -0.5, 1.5, ALU.mult, ALU.add))
                    chain.link(dve.tensor_tensor(dis[:, :, :], dis[:, :, :], root[:, :, :], ALU.mult))
                    chain.link(dve.tensor_tensor(dis[:, :, :], dis[:, :, :], mask[:, :, :], ALU.mult))
                    dve.tensor_tensor(by_head(XT[:, :, :]), by_head(XR[:, :, :]),
                                      dis[:, :, :].unsqueeze(3).to_broadcast([P, T, HEADS, HD]), ALU.mult).then_inc(xs_ready, 1)
                    if is_graph(i + 1):
                        make_X(i + 1)
                if is_graph(i - 1):
                    finish(i - 1)

            chain.at(0)
            dve.wait_ge(x_loaded, 16)
            norm_in.stats(dve, X, 0, 0)
            norm_in.apply(dve, X, X, 0, 0).then_inc(xn_ready, 1)
            leak_qk(0)
            split_lo(0)
            make_X(0)
            over_rounds(dve, body)


SH, SP_, G_N = 8, 64, 64
INNER = SH * SP_
KT = INNER // P
NS = 64
CONV_K = 3
IN_PROJ = 2 * INNER + 2 * NS + 2 * SH
LAG = 4
SW_BUFS = 8


def slicing_stage(nc, x_in, W_x, b_xT, W_sliceT, b_slice, temperature, W_fxT, b_fx, ident, SWT, ST, scratch):
    with ExitStack() as ctx:
        sb = lambda name, shape, dt=fp32: ctx.enter_context(nc.sbuf_tensor("s_" + name, shape, dt))
        ps = lambda name, shape: ctx.enter_context(nc.psum_tensor("s_" + name, shape, fp32))
        sem = lambda name: ctx.enter_context(nc.semaphore("s_" + name))

        wx = scratch[0:SP_, 0:SH * P].rearrange("c (h d) -> c h d", h=SH)
        bx = scratch[0:SP_, SH * P:2 * SH * P].rearrange("c (h d) -> c h d", h=SH)
        bxc, wsl = sb("bxc", [SP_, SH]), sb("wsl", [SP_, G_N])
        bsl, temp = sb("bsl", [P, G_N]), sb("temp", [P, SH])
        Wc, bias = sb("Wc", [P, INNER]), sb("bias", [P, INNER])
        wfx, bfx = sb("wfx", [P, INNER]), sb("bfx", [1, INNER])
        power = sb("power", [P, T])
        X = sb("X", [P, T, D])
        xn = [sb(f"xn{u}", [P, T, D + 1]) for u in range(2)]
        xnT = [sb(f"xnT{u}", [P, N]) for u in range(2)]
        SW = [sb(f"SW{k}", [P, SH, G_N]) for k in range(SW_BUFS)]
        top = [sb(f"top{u}", [P, SH]) for u in range(2)]
        total, inv = sb("total", [P, SH]), [sb(f"inv{u}", [P, SH]) for u in range(2)]
        sn, xs = sb("sn", [P, KT]), sb("xs", [P, KT, D + 1])
        xsT, snT = sb("xsT", [P, KT, P]), sb("snT", [1, KT, P])
        zeros = scratch[:, 2 * SH * P:2 * SH * P + 512]

        TP = ps("TP", [P, T, P])
        LG = [ps(f"LG{u}", [P, INNER]) for u in range(2)]
        XS = ps("XS", [P, KT, 256])
        SP_T = [ps(f"SPT{u}", [P, KT, P]) for u in range(2)]

        w_loaded, consts, x_loaded = sem("w_loaded"), sem("consts"), sem("x_loaded")
        norm_in = LayerNorm(sb, sem)
        xn_ready, xnT_psum, xnT_ready = sem("xn_ready"), sem("xnT_psum"), sem("xnT_ready")
        lg_psum, lg_read, centred = sem("lg_psum"), sem("lg_read"), sem("centred")
        top_ready, exp_ready, inv_ready, sw_ready = sem("top_ready"), sem("exp_ready"), sem("inv_ready"), sem("sw_ready")
        sw_used, swT_ready = sem("sw_used"), sem("swT_ready")
        xs_ready, xsT_psum, xsT_ready, st_psum, st_ready = (
            sem("xs_ready"), sem("xsT_psum"), sem("xsT_ready"), sem("st_psum"), sem("st_ready"))
        dve_step = sem("dve_step")
        block = ctx.enter_context(nc.Block())
        LOADS = 7
        SETUP_STEPS = 4

        @block.sync
        def _(sp):
            row = lambda b, parts: b.rearrange("(a n) -> a n", a=1).to_broadcast([parts, b.shape[0]])
            sp.dma_start(wx, W_x.rearrange("(h c) d -> c h d", c=SP_)).then_inc(w_loaded, 16)
            sp.dma_start(bxc[:, :], b_xT).then_inc(w_loaded, 16)
            sp.dma_start(wsl[:, :], W_sliceT).then_inc(w_loaded, 16)
            sp.dma_start(bsl[:, :], row(b_slice, P)).then_inc(w_loaded, 16)
            sp.dma_start(temp[:, :], row(temperature.rearrange("a h b c -> (a h b c)"), P)).then_inc(w_loaded, 16)
            sp.dma_start(wfx[:, :], W_fxT).then_inc(w_loaded, 16)
            sp.dma_start(bfx[:, :], row(b_fx, 1)).then_inc(w_loaded, 16)

            def load_x(i):
                wait(sp, xn_ready, i)
                sp.dma_start(X[:, :, :], tiled(x_in[i])).then_inc(x_loaded, 16)

            load_x(0)
            load_x(1)
            with sp.Fori(2, B) as i:
                load_x(i)

        @block.gpsimd
        def _(pool):
            pool.memset(power[:, :], -0.5).then_inc(consts, 1)
            pool.memset(top[0][:, :], -1.0)
            pool.memset(zeros, 0.0).then_inc(consts, 1)
            for u in range(2):
                pool.memset(xn[u][:, :, D:D + 1], 1.0).then_inc(consts, 1)
            pool.wait_ge(dve_step, 2)
            pool.wait_ge(consts, 4)
            pool.tensor_tensor(temp[:, :], temp[:, :], top[0][:, :], ALU.pow).then_inc(consts, 1)
            norm_in.power(pool, power, 0, 0)

            def centre(i, t):
                k = t % SW_BUFS
                pool.wait_ge(top_ready, T * i + t + 1)
                pool.tensor_tensor(SW[k][:, :, :], SW[k][:, :, :], top[t % 2][:, :].unsqueeze(2).to_broadcast([P, SH, G_N]),
                                   ALU.subtract).then_inc(centred, 1)

            def scale(i, t):
                k = t % SW_BUFS
                pool.wait_ge(inv_ready, T * i + t + 1)
                pool.tensor_tensor(SW[k][:, :, :], SW[k][:, :, :], inv[t % 2][:, :].unsqueeze(2).to_broadcast([P, SH, G_N]),
                                   ALU.mult).then_inc(sw_ready, 1)

            def body(i, u, first, last):
                for t in range(T):
                    centre(i, t)
                    if t == 0:
                        if not first:
                            scale(i - 1, T - 1)
                    else:
                        scale(i, t - 1)
                    if t == 4 and not last:
                        norm_in.power(pool, power, i + 1, 1 - u)
                if last:
                    scale(i, T - 1)

            over_batches(pool, body)

        @block.tensor
        def _(pe):
            pe.wait_ge(w_loaded, 16 * LOADS)
            pe.wait_ge(consts, 4)
            for h in range(SH):
                pe.matmul(LG[0][:, h * G_N:(h + 1) * G_N], wx[:, h, :], wsl[:, :], start=True, stop=True)
            pe.wait_ge(dve_step, 1)
            for h in range(SH):
                mm = pe.matmul(LG[1][:, h * G_N:(h + 1) * G_N], bx[:, h, :], wsl[:, :], start=True, stop=True)
            mm.then_inc(lg_psum, 1)

            def xn_transposes(i, u):
                pe.wait_ge(xn_ready, i + 1)
                wait(pe, st_ready, i - 1)
                transposes(pe, TP, xn[u][:, :, 0:D], ident)[-1].then_inc(xnT_psum, 1)

            def logits(i, u, t):
                if t == 0:
                    pe.wait_ge(xnT_ready, i + 1)
                pe.wait_ge(lg_read, 1 if isinstance(i, int) and i == 0 and t < 2 else T * i + t)
                pe.matmul(LG[t % 2][:, :], xnT[u][:, t * P:(t + 1) * P], Wc[:, :], start=True, stop=True).then_inc(lg_psum, 1)

            def use(i, u, t, first=False):
                n = T * i + t
                pe.wait_ge(sw_ready, n + 1)
                if t == 0:
                    wait(pe, xs_ready, i)
                    for b in range(2):
                        pe.matmul(XS[:, 2 * b:2 * b + 2, :], zeros[:, 0:P], zeros, start=True, stop=False)
                flat = SW[t % SW_BUFS][:, :, :].rearrange("p h g -> p (h g)")
                for k in range(KT):
                    pe.matmul(XS[:, k, 0:D + 1], flat[:, k * P:(k + 1) * P], xn[u][:, t, :], start=False,
                              stop=(t == T - 1 and k % 2 == 1))
                wait(pe, swT_ready, n - 1)
                for k in range(KT):
                    mm = pe.transpose(SP_T[t % 2][:, k, :], flat[:, k * P:(k + 1) * P], ident[:, :])
                mm.then_inc(sw_used, 1)

            def xs_transposes(i):
                pe.wait_ge(xs_ready, i + 1)
                if exists(i + 1):
                    pe.wait_ge(xnT_ready, i + 2)
                for k in range(KT):
                    pe.transpose(TP[:, k, :], xs[:, k, 0:D], ident[:, :])
                for k in range(KT):
                    mm = pe.transpose(TP[0:1, KT + k, :], xs[:, k, D:D + 1], ident[:, :])
                mm.then_inc(xsT_psum, 1)

            def slice_tokens(i):
                pe.wait_ge(xsT_ready, i + 1)
                for h in range(SH):
                    k, q = h // 2, h % 2
                    cols, heads = slice(q * G_N, (q + 1) * G_N), slice(h * SP_, (h + 1) * SP_)
                    out = TP[q * SP_:(q + 1) * SP_, k, 0:G_N]
                    pe.matmul(out, wfx[:, heads], xsT[:, k, cols], start=True, stop=False)
                    mm = pe.matmul(out, bfx[:, heads], snT[:, k, cols], start=False, stop=True)
                mm.then_inc(st_psum, 1)

            def body(i, u, first, last):
                for t in range(T):
                    logits(i, u, t)
                    if t >= LAG:
                        use(i, u, t - LAG)
                    elif not first:
                        use(i - 1, 1 - u, t - LAG + T)
                    if t == 4 and not first:
                        xs_transposes(i - 1)
                    if t == 5 and not first:
                        slice_tokens(i - 1)
                    if t == 6 and not last:
                        xn_transposes(i + 1, 1 - u)
                if last:
                    for t in range(T - LAG, T):
                        use(i, u, t)
                    xs_transposes(i)
                    slice_tokens(i)

            xn_transposes(0, 0)
            over_batches(pe, body)

        @block.scalar
        def _(act):
            def copy_xnT(i, u):
                act.wait_ge(xnT_psum, i + 1)
                act.activation(xnT[u][:, :], TP[:, :, :].rearrange("p t n -> p (t n)"), ACT.Copy).then_inc(xnT_ready, 1)

            def copy_swT(i, t):
                act.wait_ge(sw_used, T * i + t + 1)
                act.activation(SWT[:, i, t, :, :], SP_T[t % 2][:, :, :], ACT.Copy).then_inc(swT_ready, 1)

            def copy_xsT(i):
                act.wait_ge(xsT_psum, i + 1)
                act.activation(xsT[:, :, :], TP[:, 0:KT, :], ACT.Copy)
                act.activation(snT[:, :, :], TP[0:1, KT:2 * KT, :], ACT.Copy).then_inc(xsT_ready, 1)

            def copy_st(i):
                act.wait_ge(st_psum, i + 1)
                act.activation(ST[:, :, i, :], TP[:, 0:KT, 0:G_N], ACT.Copy).then_inc(st_ready, 1)

            def body(i, u, first, last):
                for t in range(T):
                    act.wait_ge(centred, T * i + t + 1)
                    act.activation(SW[t % SW_BUFS][:, :, :], SW[t % SW_BUFS][:, :, :], ACT.Exp).then_inc(exp_ready, 1)
                    if t >= LAG:
                        copy_swT(i, t - LAG)
                    elif not first:
                        copy_swT(i - 1, t - LAG + T)
                    if t == 4 and not first:
                        copy_xsT(i - 1)
                    if t == 5 and not first:
                        copy_st(i - 1)
                    if t == 6 and not last:
                        copy_xnT(i + 1, 1 - u)
                if last:
                    for t in range(T - LAG, T):
                        copy_swT(i, t)
                    copy_xsT(i)
                    copy_st(i)

            copy_xnT(0, 0)
            over_batches(act, body)

        @block.vector
        def _(dve):
            def norm_x(i, u):
                dve.wait_ge(x_loaded, 16 * i + 16)
                norm_in.stats(dve, X, i, u)

            def apply(i, u):
                norm_in.apply(dve, X, xn[u][:, :, 0:D], i, u).then_inc(xn_ready, 1)

            chain = Chain(dve, dve_step)
            dve.wait_ge(w_loaded, 16 * LOADS)
            chain.link(dve.tensor_copy(bx, bxc[:, :].unsqueeze(2).to_broadcast([SP_, SH, P])))
            chain.link(dve.tensor_scalar(temp[:, :], temp[:, :], 1e-6, None, ALU.max))
            norm_x(0, 0)
            apply(0, 0)
            dve.wait_ge(consts, 5)
            dve.wait_ge(lg_psum, 1)
            by_head = lambda a: a.rearrange("p (h g) -> p h g", h=SH)
            over_slices = temp[:, :].unsqueeze(2).to_broadcast([P, SH, G_N])
            dve.tensor_tensor(by_head(Wc[:, :]), by_head(LG[0][:, :]), over_slices, ALU.mult)
            chain.link(dve.tensor_tensor(by_head(bias[:, :]), by_head(LG[1][:, :]),
                                         bsl[:, :].unsqueeze(1).to_broadcast([P, SH, G_N]), ALU.add))
            chain.link(dve.tensor_tensor(by_head(bias[:, :]), by_head(bias[:, :]), over_slices, ALU.mult))
            dve.sem_inc(lg_read, 1)

            def lift(i, t):
                n, k = T * i + t, t % SW_BUFS
                dve.wait_ge(lg_psum, n + 2)
                wait(dve, sw_used, n + 1 - SW_BUFS)
                dve.tensor_tensor(SW[k][:, :, :], by_head(LG[t % 2][:, :]), by_head(bias[:, :]), ALU.add).then_inc(lg_read, 1)
                dve.wait_ge(lg_read, n + 2)
                wait(dve, centred, n - 1)
                dve.tensor_reduce(top[t % 2][:, :], SW[k][:, :, :], AX.X, ALU.max).then_inc(top_ready, 1)

            def invert(i, t):
                n, k = T * i + t, t % SW_BUFS
                dve.wait_ge(exp_ready, n + 1)
                wait(dve, inv_ready, n)
                chain.link(dve.tensor_reduce(total[:, :], SW[k][:, :, :], AX.X, ALU.add))
                wait(dve, sw_ready, n - 1)
                dve.reciprocal(inv[t % 2][:, :], total[:, :]).then_inc(inv_ready, 1)

            def slice_sums(i):
                dve.wait_ge(sw_used, T * i + T)
                wait(dve, xsT_psum, i)
                chain.link(dve.tensor_scalar(sn[:, :], XS[:, :, D], 1e-5, None, ALU.add))
                chain.link(dve.reciprocal(sn[:, :], sn[:, :]))
                dve.tensor_tensor(xs[:, :, :], XS[:, :, 0:D + 1], sn[:, :].unsqueeze(2).to_broadcast([P, KT, D + 1]),
                                  ALU.mult).then_inc(xs_ready, 1)

            def body(i, u, first, last):
                chain.at(SETUP_STEPS if first else T * i + 2 * (i - 1) - 1 + SETUP_STEPS)
                for t in range(T):
                    lift(i, t)
                    if t == LAG - 1 and not first:
                        slice_sums(i - 1)
                    if t > 0:
                        invert(i, t - 1)
                    elif not first:
                        invert(i - 1, T - 1)
                    if t == 4 and not last:
                        norm_x(i + 1, 1 - u)
                    if t == 5 and not last:
                        apply(i + 1, 1 - u)
                if last:
                    invert(i, T - 1)
                    slice_sums(i)

            over_batches(dve, body)


ROWS_ALL = B * G_N
BP = B // 2
DTS = 2 * SH


def hydra_stage(nc, in_wT, conv_w, conv_b, dt_bias, A_log, Dp, fcD_wT, norm_w, hy_out_wT, out_wT, dA_rows, ident, ST, M):
    with ExitStack() as ctx:
        sb = lambda name, shape, dt=fp32: ctx.enter_context(nc.sbuf_tensor("h_" + name, shape, dt))
        sem = lambda name: ctx.enter_context(nc.semaphore("h_" + name))

        inw = sb("inw", [P, KT * IN_PROJ])
        in_w = inw[:, :].rearrange("p (k j) -> p k j", k=KT)
        outw = sb("outw", [P, KT, INNER])
        foldw = sb("foldw", [P, KT, D])
        cw, cb = sb("cw", [P, KT, CONV_K]), sb("cb", [P, KT])
        cwn, cbn = sb("cwn", [NS, 2, CONV_K]), sb("cbn", [NS, 2])
        fcD, Dc, nw = sb("fcD", [P, KT, SH]), sb("Dc", [P, KT]), sb("nw", [P, KT])
        dtb, A = sb("dtb", [DTS, 1]), sb("A", [DTS, 1])
        power, ones = sb("power", [P, B]), sb("ones", [P, P])
        diag = sb("diag", [P, G_N])
        XC = sb("XC", [P, KT, ROWS_ALL])
        Z = sb("Z", [P, KT, ROWS_ALL])
        BC = sb("BC", [NS, 2, ROWS_ALL])
        TH = [sb(f"TH{u}", [P, ROWS_ALL]) for u in range(2)]
        dts = TH[1][0:DTS, :]
        m2, rstd = sb("m2", [P, B]), sb("rstd", [P, B])
        tmp = [M[0:DTS, k * ROWS_ALL:(k + 1) * ROWS_ALL] for k in range(6)]
        dA = tmp[5]
        decay = M[:, :].rearrange("p (j b l) -> p j b l", j=DTS, b=BP)
        mix = M[:, 0:SH * BP * G_N].rearrange("p (h b l) -> p h b l", h=SH, b=BP)
        reach = inw[:, 0:DTS * BP * G_N].rearrange("p (j b l) -> p j b l", j=DTS, b=BP)
        OT = inw[:, 0:KT * ROWS_ALL].rearrange("p (k r) -> p k r", k=KT)
        xtok = ST[:, :, :, :].rearrange("p k b g -> p (k b g)").rearrange("p (b c) -> p b c", b=BP)
        YN = ST[:, :, :, :].rearrange("p k b g -> p k (b g)")
        st = YN

        bank_ = [ctx.enter_context(nc.psum_tensor(f"h_K{k}", [P, ROWS_ALL], fp32)) for k in range(8)]

        loaded, decay_loaded = sem("loaded"), sem("decay_loaded")
        later = sem("later")
        pe_done, act_done, dve_done, pool_done = sem("pe_done"), sem("act_done"), sem("dve_done"), sem("pool_done")
        dve_step = sem("dve_step")
        block = ctx.enter_context(nc.Block())

        (PE_X, PE_B, PE_C, PE_DT, PE_Z, PE_XTOK, PE_G, PE_DTTOK, PE_FCD, PE_Y, PE_SUM, PE_OUT, PE_M
         ) = (1, 5, 6, 7, 8, 12, 16, 17, 18, 22, 23, 24, 28)
        (ACT_A, ACT_TX, ACT_TB, ACT_TC, ACT_E, ACT_TZ, ACT_LN, ACT_DA, ACT_XTOK, ACT_YG, ACT_OUT, ACT_M
         ) = (1, 2, 6, 7, 8, 9, 13, 14, 15, 19, 27, 31)
        (DVE_CX, DVE_CB, DVE_CC, DVE_ABS, DVE_X, DVE_B, DVE_C, DVE_U, DVE_Z, DVE_DT, DVE_DELTA, DVE_MIX, DVE_YG,
         DVE_VAR) = (1, 5, 6, 7, 8, 12, 13, 14, 15, 19, 20, 21, 22, 26)
        LOADS = 15
        POOL_CONST, POOL_ENDS, POOL_RSTD = 2, 4, 5

        @block.sync
        def _(sp):
            def load(dst, src):
                sp.dma_start(dst, src).then_inc(loaded, 16)

            col = lambda a: a.rearrange("(n a) -> n a", a=1)
            for k in range(KT):
                load(in_w[:, k, :], in_wT[k * P:(k + 1) * P, :])
            load(cw[:, :, :], conv_w[0:INNER, :].rearrange("(k p) t -> p k t", p=P))
            load(cwn[:, :, :], conv_w[INNER:INNER + 2 * NS, :].rearrange("(k p) t -> p k t", p=NS))
            load(cb[:, :], conv_b[:, 0:KT])
            load(cbn[:, :], conv_b[0:NS, KT:KT + 2])
            for h in range(2):
                load(dtb[h * SH:(h + 1) * SH, :], col(dt_bias))
                load(A[h * SH:(h + 1) * SH, :], col(A_log))
            load(fcD[:, :, :], fcD_wT.rearrange("(k p) h -> p k h", p=P))
            load(nw[:, :], norm_w)
            load(Dc[:, :], Dp)
            for dst, src in ((outw, hy_out_wT), (foldw, out_wT)):
                sp.dma_start(dst[:, :, :], src.rearrange("(k p) j -> p k j", p=P)).then_inc(later, 16)
            sp.wait_ge(act_done, ACT_DA)
            sp.dma_start(dA_rows, dA).then_inc(later, 16)
            sp.wait_ge(later, 48)
            sp.wait_ge(dve_done, DVE_DT)
            by_pair = dA_rows.rearrange("j (b q l) -> q j b l", b=BP, q=2)
            for q in range(2):
                sp.dma_start(decay[q * G_N:(q + 1) * G_N, :, :, :],
                             by_pair[q:q + 1, :, :, :].to_broadcast([G_N, DTS, BP, G_N])).then_inc(decay_loaded, 16)

        @block.gpsimd
        def _(pool):
            pool.memset(power[:, :], -0.5).then_inc(pool_done, 1)
            pool.memset(ones[:, :], 1.0).then_inc(pool_done, 1)
            pool.wait_ge(decay_loaded, 32)
            pool.memset(decay[:, 0:SH, :, 0:1], 0.0).then_inc(pool_done, 1)
            pool.memset(decay[:, SH:DTS, :, G_N - 1:G_N], 0.0).then_inc(pool_done, 1)
            pool.wait_ge(dve_done, DVE_VAR)
            pool.tensor_tensor(rstd[:, :], m2[:, :], power[:, :], ALU.pow).then_inc(pool_done, 1)

        @block.tensor
        def _(pe):
            pe.wait_ge(loaded, 16 * LOADS)
            pe.wait_ge(pool_done, POOL_CONST)

            def project(out, j0, width):
                for k in range(KT):
                    mm = pe.matmul(out, in_w[:, k, j0:j0 + width], st[:, k, :], start=(k == 0), stop=(k == KT - 1))
                mm.then_inc(pe_done, 1)

            for k in range(KT):
                project(bank_[k][:, :], INNER + k * P, P)
            project(bank_[4][0:NS, :], 2 * INNER, NS)
            project(bank_[5][0:NS, :], 2 * INNER + NS, NS)
            project(bank_[6][0:DTS, :], 2 * INNER + 2 * NS, DTS)
            for k, bank in enumerate((7, 0, 1, 2)):
                if k > 0:
                    pe.wait_ge(dve_done, DVE_CX + k - 1)
                project(bank_[bank][:, :], k * P, P)
            pe.wait_ge(dve_done, DVE_X + KT - 1)
            for b in range(BP):
                if b >= 2:
                    pe.wait_ge(act_done, ACT_XTOK + b - 2)
                for k in range(KT):
                    mm = pe.transpose(bank_[5 + b % 2][:, k * P:(k + 1) * P], XC[:, k, b * P:(b + 1) * P], ident[:, :])
                mm.then_inc(pe_done, 1)
            pe.wait_ge(dve_done, DVE_C)
            for b in range(B):
                cols = slice(b * G_N, (b + 1) * G_N)
                q = b % 2 * G_N
                mm = pe.matmul(bank_[4][q:q + G_N, b // 2 * G_N:(b // 2 + 1) * G_N], BC[:, 0, cols], BC[:, 1, cols],
                               start=True, stop=True)
            mm.then_inc(pe_done, 1)
            pe.wait_ge(dve_done, DVE_DT)
            for b in range(BP):
                mm = pe.transpose(bank_[3][:, b * DTS:(b + 1) * DTS], dts[:, b * P:(b + 1) * P], ident[0:DTS, 0:DTS])
            mm.then_inc(pe_done, 1)
            for k, bank in enumerate((7, 0, 1, 2)):
                pe.wait_ge(dve_done, DVE_Z + k)
                for q in range(2):
                    for c in range(KT):
                        mm = pe.matmul(bank_[bank][q * SP_:(q + 1) * SP_, :],
                                       fcD[:, c, 2 * k + q:2 * k + q + 1].to_broadcast([P, SP_]), XC[:, c, :],
                                       start=(c == 0), stop=(c == KT - 1))
                mm.then_inc(pe_done, 1)
            pe.wait_ge(dve_done, DVE_MIX)
            pe.wait_ge(act_done, ACT_XTOK + BP - 1)
            for k in range(KT):
                for q in range(2):
                    h = 2 * k + q
                    for b in range(B):
                        part = slice(b % 2 * G_N, (b % 2 + 1) * G_N)
                        at = (k % 2 * BP + b // 2) * G_N
                        mm = pe.matmul(bank_[3 + k // 2 * 2 + b % 2][q * SP_:(q + 1) * SP_, at:at + G_N],
                                       xtok[part, b // 2, h * SP_:(h + 1) * SP_], mix[part, h, b // 2, :],
                                       start=True, stop=True)
            mm.then_inc(pe_done, 1)
            pe.wait_ge(act_done, ACT_YG + 2 * KT - 1)
            pe.wait_ge(later, 48)
            for k in range(KT):
                mm = pe.matmul(bank_[7][:, :], ones[:, :], Z[:, k, :], start=(k == 0), stop=(k == KT - 1))
            mm.then_inc(pe_done, 1)
            for j in range(KT):
                for k in range(KT):
                    mm = pe.matmul(bank_[j][:, :], outw[:, k, j * P:(j + 1) * P], YN[:, k, :], start=(k == 0), stop=(k == KT - 1))
                mm.then_inc(pe_done, 1)
            pe.wait_ge(act_done, ACT_OUT + KT - 1)
            pe.wait_ge(dve_done, DVE_VAR)
            for b in range(B):
                bank = (4 + b) % 8
                for k in range(KT):
                    for q in range(2):
                        part = slice(q * SP_, (q + 1) * SP_)
                        mm = pe.matmul(bank_[bank][part, k * D:(k + 1) * D], OT[part, k, b * G_N:(b + 1) * G_N],
                                       foldw[part, k, :], start=True, stop=True)
                mm.then_inc(pe_done, 1)

        @block.scalar
        def _(act):
            act.wait_ge(loaded, 16 * LOADS)

            def tanh_half(out, src):
                act.activation(out, src, ACT.Tanh, scale=0.5).then_inc(act_done, 1)

            act.activation(A[:, :], A[:, :], ACT.Exp).then_inc(act_done, 1)
            for k in range(KT):
                act.wait_ge(dve_done, DVE_CX + k)
                if k >= 2:
                    act.wait_ge(dve_done, DVE_X + k - 2)
                act.activation(TH[k % 2][:, :], XC[:, k, :], ACT.Tanh).then_inc(act_done, 1)
            for k, ready in enumerate((DVE_CB, DVE_CC)):
                act.wait_ge(dve_done, ready)
                act.wait_ge(dve_done, DVE_X + 2 + k)
                act.activation(TH[k][0:NS, :], BC[:, k, :], ACT.Tanh).then_inc(act_done, 1)
            act.wait_ge(dve_done, DVE_ABS)
            act.activation(tmp[1], tmp[1], ACT.Exp, scale=-1.0).then_inc(act_done, 1)
            for k, bank in enumerate((7, 0, 1, 2)):
                act.wait_ge(pe_done, PE_Z + k)
                act.wait_ge(dve_done, (DVE_B, DVE_C, DVE_Z, DVE_Z + 1)[k])
                act.activation(TH[k % 2][:, :], bank_[bank][:, :], ACT.Tanh, scale=0.5).then_inc(act_done, 1)
            act.wait_ge(dve_done, DVE_U)
            act.activation(tmp[3], tmp[2], ACT.Ln).then_inc(act_done, 1)
            act.wait_ge(dve_done, DVE_DT)
            act.activation(dA, dts, ACT.Exp, scale=A[:, :]).then_inc(act_done, 1)
            for b in range(BP):
                act.wait_ge(pe_done, PE_XTOK + b)
                act.activation(xtok[:, b, :], bank_[5 + b % 2][:, :], ACT.Copy).then_inc(act_done, 1)
            for k in range(KT):
                act.wait_ge(dve_done, DVE_YG + k)
                act.activation(Z[:, k, :], XC[:, k, :], ACT.Square).then_inc(act_done, 1)
                act.activation(YN[:, k, :], XC[:, k, :], ACT.Copy, scale=nw[:, k:k + 1]).then_inc(act_done, 1)
            for j in range(KT):
                act.wait_ge(pe_done, PE_OUT + j)
                act.activation(OT[:, j, :], bank_[j][:, :], ACT.Copy).then_inc(act_done, 1)
            act.wait_ge(pool_done, POOL_RSTD)
            for b in range(B):
                act.wait_ge(pe_done, PE_M + b)
                act.activation(M[:, b * KT * D:(b + 1) * KT * D], bank_[(4 + b) % 8][:, :], ACT.Copy,
                               scale=rstd[:, b:b + 1]).then_inc(act_done, 1)
            act.wait_ge(act_done, ACT_M + B - 1)

        @block.vector
        def _(dve):
            chain = Chain(dve, dve_step)
            link = chain.link
            done = lambda ins: ins.then_inc(dve_done, 1)
            by_graph = lambda a: a.rearrange("p (b l) -> p b l", b=B)
            dve.wait_ge(loaded, 16 * LOADS)
            dve.tensor_tensor(diag[:, :], ident[:, 0:G_N], ident[:, G_N:P], ALU.add)
            for w in (cw[:, :, :], cb[:, :], cwn[:, :, :], cbn[:, :]):
                ins = dve.tensor_scalar(w, w, 0.5, None, ALU.mult)
            link(ins)

            def convolve(out, src, w, bias):
                link(dve.tensor_scalar(out, src, w[:, 2:3], bias, ALU.mult, ALU.add))
                o, x = by_graph(out), by_graph(src)
                link(dve.scalar_tensor_tensor(out=o[:, :, 1:], in0=x[:, :, :G_N - 1], scalar=w[:, 1:2], in1=o[:, :, 1:],
                                              op0=ALU.mult, op1=ALU.add))
                done(dve.scalar_tensor_tensor(out=o[:, :, 2:], in0=x[:, :, :G_N - 2], scalar=w[:, 0:1], in1=o[:, :, 2:],
                                              op0=ALU.mult, op1=ALU.add))

            for k in range(KT):
                dve.wait_ge(pe_done, PE_X + k)
                convolve(XC[:, k, :], bank_[k][:, :], cw[:, k, :], cb[:, k:k + 1])
            for k in range(2):
                dve.wait_ge(pe_done, (PE_B, PE_C)[k])
                convolve(BC[:, k, :], bank_[4 + k][0:NS, :], cwn[:, k, :], cbn[:, k:k + 1])
            dve.wait_ge(pe_done, PE_DT)
            link(dve.tensor_scalar(tmp[0], bank_[6][0:DTS, :], dtb[:, :], None, ALU.add))
            link(dve.tensor_scalar(tmp[2], tmp[0], -1.0, None, ALU.mult))
            done(dve.tensor_tensor(tmp[1], tmp[0], tmp[2], ALU.max))

            def gate(out, x, th, count):
                dve.wait_ge(act_done, count)
                done(dve.scalar_tensor_tensor(out=out, in0=th, scalar=1.0, in1=x, op0=ALU.add, op1=ALU.mult))

            for k in range(KT):
                gate(XC[:, k, :], XC[:, k, :], TH[k % 2][:, :], ACT_TX + k)
            for k in range(2):
                gate(BC[:, k, :], BC[:, k, :], TH[k][0:NS, :], (ACT_TB, ACT_TC)[k])
            dve.wait_ge(act_done, ACT_E)
            dve.tensor_scalar(A[:, :], A[:, :], -1.0, None, ALU.mult)
            done(dve.tensor_scalar(tmp[2], tmp[1], 1.0, None, ALU.add))
            for k, bank in enumerate((7, 0, 1, 2)):
                gate(Z[:, k, :], bank_[bank][:, :], TH[k % 2][:, :], ACT_TZ + k)
            dve.wait_ge(act_done, ACT_LN)
            link(dve.tensor_scalar(tmp[4], tmp[2], -1.0, 2.0 ** -23, ALU.add, ALU.max))
            link(dve.reciprocal(tmp[4], tmp[4]))
            link(dve.tensor_tensor(tmp[3], tmp[3], tmp[4], ALU.mult))
            link(dve.scalar_tensor_tensor(out=tmp[4], in0=tmp[2], scalar=1.0, in1=tmp[3], op0=ALU.is_equal, op1=ALU.add))
            link(dve.tensor_tensor(tmp[4], tmp[4], tmp[1], ALU.mult))
            done(dve.scalar_tensor_tensor(out=dts, in0=tmp[0], scalar=0.0, in1=tmp[4], op0=ALU.max, op1=ALU.add))
            dve.wait_ge(pe_done, PE_DTTOK)
            done(dve.tensor_tensor(reach, bank_[3][:, 0:BP * DTS].rearrange("p (b j) -> p j b", j=DTS).unsqueeze(3).to_broadcast(
                [P, DTS, BP, G_N]), diag[:, :].unsqueeze(1).unsqueeze(1).to_broadcast([P, DTS, BP, G_N]), ALU.mult))
            dve.wait_ge(dve_done, DVE_DELTA)
            dve.wait_ge(pool_done, POOL_ENDS)
            half = SH * BP * G_N
            for lo, step in ((0, 1), (half, -1)):
                r, d = inw[:, lo:lo + half], M[:, lo:lo + half]
                ins = dve.tensor_tensor_scan(r[:, ::step], d[:, ::step], r[:, ::step], 0.0, ALU.mult, ALU.add)
            link(ins)
            dve.wait_ge(pe_done, PE_G)
            for j in range(DTS):
                ins = dve.tensor_tensor(reach[:, j, :, :], reach[:, j, :, :],
                                        bank_[4][:, 0:BP * G_N].rearrange("p (b l) -> p b l", b=BP), ALU.mult)
            link(ins)
            fw, bw = reach[:, 0:SH, :, :], reach[:, SH:DTS, :, :]
            by_hb = lambda a, lo, hi: a.rearrange("p h b l -> p (h b) l")[:, :, lo:hi]
            dve.tensor_tensor(by_hb(mix, 1, G_N - 1), by_hb(fw, 0, G_N - 2), by_hb(bw, 2, G_N), ALU.add)
            dve.tensor_copy(by_hb(mix, 0, 1), by_hb(bw, 1, 2))
            done(dve.tensor_copy(by_hb(mix, G_N - 1, G_N), by_hb(fw, G_N - 2, G_N - 1)))
            dve.wait_ge(pe_done, PE_Y)
            for k, bank in enumerate((7, 0, 1, 2)):
                link(dve.scalar_tensor_tensor(out=XC[:, k, :], in0=bank_[bank][:, :], scalar=Dc[:, k:k + 1], in1=XC[:, k, :],
                                              op0=ALU.add, op1=ALU.mult))
                for odd in range(2):
                    part = XC[:, k, :].rearrange("p (b q l) -> p b q l", b=BP, q=2)[:, :, odd, :]
                    y = bank_[3 + k // 2 * 2 + odd][:, k % 2 * BP * G_N:(k % 2 + 1) * BP * G_N]
                    ins = dve.tensor_tensor(part, y.rearrange("p (b l) -> p b l", b=BP), part, ALU.add)
                link(ins)
                done(dve.scalar_tensor_tensor(out=XC[:, k, :], in0=XC[:, k, :], scalar=0.5, in1=Z[:, k, :],
                                              op0=ALU.mult, op1=ALU.mult))
            dve.wait_ge(pe_done, PE_SUM)
            sq = TH[0][:, :]
            link(dve.tensor_tensor(by_graph(sq), by_graph(bank_[7][:, :]), diag[:, :].unsqueeze(1).to_broadcast([P, B, G_N]), ALU.mult))
            link(dve.tensor_reduce(m2[:, :], by_graph(sq), AX.X, ALU.add))
            done(dve.tensor_scalar(m2[:, :], m2[:, :], 1.0 / INNER, 1e-5, ALU.mult, ALU.add))


def deslicing_stage(nc, x_in, x_out, out_b, SWT, M):
    with ExitStack() as ctx:
        sb = lambda name, shape, dt=fp32: ctx.enter_context(nc.sbuf_tensor("o_" + name, shape, dt))
        sem = lambda name: ctx.enter_context(nc.semaphore("o_" + name))

        bias = sb("bias", [P, D])
        R = [sb(f"R{u}", [P, T, D]) for u in range(2)]
        OUT = [ctx.enter_context(nc.psum_tensor(f"o_OUT{u}", [P, T, D], fp32)) for u in range(2)]
        r_loaded = [sem(f"r_loaded{u}") for u in range(2)]
        out_psum, summed = sem("out_psum"), sem("summed")
        stored = sem("stored")
        block = ctx.enter_context(nc.Block())

        @block.sync
        def _(sp):
            sp.dma_start(bias[:, :], out_b.rearrange("(a n) -> a n", a=1).to_broadcast([P, D])).then_inc(r_loaded[0], 16)

            def load(i, u):
                sp.dma_start(R[u][:, :, :], tiled(x_in[i])).then_inc(r_loaded[u], 16)

            def body(i, u, first, last):
                sp.wait_ge(summed, 2 * i + 2)
                sp.dma_start(tiled(x_out[i]), R[u][:, :, :]).then_inc(stored, 16)
                if exists(i + 2):
                    sp.wait_ge(stored, 16 * i + 16)
                    load(i + 2, u)

            load(0, 0)
            load(1, 1)
            over_batches(sp, body)
            sp.wait_ge(stored, 16 * B)

        @block.tensor
        def _(pe):
            mixed = M[:, :].rearrange("p (b k d) -> p b k d", b=B, k=KT)
            for i in range(B):
                if i >= 2:
                    pe.wait_ge(summed, 2 * i - 2)
                for t in range(T):
                    for k in range(KT):
                        mm = pe.matmul(OUT[i % 2][:, t, :], SWT[:, i, t, k, :], mixed[:, i, k, :],
                                       start=(k == 0), stop=(k == KT - 1))
                mm.then_inc(out_psum, 1)

        @block.vector
        def _(dve):
            def body(i, u, first, last):
                dve.wait_ge(r_loaded[u], 8 * (i - u) + (32, 16)[u])
                dve.tensor_tensor(R[u][:, :, :], R[u][:, :, :], bias[:, :].unsqueeze(1).to_broadcast([P, T, D]),
                                  ALU.add).then_inc(summed, 1)
                dve.wait_ge(out_psum, i + 1)
                dve.wait_ge(summed, 2 * i + 1)
                dve.tensor_tensor(R[u][:, :, :], R[u][:, :, :], OUT[u][:, :, :], ALU.add).then_inc(summed, 1)

            over_batches(dve, body)


def graph_transformer(nc, x, adjT, g0_W_t, g0_b_t, g0_W_h, g0_theta, Wr, expert_blobs,
                      g1_W_lin, g1_b_lin, g1_W_q, g1_W_k, g1_ln_g, g1_ln_b,
                      W_x, b_xT, W_sliceT, b_slice, temperature, W_fxT, b_fx,
                      hy_in_wT, hy_conv_w, hy_conv_b, hy_dt_bias, hy_A_log, hy_D, hy_fcD_wT, hy_norm_w, hy_out_wT,
                      out_wT, out_b, out):
    stream = [nc.dram_tensor(f"stream{k}", [B, N, D], fp32).ap() for k in range(2)]
    rows = nc.dram_tensor("rows", [TOK + ROUTED * G, ROW], fp32).ap()
    sums = nc.dram_tensor("sums", [TOK + SPARE, D], fp32).ap()
    dA_rows = nc.dram_tensor("dA_rows", [DTS, ROWS_ALL], fp32).ap()
    with ExitStack() as ctx:
        ident = ctx.enter_context(nc.sbuf_tensor("ident", [P, P], fp32))
        setup_stage(nc, ident)
        gated_gnn_stage(nc, x, stream[0], adjT, g0_W_t, g0_b_t, g0_W_h, g0_theta, ident, rows, sums)
        with ExitStack() as routing:
            sb = lambda name, shape, dt: routing.enter_context(nc.sbuf_tensor(name, shape, dt))
            slots, w_top = sb("slots", [P, 2, TILES], u32), sb("w_top", [P, 2, TILES], fp32)
            expert_of = sb("expert_of", [P, ROUTED], i32)
            routing_stage(nc, stream[0], rows, Wr, ident, slots, w_top, expert_of)
            experts_stage(nc, stream[0], rows, sums, expert_blobs, ident, slots, w_top, expert_of)
        after_experts = sums[0:TOK, :].rearrange("(b n) d -> b n d", b=B)
        attention_gnn_stage(nc, after_experts, stream[1], adjT, g1_W_lin, g1_b_lin, g1_W_q, g1_W_k, g1_ln_g, g1_ln_b, ident)
        SWT = ctx.enter_context(nc.sbuf_tensor("SWT", [P, B, T, KT, P], fp32))
        M = ctx.enter_context(nc.sbuf_tensor("M", [P, B * KT * D], fp32))
        ST = ctx.enter_context(nc.sbuf_tensor("ST", [P, KT, B, G_N], fp32))
        slicing_stage(nc, stream[1], W_x, b_xT, W_sliceT, b_slice, temperature, W_fxT, b_fx, ident, SWT, ST, M)
        hydra_stage(nc, hy_in_wT, hy_conv_w, hy_conv_b, hy_dt_bias, hy_A_log, hy_D, hy_fcD_wT, hy_norm_w, hy_out_wT,
                    out_wT, dA_rows, ident, ST, M)
        deslicing_stage(nc, stream[1], out, out_b, SWT, M)


def laid_out(a):
    import numpy as np

    def expert_blob(W1, b1, W2, b2):
        E = len(W1)
        return np.concatenate([W1, b1.reshape(E, FT, P).transpose(0, 2, 1),
                               W2.reshape(E, FT, P, D).transpose(0, 2, 1, 3).reshape(E, P, FT * D),
                               b2.reshape(E, P, 1)], axis=2)

    f = lambda name: a["L0_ffn_" + name]
    h = lambda name: a["L1_ffn_hy_" + name]
    blobs = np.concatenate([expert_blob(f("W1p"), f("b1p"), f("W2p"), f("b2p")),
                            expert_blob(f("W1s")[None], f("b1s")[None], f("W2s")[None], f("b2s")[None])])
    by_tile = lambda v: v.reshape(KT, P).T
    conv_bn = h("conv_b")[INNER:].reshape(2, NS).T
    return [
        a["x"], a["adj"].transpose(0, 2, 1),
        a["L0_gnn_W_t"], a["L0_gnn_b_t"], a["L0_gnn_W_h"], a["L0_gnn_theta"],
        f("Wr"), blobs,
        a["L1_gnn_W_lin"], a["L1_gnn_b_lin"], a["L1_gnn_W_q"], a["L1_gnn_W_k"], a["L1_gnn_ln_g"], a["L1_gnn_ln_b"],
        a["L1_ffn_W_x"], a["L1_ffn_b_x"].reshape(SH, SP_).T, a["L1_ffn_W_slice"].T, a["L1_ffn_b_slice"],
        a["L1_ffn_temperature"], a["L1_ffn_W_fx"].T, a["L1_ffn_b_fx"],
        h("in_w").T, h("conv_w"),
        np.concatenate([by_tile(h("conv_b")[:INNER]), np.concatenate([conv_bn, conv_bn])], axis=1),
        h("dt_bias"), h("A_log"), by_tile(np.repeat(h("D"), SP_)), h("fcD_w").T, by_tile(h("norm_w")), h("out_w").T,
        a["L1_ffn_out_w"].T, a["L1_ffn_out_b"],
    ]


def kernel(**inputs):
    import numpy as _np
    import concourse.bacc as _bacc
    from concourse import mybir as _mybir
    from concourse.bass_utils import run_bass_kernel_spmd as _run

    nc = _bacc.Bacc("TRN2", target_bir_lowering=False, num_devices=1)
    arrays, args = {}, []
    for i, a in enumerate(laid_out({name: _np.asarray(v) for name, v in inputs.items()})):
        a = _np.ascontiguousarray(a)
        arrays[f"in_{i}_dram"] = a
        args.append(nc.dram_tensor(f"in_{i}_dram", a.shape, _mybir.dt.from_np(a.dtype), kind="ExternalInput").ap())
    out = nc.dram_tensor("out_0_dram", (B, N, D), _mybir.dt.float32, kind="ExternalOutput").ap()
    graph_transformer(nc, *args, out)
    r = _run(nc, [arrays], core_ids=[0])
    return r.results[0]["out_0_dram"]
```
